# Optimizing a Trainium2 kernel written in Bass

```python
import numpy as np
import jax
import jax.numpy as jnp

def _softmax(x, axis=-1):
    return jax.nn.softmax(x, axis=axis)

def _gelu(x):
    return jax.nn.gelu(x, approximate=True)

def _silu(x):
    return jax.nn.silu(x)

def _sigmoid(x):
    return jax.nn.sigmoid(x)

def _layernorm(x, axis=-1, eps=1e-05):
    m = jnp.mean(x, axis=axis, keepdims=True)
    v = jnp.var(x, axis=axis, keepdims=True)
    return (x - m) / jnp.sqrt(v + eps)

def _scatter_add(tgt, idx, src, axis=0):
    return tgt.at[idx].add(src)

def _segment_sum(src, seg, n):
    return jax.ops.segment_sum(src, seg, n)
kernel_name = 'mk_flamingo_gated_d2_seqx_r8_6c0351'

def setup_inputs(seed: int=0):
    np.random.seed(seed)
    _w = jnp.asarray

    def _rec_inputs():
        import jax
        import jax.numpy as jnp
        _rk = jax.random.key(seed)
        x = -0.0003929 + 0.9999 * jax.random.normal(jax.random.fold_in(_rk, 1), (8, 128, 128), jnp.float32)
        _lenS = 128 - jax.random.randint(jax.random.fold_in(_rk, 7), (8,), 0, max(1, 128 // 4) + 1, jnp.int32)
        _lenS2 = 128 - jax.random.randint(jax.random.fold_in(_rk, 8), (8,), 0, max(1, 128 // 4) + 1, jnp.int32)
        _ctx_1024P = jax.random.normal(jax.random.fold_in(_rk, 11), (8, 16, 128), jnp.float32)
        _ctx_1024c = jax.random.dirichlet(jax.random.fold_in(_rk, 511), 0.3 * jnp.ones((16,), jnp.float32), (8, 128))
        _ctx_1024t = jnp.einsum('bsk,bkd->bsd', _ctx_1024c, _ctx_1024P)
        _ctx_1024t = _ctx_1024t * jax.lax.rsqrt(jnp.mean(jnp.square(_ctx_1024t)) + 1e-12) * 0.953939
        ctx_1024 = 2.81802e-05 + 1.00001 * (_ctx_1024t + 0.3 * jax.random.normal(jax.random.fold_in(_rk, 611), (8, 128, 128), jnp.float32))
        _validS = jnp.arange(128)[None, :] < _lenS[:, None]
        _validS2 = jnp.arange(128)[None, :] < _lenS2[:, None]
        _causal = jnp.tril(jnp.ones((128, 128), dtype=bool))
        mask_BxS2_bf1 = jnp.ones((8, 128), dtype=bool)
        _g = jax.random.normal(jax.random.fold_in(_rk, 9001), (2, 2), jnp.float32)
        _g = jnp.sign(_g) * jnp.maximum(jnp.abs(_g), 1.0) + (_g == 0) * 1.0
        g_xattn = _g[0]
        g_ffn = _g[1]
        return (x, ctx_1024, mask_BxS2_bf1, g_xattn, g_ffn)
    x, ctx_1024, mask_BxS2_bf1, g_xattn, g_ffn = _rec_inputs()

    def _L0_xattn_setup():
        import jax, jax.numpy as jnp
        import numpy as np
        WINDOW_SIZE = 20
        NEG_BIG = -100000000.0

        def band_mask(S):
            idx = jnp.arange(S)
            return jnp.where(jnp.abs(idx[:, None] - idx[None, :]) <= WINDOW_SIZE, 0.0, NEG_BIG).astype(jnp.float32)
        key = jax.random.key(seed)
        k1, k2, k3, k4 = jax.random.split(key, 4)
        B, S, Dq, Dk = (8, 256, 128, 128)
        queries = jax.random.normal(k1, (B, S, Dq), dtype=jnp.float32)
        keys = jax.random.normal(k2, (B, S, Dk), dtype=jnp.float32)
        lim = 1.0 / np.sqrt(Dk)
        W_reduce = jax.random.uniform(k3, (Dq, Dk), jnp.float32, -lim, lim)
        b_reduce = jax.random.uniform(k4, (Dq,), jnp.float32, -lim, lim)
        return {'queries': queries, 'keys': keys, 'W_reduce': W_reduce, 'b_reduce': b_reduce}
    _L0_xattn_all = _L0_xattn_setup()
    _L0_xattn_in = {k: v for k, v in _L0_xattn_all.items() if k in ('W_reduce', 'b_reduce')}
    del _L0_xattn_all

    def _L0_ffn_setup():
        import jax, jax.numpy as jnp
        import numpy as np
        D_MODEL = 128
        HIDDEN = 512
        N_ROUTING = 2
        key = jax.random.key(seed)
        ks = jax.random.split(key, 10)
        s = 0.02
        x = jax.random.normal(ks[0], (4, 512, D_MODEL), dtype=jnp.float32)
        gate_w = jax.random.normal(ks[1], (N_ROUTING, D_MODEL), dtype=jnp.float32) * s
        w1 = jax.random.normal(ks[2], (N_ROUTING, D_MODEL, HIDDEN), dtype=jnp.float32) * s
        b1 = jax.random.normal(ks[3], (N_ROUTING, HIDDEN), dtype=jnp.float32) * s
        w2 = jax.random.normal(ks[4], (N_ROUTING, HIDDEN, D_MODEL), dtype=jnp.float32) * s
        b2 = jax.random.normal(ks[5], (N_ROUTING, D_MODEL), dtype=jnp.float32) * s
        sw1 = jax.random.normal(ks[6], (D_MODEL, HIDDEN), dtype=jnp.float32) * s
        sb1 = jax.random.normal(ks[7], (HIDDEN,), dtype=jnp.float32) * s
        sw2 = jax.random.normal(ks[8], (HIDDEN, D_MODEL), dtype=jnp.float32) * s
        sb2 = jax.random.normal(ks[9], (D_MODEL,), dtype=jnp.float32) * s
        return {'x': x, 'gate_w': gate_w, 'w1': w1, 'b1': b1, 'w2': w2, 'b2': b2, 'sw1': sw1, 'sb1': sb1, 'sw2': sw2, 'sb2': sb2}
    _L0_ffn_all = _L0_ffn_setup()
    _L0_ffn_in = {k: v for k, v in _L0_ffn_all.items() if k in ('gate_w', 'w1', 'b1', 'w2', 'b2', 'sw1', 'sb1', 'sw2', 'sb2')}
    del _L0_ffn_all

    def _L1_xattn_setup():
        import jax, jax.numpy as jnp
        import numpy as np
        EPS = 1e-06
        NUM_HEADS = 16
        DIM_HEADS = 64

        def _ln(x, scale, bias):
            mu = jnp.mean(x, axis=-1, keepdims=True)
            var = jnp.mean(jnp.square(x - mu), axis=-1, keepdims=True)
            return (x - mu) * jax.lax.rsqrt(var + EPS) * scale + bias
        key = jax.random.key(seed)
        ks = jax.random.split(key, 8)
        b, n, m, dim, ctx_dim = (8, 512, 32, 128, 128)
        inner = NUM_HEADS * DIM_HEADS
        x = jax.random.normal(ks[0], (b, n, dim), dtype=jnp.float32)
        context = jax.random.normal(ks[1], (b, m, ctx_dim), dtype=jnp.float32)
        mask = jnp.ones((b, m), dtype=bool)
        Wq = jax.random.normal(ks[2], (dim, inner), dtype=jnp.float32) / np.sqrt(dim)
        Wkv = jax.random.normal(ks[3], (ctx_dim, 2 * inner), dtype=jnp.float32) / np.sqrt(ctx_dim)
        null_kv = jax.random.normal(ks[4], (2, DIM_HEADS), dtype=jnp.float32)
        Wo = jax.random.normal(ks[5], (inner, dim), dtype=jnp.float32) / np.sqrt(inner)
        return {'x': x, 'context': context, 'mask': mask, 'ln1_s': jnp.ones((dim,), jnp.float32), 'ln1_b': jnp.zeros((dim,), jnp.float32), 'lnc_s': jnp.ones((ctx_dim,), jnp.float32), 'lnc_b': jnp.zeros((ctx_dim,), jnp.float32), 'Wq': Wq, 'Wkv': Wkv, 'null_kv': null_kv, 'Wo': Wo, 'lno_s': jnp.ones((dim,), jnp.float32), 'lno_b': jnp.zeros((dim,), jnp.float32)}
    _L1_xattn_all = _L1_xattn_setup()
    _L1_xattn_in = {k: v for k, v in _L1_xattn_all.items() if k in ('ln1_s', 'ln1_b', 'lnc_s', 'lnc_b', 'Wq', 'Wkv', 'null_kv', 'Wo', 'lno_s', 'lno_b')}
    del _L1_xattn_all

    def _L1_ffn_setup():
        import jax, jax.numpy as jnp
        import numpy as np
        DIM = 128
        E = 16
        TOPK = 2
        G = 4
        TOPK_G = 2
        INTER = 64
        N_SHARED = 2
        ROUTE_SCALE = 1.0

        def _gate(xf, gate_w, gate_b):
            scores = xf @ gate_w.T
            scores = jax.nn.softmax(scores.astype(jnp.float32), axis=-1)
            orig = scores
            scores = scores + gate_b
            T = xf.shape[0]
            sg = scores.reshape(T, G, E // G)
            group_scores = jax.lax.top_k(sg, 2)[0].sum(-1)
            _, gidx = jax.lax.top_k(group_scores, TOPK_G)
            keep = jax.nn.one_hot(gidx, G).sum(axis=1) > 0
            sg = jnp.where(keep[:, :, None], sg, -jnp.inf)
            scores = sg.reshape(T, E)
            _, idx = jax.lax.top_k(scores, TOPK)
            weights = jnp.take_along_axis(orig, idx, axis=1)
            weights = (weights * ROUTE_SCALE).astype(xf.dtype)
            return (weights, idx)
        key = jax.random.key(seed)
        ks = jax.random.split(key, 16)
        s = lambda fan_in: 1.0 / np.sqrt(fan_in)
        inp = {'x': jax.random.normal(ks[0], (4, 128, DIM), dtype=jnp.float32), 'gate_w': jax.random.normal(ks[1], (E, DIM), dtype=jnp.float32) * s(DIM), 'gate_b': jnp.zeros((E,), dtype=jnp.float32), 'We1': jax.random.normal(ks[2], (E, DIM, INTER), dtype=jnp.float32) * s(DIM), 'be1': jnp.zeros((E, INTER), dtype=jnp.float32), 'We2': jax.random.normal(ks[3], (E, INTER, DIM), dtype=jnp.float32) * s(INTER), 'be2': jnp.zeros((E, DIM), dtype=jnp.float32), 'We3': jax.random.normal(ks[4], (E, DIM, INTER), dtype=jnp.float32) * s(DIM), 'be3': jnp.zeros((E, INTER), dtype=jnp.float32), 'ws1': jax.random.normal(ks[5], (DIM, N_SHARED * INTER), dtype=jnp.float32) * s(DIM), 'bs1': jnp.zeros((N_SHARED * INTER,), dtype=jnp.float32), 'ws2': jax.random.normal(ks[6], (N_SHARED * INTER, DIM), dtype=jnp.float32) * s(N_SHARED * INTER), 'bs2': jnp.zeros((DIM,), dtype=jnp.float32), 'ws3': jax.random.normal(ks[7], (DIM, N_SHARED * INTER), dtype=jnp.float32) * s(DIM), 'bs3': jnp.zeros((N_SHARED * INTER,), dtype=jnp.float32)}
        return inp
    _L1_ffn_all = _L1_ffn_setup()
    _L1_ffn_in = {k: v for k, v in _L1_ffn_all.items() if k in ('gate_w', 'gate_b', 'We1', 'be1', 'We2', 'be2', 'We3', 'be3', 'ws1', 'bs1', 'ws2', 'bs2', 'ws3', 'bs3')}
    del _L1_ffn_all
    return {'x': x, 'ctx_1024': ctx_1024, 'mask_BxS2_bf1': mask_BxS2_bf1, 'g_xattn': g_xattn, 'g_ffn': g_ffn, 'L0_xattn_W_reduce': _L0_xattn_in['W_reduce'], 'L0_xattn_b_reduce': _L0_xattn_in['b_reduce'], 'L0_ffn_gate_w': _L0_ffn_in['gate_w'], 'L0_ffn_w1': _L0_ffn_in['w1'], 'L0_ffn_b1': _L0_ffn_in['b1'], 'L0_ffn_w2': _L0_ffn_in['w2'], 'L0_ffn_b2': _L0_ffn_in['b2'], 'L0_ffn_sw1': _L0_ffn_in['sw1'], 'L0_ffn_sb1': _L0_ffn_in['sb1'], 'L0_ffn_sw2': _L0_ffn_in['sw2'], 'L0_ffn_sb2': _L0_ffn_in['sb2'], 'L1_xattn_ln1_s': _L1_xattn_in['ln1_s'], 'L1_xattn_ln1_b': _L1_xattn_in['ln1_b'], 'L1_xattn_lnc_s': _L1_xattn_in['lnc_s'], 'L1_xattn_lnc_b': _L1_xattn_in['lnc_b'], 'L1_xattn_Wq': _L1_xattn_in['Wq'], 'L1_xattn_Wkv': _L1_xattn_in['Wkv'], 'L1_xattn_null_kv': _L1_xattn_in['null_kv'], 'L1_xattn_Wo': _L1_xattn_in['Wo'], 'L1_xattn_lno_s': _L1_xattn_in['lno_s'], 'L1_xattn_lno_b': _L1_xattn_in['lno_b'], 'L1_ffn_gate_w': _L1_ffn_in['gate_w'], 'L1_ffn_gate_b': _L1_ffn_in['gate_b'], 'L1_ffn_We1': _L1_ffn_in['We1'], 'L1_ffn_be1': _L1_ffn_in['be1'], 'L1_ffn_We2': _L1_ffn_in['We2'], 'L1_ffn_be2': _L1_ffn_in['be2'], 'L1_ffn_We3': _L1_ffn_in['We3'], 'L1_ffn_be3': _L1_ffn_in['be3'], 'L1_ffn_ws1': _L1_ffn_in['ws1'], 'L1_ffn_bs1': _L1_ffn_in['bs1'], 'L1_ffn_ws2': _L1_ffn_in['ws2'], 'L1_ffn_bs2': _L1_ffn_in['bs2'], 'L1_ffn_ws3': _L1_ffn_in['ws3'], 'L1_ffn_bs3': _L1_ffn_in['bs3']}

def reference(x, ctx_1024, mask_BxS2_bf1, g_xattn, g_ffn, L0_xattn_W_reduce, L0_xattn_b_reduce, L0_ffn_gate_w, L0_ffn_w1, L0_ffn_b1, L0_ffn_w2, L0_ffn_b2, L0_ffn_sw1, L0_ffn_sb1, L0_ffn_sw2, L0_ffn_sb2, L1_xattn_ln1_s, L1_xattn_ln1_b, L1_xattn_lnc_s, L1_xattn_lnc_b, L1_xattn_Wq, L1_xattn_Wkv, L1_xattn_null_kv, L1_xattn_Wo, L1_xattn_lno_s, L1_xattn_lno_b, L1_ffn_gate_w, L1_ffn_gate_b, L1_ffn_We1, L1_ffn_be1, L1_ffn_We2, L1_ffn_be2, L1_ffn_We3, L1_ffn_be3, L1_ffn_ws1, L1_ffn_bs1, L1_ffn_ws2, L1_ffn_bs2, L1_ffn_ws3, L1_ffn_bs3):
    import jax
    import jax.numpy as jnp

    def _L0_xattn_ref(queries, keys, W_reduce, b_reduce):
        import jax, jax.numpy as jnp
        import numpy as np
        WINDOW_SIZE = 20
        NEG_BIG = -100000000.0

        def band_mask(S):
            idx = jnp.arange(S)
            return jnp.where(jnp.abs(idx[:, None] - idx[None, :]) <= WINDOW_SIZE, 0.0, NEG_BIG).astype(jnp.float32)
        values = keys
        keys_r = jnp.einsum('bkd,qd->bkq', keys, W_reduce) + b_reduce
        sims = jnp.einsum('bqd,bkd->bqk', queries, keys_r)
        sims = sims + band_mask(queries.shape[1])
        weights = jax.nn.softmax(sims, axis=-1)
        return jnp.einsum('bqk,bkd->bqd', weights, values)

    def _L0_ffn_ref(x, gate_w, w1, b1, w2, b2, sw1, sb1, sw2, sb2):
        import jax, jax.numpy as jnp
        import numpy as np
        D_MODEL = 128
        HIDDEN = 512
        N_ROUTING = 2
        B, S, D = x.shape
        xf = x.reshape(-1, D)
        gate_scores = xf @ gate_w.T
        gate_probs = jax.nn.softmax(gate_scores, axis=-1)
        top1 = jnp.argmax(gate_probs, axis=-1)
        one_hot = jax.nn.one_hot(top1, N_ROUTING, dtype=xf.dtype)
        masked = xf[None, :, :] * one_hot.T[:, :, None]
        h = jax.nn.relu(jnp.einsum('end,edh->enh', masked, w1) + b1[:, None, :])
        expert_out = jnp.einsum('enh,ehd->end', h, w2) + b2[:, None, :]
        routing_output = expert_out.sum(axis=0)
        shared = jax.nn.relu(xf @ sw1 + sb1) @ sw2 + sb2
        return (routing_output + shared).reshape(B, S, D)

    def _L1_xattn_ref(x, context, mask, ln1_s, ln1_b, lnc_s, lnc_b, Wq, Wkv, null_kv, Wo, lno_s, lno_b):
        import jax, jax.numpy as jnp
        import numpy as np
        EPS = 1e-06
        NUM_HEADS = 16
        DIM_HEADS = 64

        def _ln(x, scale, bias):
            mu = jnp.mean(x, axis=-1, keepdims=True)
            var = jnp.mean(jnp.square(x - mu), axis=-1, keepdims=True)
            return (x - mu) * jax.lax.rsqrt(var + EPS) * scale + bias
        b, n, _ = x.shape
        h, d = (NUM_HEADS, DIM_HEADS)
        scale = h ** (-0.5)
        xn = _ln(x, ln1_s, ln1_b)
        cn = _ln(context, lnc_s, lnc_b)
        q = xn @ Wq
        kv = cn @ Wkv
        k, v = jnp.split(kv, 2, axis=-1)

        def to_heads(t):
            return t.reshape(t.shape[0], t.shape[1], h, d).transpose(0, 2, 1, 3)
        q, k, v = (to_heads(q), to_heads(k), to_heads(v))
        nk = jnp.broadcast_to(null_kv[0], (b, h, 1, d))
        nv = jnp.broadcast_to(null_kv[1], (b, h, 1, d))
        k = jnp.concatenate((nk, k), axis=2)
        v = jnp.concatenate((nv, v), axis=2)
        sim = jnp.einsum('bhid,bhjd->bhij', q * scale, k)
        mfull = jnp.pad(mask, ((0, 0), (1, 0)), constant_values=True)[:, None, None, :]
        max_neg = -jnp.finfo(sim.dtype).max
        sim = jnp.where(mfull, sim, max_neg)
        attn = jax.nn.softmax(sim, axis=-1)
        out = jnp.einsum('bhij,bhjd->bhid', attn, v)
        out = out.transpose(0, 2, 1, 3).reshape(b, n, h * d)
        out = out @ Wo
        return _ln(out, lno_s, lno_b)

    def _L1_ffn_ref(x, gate_w, gate_b, We1, be1, We2, be2, We3, be3, ws1, bs1, ws2, bs2, ws3, bs3):
        import jax, jax.numpy as jnp
        import numpy as np
        DIM = 128
        E = 16
        TOPK = 2
        G = 4
        TOPK_G = 2
        INTER = 64
        N_SHARED = 2
        ROUTE_SCALE = 1.0

        def _gate(xf, gate_w, gate_b):
            scores = xf @ gate_w.T
            scores = jax.nn.softmax(scores.astype(jnp.float32), axis=-1)
            orig = scores
            scores = scores + gate_b
            T = xf.shape[0]
            sg = scores.reshape(T, G, E // G)
            group_scores = jax.lax.top_k(sg, 2)[0].sum(-1)
            _, gidx = jax.lax.top_k(group_scores, TOPK_G)
            keep = jax.nn.one_hot(gidx, G).sum(axis=1) > 0
            sg = jnp.where(keep[:, :, None], sg, -jnp.inf)
            scores = sg.reshape(T, E)
            _, idx = jax.lax.top_k(scores, TOPK)
            weights = jnp.take_along_axis(orig, idx, axis=1)
            weights = (weights * ROUTE_SCALE).astype(xf.dtype)
            return (weights, idx)
        shape = x.shape
        xf = x.reshape(-1, DIM)
        weights, idx = _gate(xf, gate_w, gate_b)
        combine = (jax.nn.one_hot(idx, E, dtype=xf.dtype) * weights[..., None]).sum(1)
        h1 = jnp.einsum('td,edi->tei', xf, We1) + be1
        h3 = jnp.einsum('td,edi->tei', xf, We3) + be3
        h = jax.nn.silu(h1) * h3
        yo = jnp.einsum('tei,eid->ted', h, We2) + be2
        y = jnp.einsum('te,ted->td', combine, yo)
        z = jax.nn.silu(xf @ ws1 + bs1) * (xf @ ws3 + bs3) @ ws2 + bs2
        return (y + z).reshape(shape)
    x = x + jnp.tanh(g_xattn[0]) * _L0_xattn_ref(_layernorm(x, axis=-1), ctx_1024, L0_xattn_W_reduce, L0_xattn_b_reduce)
    x = x + jnp.tanh(g_ffn[0]) * _L0_ffn_ref(_layernorm(x, axis=-1), L0_ffn_gate_w, L0_ffn_w1, L0_ffn_b1, L0_ffn_w2, L0_ffn_b2, L0_ffn_sw1, L0_ffn_sb1, L0_ffn_sw2, L0_ffn_sb2)
    x = x + jnp.tanh(g_xattn[1]) * _L1_xattn_ref(_layernorm(x, axis=-1), ctx_1024, mask_BxS2_bf1, L1_xattn_ln1_s, L1_xattn_ln1_b, L1_xattn_lnc_s, L1_xattn_lnc_b, L1_xattn_Wq, L1_xattn_Wkv, L1_xattn_null_kv, L1_xattn_Wo, L1_xattn_lno_s, L1_xattn_lno_b)
    x = x + jnp.tanh(g_ffn[1]) * _L1_ffn_ref(_layernorm(x, axis=-1), L1_ffn_gate_w, L1_ffn_gate_b, L1_ffn_We1, L1_ffn_be1, L1_ffn_We2, L1_ffn_be2, L1_ffn_We3, L1_ffn_be3, L1_ffn_ws1, L1_ffn_bs1, L1_ffn_ws2, L1_ffn_bs2, L1_ffn_ws3, L1_ffn_bs3)
    return x

_drawn_inputs = setup_inputs


def setup_inputs(seed=0):
    import zlib

    import numpy as np

    out = dict(_drawn_inputs(seed))
    spreads = {'g_ffn': (-1.0, 0.6),
     'L1_xattn_ln1_s': (1.0, 0.2),
     'L1_xattn_ln1_b': (0.0, 0.1),
     'L1_xattn_lnc_s': (1.0, 0.2),
     'L1_xattn_lnc_b': (0.0, 0.1),
     'L1_xattn_lno_s': (1.0, 0.2),
     'L1_xattn_lno_b': (0.0, 0.1),
     'L1_ffn_gate_b': (0.0, 0.1),
     'L1_ffn_be1': (0.0, 0.8),
     'L1_ffn_be2': (0.0, 0.521),
     'L1_ffn_be3': (0.0, 0.8),
     'L1_ffn_bs1': (0.0, 0.274),
     'L1_ffn_bs2': (0.0, 0.1),
     'L1_ffn_bs3': (0.0, 0.1)}
    factors = {'L0_xattn_b_reduce': 8.0,
     'L0_ffn_b1': 8.0,
     'L0_ffn_b2': 2.997,
     'L0_ffn_sb1': 8.0,
     'L0_ffn_sb2': 3.788}
    for name, (base, spread) in spreads.items():
        noise = np.random.default_rng([zlib.crc32(name.encode()), seed]).standard_normal(out[name].shape)
        drawn = base * np.exp(spread * noise) if base else spread * noise
        out[name] = jnp.asarray(drawn.astype(out[name].dtype))
    for name, factor in factors.items():
        out[name] = (out[name] * factor).astype(out[name].dtype)
    return out
```

```python
import concourse.bass as bass
from concourse import mybir
from contextlib import ExitStack

P = 128
B = 8
GB = 4
NG = B // GB
N = GB * P
HEADS = 16
QUADS = HEADS // 4
WINDOW = 20
FC = 4
EXPERTS = 16
EC = 8
STEPS = NG * QUADS * GB
NEG_BIG = -100000000.0
MASKED = -1e30
PAD = -2e38
LOW = -1e38
TAKEN = -3e38
EPS0, EPS1 = 1e-5, 1e-6

C_BRED, C_B1, C_LN1S, C_LN1B, C_BE1, C_BE3, C_NK, C_NV, NCOLS = 0, 1, 13, 14, 15, 24, 33, 34, 35
R_GW, R_B2, R_LNCS, R_LNCB, R_LNOS, R_LNOB, R_BS2, R_GB, R_G, NROWS = (
    0, 256, 640, 768, 896, 1024, 1152, 1280, 1296, 1300)
MISC = ["q0_0", "s0_0", "q0_1", "s0_1", "p0_0", "x3_0", "lg_0", "cT_0", "p0_1", "x3_1", "lg_1", "cT_1"]


def gated_layers(nc, x, ctx_in, ctxT_in, wredT_in, cols_in, rows_in, w1_in, w2_in, wqT_in, wkT_in,
                 wvT_in, wo_in, gw_in, we1_in, we3_in, we2_in, be2_in, mask_in, out):
    fp32, fp32r, bf16, u8 = mybir.dt.float32, mybir.dt.float32r, mybir.dt.bfloat16, mybir.dt.uint8
    ALU = mybir.AluOpType
    ACT = mybir.ActivationFunctionType
    AX = mybir.AxisListType

    with ExitStack() as stack:
        def sb(name, shape, dt=fp32):
            return stack.enter_context(nc.sbuf_tensor(name, shape, dt))

        def sem(name):
            return stack.enter_context(nc.semaphore(name))

        xr = sb("xr", [P, B, P])
        ctx = sb("ctx", [P, B, P])
        ctxT = sb("ctxT", [P, B * P])
        wredT = sb("wredT", [P, P])
        cols = sb("cols", [P, NCOLS])
        rows = sb("rows", [P, NROWS])
        w1 = sb("w1", [P, 3 * FC, P])
        w2 = sb("w2", [P, 3 * FC, P])
        wqT = sb("wqT", [P, 8, P])
        wkT = sb("wkT", [P, 8, P])
        wvT = sb("wvT", [P, 8, P])
        wo = sb("wo", [P, 8, P])
        gw = sb("gw", [P, EXPERTS])
        we1 = sb("we1", [P, EC + 1, P])
        we3 = sb("we3", [P, EC + 1, P])
        we2 = sb("we2", [P, EC + 1, P])
        be2 = sb("be2", [EXPERTS, P])
        mask8 = sb("mask8", [1, B * P], u8)
        ident = sb("ident", [P, P])
        band = sb("band", [P, P])
        mhalf = sb("mhalf", [P, GB])
        ones = sb("ones", [1, P], bf16)
        sel = sb("sel", [64, EC, 2, 64])
        selr = sb("selr", [64, EC * P], fp32r)
        maskf = sb("maskf", [1, B * P])
        maskb = sb("maskb", [1, B * P], bf16)
        nvblk = sb("nvblk", [P, 8, 16])
        nkblk = sb("nkblk", [P, 2])
        gwd = sb("gwd", [P, P])
        b2bc = sb("b2bc", [P, P])
        tg = sb("tg", [P, 4])
        st = sb("st", [P, P])
        bt = sb("bt", [P, P])
        G = sb("G", [P, HEADS, P])
        Wvo = sb("Wvo", [P, HEADS, P])
        wnull = sb("wnull", [P, HEADS])
        nw = sb("nw", [HEADS, P])
        stats = sb("stats", [P, GB, 6])
        mv = sb("mv", [P, GB, 2])
        ve = sb("ve", [P, GB])
        rstd = sb("rstd", [P, GB])
        xh = [sb(f"xh{g}", [P, GB, P]) for g in range(NG)]
        xm0 = [sb(f"xma{g}", [P, GB, P]) for g in range(NG)]
        xm1 = [sb(f"xmb{g}", [P, GB, P]) for g in range(NG)]
        gtmp = sb("gtmp", [P, GB, P])
        gd = sb("gd", [P, GB])
        m0 = sb("m0", [P, GB])
        xT = [sb(f"xT{g}", [P, N]) for g in range(NG)]
        krT = [sb(f"krT{g}", [P, N]) for g in range(NG)]
        sm = [sb(f"sm{g}", [P, GB, P]) for g in range(NG)]
        nm0 = sb("nm0", [P, NG, GB])
        rs0 = sb("rs0", [P, NG, GB])
        rr0 = sb("rr0", [P, NG, GB])
        p0 = [sb(f"p0{g}", [P, GB, P]) for g in range(NG)]
        pT0 = [sb(f"pT0{g}", [P, N]) for g in range(NG)]
        fT = [[sb(f"fT{g}{k}", [P, N]) for k in range(3)] for g in range(NG)]
        hT = [sb(f"hT{k}", [P, N]) for k in range(4)]
        acc = sb("acc", [P, GB, P])
        cn = sb("cn", [P, B, P])
        cnT = sb("cnT", [P, B * P])
        xnT = [sb(f"xnT{g}", [P, N]) for g in range(NG)]
        q0T = sb("q0T", [HEADS, N])
        ns0 = sb("ns0", [P, B, HEADS])
        tT = [[xT[0], xT[1], krT[0], krT[1]],
              [t[:, :, :].rearrange("p b n -> p (b n)") for t in (sm[0], sm[1], p0[0], p0[1])]]
        nmx = sb("nmx", [P, 2, 4])
        nm = sb("nm", [P, 2, 4])
        d0 = sb("d0", [P, 2, 4])
        pr = [sb(f"pr{k}", [P, 4, P]) for k in range(3)]
        rs = sb("rs", [P, 2, 4])
        pz = sb("pz", [P, 2, 4])
        rt = sb("rt", [P, 4])
        rr = sb("rr", [P, 2, 4])
        p0n = sb("p0n", [P, B, HEADS])
        p0T = sb("p0T", [HEADS, N])
        pT = [sb(f"pT{k}", [P, N]) for k in range(2)]
        uT = [sb(f"uT{k}", [P, N]) for k in range(2)]
        z = [fT[g][1][:, :].rearrange("p (b n) -> p b n", b=GB) for g in range(NG)]
        xb = xm0
        x3T = [fT[g][0] for g in range(NG)]
        sh = sb("sh", [P, GB, EXPERTS])
        ex = sb("ex", [P, GB, EXPERTS])
        pb = sb("pb", [P, GB, EXPERTS])
        sc = sb("sc", [P, GB, EXPERTS])
        g4 = sb("g4", [P, GB])
        g4r = sb("g4r", [P, GB])
        pmx = sb("pmx", [P, 16, 2])
        pmn = sb("pmn", [P, 16, 2])
        t1 = sb("t1", [P, 16])
        t2 = sb("t2", [P, 16])
        t3 = sb("t3", [P, 16])
        gsp = sb("gsp", [P, GB, 12])
        gsr = sb("gsr", [P, GB, 12])
        top8 = sb("top8", [P, GB, 8])
        want = sb("want", [P, GB, 8])
        keep = sb("keep", [P, GB, 4])
        pen = sb("pen", [P, GB, 4])
        skp = sb("skp", [P, GB, EXPERTS])
        msp = sb("msp", [P, GB, 24])
        msr = sb("msr", [P, GB, 24])
        comb = [sb(f"comb{g}", [P, GB, EXPERTS]) for g in range(NG)]
        cTf = [sb(f"cTf{g}", [EXPERTS, N]) for g in range(NG)]
        cTs = [sb(f"cTs{g}", [64, N], fp32r) for g in range(NG)]
        sa, su, hc = hT[0:2], hT[2:4], pT0
        bank = [stack.enter_context(nc.psum_tensor(f"bank{k}", [P, N], fp32)) for k in range(8)]

        ld = {n: sem("ld_" + n) for n in
              ["x0", "x1", "ctx", "ctxT", "wredT", "cols", "rows", "w1", "w2", "wqk", "wvo", "moe", "small"]}
        consts = sem("consts")
        prep = sem("prep")
        tanh_done = sem("tanh_done")
        var_ready = sem("var_ready")
        rstd_ready = sem("rstd_ready")
        dch = sem("dve_chain")
        xh_ready = sem("xh_ready")
        kr_full, kr_sb = sem("kr_full"), sem("kr_sb")
        xT_full, xT_sb = sem("xT_full"), sem("xT_sb")
        s0_full, sm_ready = sem("s0_full"), sem("sm_ready")
        p0_ready = sem("p0_ready")
        pT0_full, pT0_sb = sem("pT0_full"), sem("pT0_sb")
        o0_full, x1_ready = sem("o0_full"), sem("x1_ready")
        gw_full, gw_sb = sem("gw_full"), sem("gw_sb")
        fm_ready = sem("fm_ready")
        fT_full, fT_sb = sem("fT_full"), sem("fT_sb")
        up_full, h_sb, dn_done = sem("up_full"), sem("h_sb"), sem("dn_done")
        acc_full, x2_ready = sem("acc_full"), sem("x2_ready")
        cn_raw, cn_ready = sem("cn_raw"), sem("cn_ready")
        cnT_full, cnT_sb = sem("cnT_full"), sem("cnT_sb")
        x2T_full, xnT_sb = sem("x2T_full"), sem("xnT_sb")
        misc_full, misc_read = sem("misc_full"), sem("misc_read")
        t_full, t_sb = sem("t_full"), sem("t_sb")
        s_full, nm_ready, exp_done = sem("s_full"), sem("nm_ready"), sem("exp_done")
        rr_ready, pn_ready = sem("rr_ready"), sem("pn_ready")
        pT_full, pT_sb = sem("pT_full"), sem("pT_sb")
        u_full, u_sb = sem("u_full"), sem("u_sb")
        out_done, o_full, o_read = sem("out_done"), sem("o_full"), sem("o_read")
        xb_ready, x3_ready = sem("xb_ready"), sem("x3_ready")
        sh_ready, ex_ready, comb_ready = sem("sh_ready"), sem("ex_ready"), sem("comb_ready")
        chi_ready, c_ready = sem("chi_ready"), sem("c_ready")
        h1_full, h3_full, cb_full = sem("h1_full"), sem("h3_full"), sem("cb_full")
        silu_done, su_done, hc_done = sem("silu_done"), sem("su_done"), sem("hc_done")
        dn1_done, y_full = sem("dn1_done"), sem("y_full")
        x4_ready, stored = sem("x4_ready"), sem("stored")

        NCONST = 16
        LN0, LN1, LN2, LNX = 0, 2, 4, 6
        GRP = [slice(g * GB, (g + 1) * GB) for g in range(NG)]

        def bc(ap, n):
            return ap.unsqueeze(2).to_broadcast([ap.shape[0], ap.shape[1], n])

        def rep(ap, n):
            return ap.unsqueeze(1).to_broadcast([ap.shape[0], n, ap.shape[1]])

        def b4(k):
            return bank[k][:, :].rearrange("p (b n) -> p b n", b=GB)

        def col(k):
            return cols[:, k:k + 1]

        def step(s):
            return s // 16, (s // 4) % 4, s % 4

        block = stack.enter_context(nc.Block())

        @block.sync
        def _(sp):
            sp.dma_start(wredT[:, :], wredT_in).then_inc(ld["wredT"], 16)
            sp.dma_start(ctxT[:, :], ctxT_in).then_inc(ld["ctxT"], 16)
            sp.dma_start(xr[:, GRP[0], :], x[:, GRP[0], :]).then_inc(ld["x0"], 16)
            sp.dma_start(cols[:, :], cols_in).then_inc(ld["cols"], 16)
            sp.dma_start(xr[:, GRP[1], :], x[:, GRP[1], :]).then_inc(ld["x1"], 16)
            sp.dma_start(rows[:, :], rows_in.partition_broadcast(P)).then_inc(ld["rows"], 16)
            sp.dma_start(ctx[:, :, :], ctx_in).then_inc(ld["ctx"], 16)
            sp.dma_start(wqT[:, :, :], wqT_in).then_inc(ld["wqk"], 16)
            sp.dma_start(wkT[:, :, :], wkT_in).then_inc(ld["wqk"], 16)
            sp.dma_start(wvT[:, :, :], wvT_in).then_inc(ld["wvo"], 16)
            sp.dma_start(wo[:, :, :], wo_in).then_inc(ld["wvo"], 16)
            sp.dma_start(w1[:, :, :], w1_in).then_inc(ld["w1"], 16)
            sp.dma_start(w2[:, :, :], w2_in).then_inc(ld["w2"], 16)
            sp.dma_start(mask8[:, :], mask_in).then_inc(ld["small"], 16)
            sp.dma_start(gw[:, :], gw_in).then_inc(ld["small"], 16)
            sp.dma_start(be2[:, :], be2_in).then_inc(ld["small"], 16)
            sp.dma_start(we1[:, :, :], we1_in).then_inc(ld["moe"], 16)
            sp.dma_start(we3[:, :, :], we3_in).then_inc(ld["moe"], 16)
            sp.dma_start(we2[:, :, :], we2_in).then_inc(ld["moe"], 16)
            for g in range(NG):
                sp.wait_ge(x4_ready, g + 1)
                sp.dma_start(out[:, GRP[g], :], xr[:, GRP[g], :]).then_inc(stored, 16)
            sp.wait_ge(stored, 16 * NG)

        @block.gpsimd
        def _(pool):
            done = 0

            def put(ins, wait=False):
                nonlocal done
                done += 1
                ins.then_inc(consts, 1)
                if wait:
                    pool.wait_ge(consts, done)

            put(pool.memset(mhalf[:, :], -0.5))
            put(pool.memset(ident[:, :], 0.0), True)
            put(pool.affine_select(out=ident[:, :], in_=ident[:, :], compare_op=ALU.not_equal, fill=1.0,
                                   base=0, pattern=[[-1, P]], channel_multiplier=1))
            put(pool.memset(band[:, :], 0.0), True)
            put(pool.affine_select(out=band[:, :], in_=band[:, :], compare_op=ALU.is_ge, fill=NEG_BIG,
                                   base=WINDOW, pattern=[[-1, P]], channel_multiplier=1), True)
            put(pool.affine_select(out=band[:, :], in_=band[:, :], compare_op=ALU.is_ge, fill=NEG_BIG,
                                   base=WINDOW, pattern=[[1, P]], channel_multiplier=-1))
            put(pool.memset(ones[:, :], 1.0))
            put(pool.memset(sel[:, :, :, :], 0.0), True)
            for half in range(2):
                put(pool.affine_select(out=sel[:, :, :, :], in_=sel[:, :, :, :], compare_op=ALU.not_equal,
                                       fill=1.0, base=-32 * half, pattern=[[-2, EC], [-1, 2], [0, 64]],
                                       channel_multiplier=1), True)
            put(pool.memset(nvblk[:, :, :], 0.0))
            put(pool.memset(nkblk[:, :], 0.0))
            put(pool.memset(gsp[:, :, :], PAD))
            put(pool.memset(msp[:, :, :], PAD))
            put(pool.memset(want[:, :, :], PAD))
            put(pool.memset(rs0[:, :, :], 0.0))
            assert done == NCONST

            n_ln = 0

            def power():
                nonlocal n_ln
                n_ln += 1
                pool.wait_ge(var_ready, n_ln)
                pool.tensor_tensor(rstd[:, :], ve[:, :], mhalf[:, :], op=ALU.pow).then_inc(rstd_ready, 1)

            for _ in range(4):
                power()
            for g in range(NG):
                power()
                pool.wait_ge(cn_raw, g + 1)
                pool.tensor_tensor(cn[:, GRP[g], :], cn[:, GRP[g], :], rep(rows[:, R_LNCS:R_LNCS + P], GB),
                                   op=ALU.mult).then_inc(cn_ready, 1)
                pool.wait_ge(cn_ready, 2 * g + 1)
                pool.tensor_tensor(cn[:, GRP[g], :], cn[:, GRP[g], :], rep(rows[:, R_LNCB:R_LNCB + P], GB),
                                   op=ALU.add).then_inc(cn_ready, 1)

            def attention_input(g):
                power()
                pool.wait_ge(x2_ready, g + 1)
                pool.wait_ge(prep, 10)
                pool.tensor_tensor(xb[g][:, :, :], xr[:, GRP[g], :], rep(bt[:, :], GB),
                                   op=ALU.add).then_inc(xb_ready, 1)

            def normalise(s):
                pool.wait_ge(rr_ready, s + 1)
                pool.tensor_tensor(pr[s % 3][:, :, :], pr[s % 3][:, :, :], bc(rr[:, s % 2, :], P),
                                   op=ALU.mult).then_inc(pn_ready, 1)

            def attention_output(g):
                power()
                pool.wait_ge(o_read, g + 1)
                pool.tensor_tensor(z[g][:, :, :], z[g][:, :, :], rep(st[:, :], GB),
                                   op=ALU.mult).then_inc(xb_ready, 1)
                pool.wait_ge(xb_ready, NG + g + 1)
                pool.tensor_tensor(xr[:, GRP[g], :], z[g][:, :, :], xb[g][:, :, :],
                                   op=ALU.add).then_inc(x3_ready, 1)

            attention_input(0)
            attention_input(1)
            for k in range(STEPS + 6):
                if 1 <= k <= STEPS:
                    normalise(k - 1)
                if k in (20, 36):
                    attention_output((k - 20) // 16)
                if k in (23, 37):
                    power()

        @block.tensor
        def _(pe):
            pe.wait_ge(ld["wredT"], 16)
            pe.wait_ge(ld["ctxT"], 16)
            for g in range(NG):
                pe.matmul(bank[g][:, :], wredT[:, :], ctxT[:, g * N:(g + 1) * N],
                          start=True, stop=True).then_inc(kr_full, 1)
            pe.wait_ge(consts, NCONST)
            for g in range(NG):
                pe.wait_ge(xh_ready, LN0 + g + 1)
                for b in range(GB):
                    mm = pe.transpose(bank[2 + g][:, b * P:(b + 1) * P], xh[g][:, b, :], ident[:, :])
                mm.then_inc(xT_full, 1)
            for g in range(NG):
                pe.wait_ge(kr_sb, g + 1)
                pe.wait_ge(xT_sb, g + 1)
                for b in range(GB):
                    mm = pe.matmul(bank[4 + g][:, b * P:(b + 1) * P], xT[g][:, b * P:(b + 1) * P],
                                   krT[g][:, b * P:(b + 1) * P], start=True, stop=True)
                mm.then_inc(s0_full, 1)
            for g in range(NG):
                pe.wait_ge(p0_ready, GB * (g + 1))
                for b in range(GB):
                    mm = pe.transpose(bank[g][:, b * P:(b + 1) * P], p0[g][:, b, :], ident[:, :])
                mm.then_inc(pT0_full, 1)
            for g in range(NG):
                pe.wait_ge(pT0_sb, g + 1)
                pe.wait_ge(ld["ctx"], 16)
                for b in range(GB):
                    mm = pe.matmul(bank[2 + g][:, b * P:(b + 1) * P], pT0[g][:, b * P:(b + 1) * P],
                                   ctx[:, g * GB + b, :], start=True, stop=True)
                mm.then_inc(o0_full, 1)

            pe.wait_ge(ld["wqk"], 32)
            pe.wait_ge(ld["wvo"], 32)
            pe.wait_ge(sm_ready, NG)
            for n in range(8):
                if n >= 4:
                    pe.wait_ge(gw_sb, n - 3)
                r = slice(64 * (n % 2), 64 * (n % 2) + 64)
                for i in range(4):
                    c = 4 * (n % 4 // 2) + i
                    left, right = (wqT, wkT) if n < 4 else (wvT, wo)
                    mm = pe.matmul(bank[4 + n % 4][:, i * P:(i + 1) * P], left[r, c, :], right[r, c, :],
                                   start=True, stop=True)
                mm.then_inc(gw_full, 1)
            pe.wait_ge(gw_sb, 5)
            pe.wait_ge(prep, 8)
            for c in range(8):
                pe.matmul(bank[4][:, 2 * c:2 * c + 2], wqT[:, c, :], nkblk[:, :], start=True, stop=True)
            for c in range(8):
                mm = pe.matmul(bank[4][0:HEADS, P:2 * P], nvblk[:, c, :], wo[:, c, :],
                               start=(c == 0), stop=(c == 7))
            mm.then_inc(gw_full, 1)

            def mlp_rows(g):
                if g:
                    pe.wait_ge(fT_sb, 3 * g)
                pe.wait_ge(fm_ready, g + 1)
                for k, src in enumerate((xh[g], xm0[g], xm1[g])):
                    for b in range(GB):
                        mm = pe.transpose(bank[k][:, b * P:(b + 1) * P], src[:, b, :], ident[:, :])
                    mm.then_inc(fT_full, 1)

            def mlp_up(g, j):
                u = 12 * g + j
                kind, c = j // FC, (j + 8) % 12
                pe.wait_ge(fT_sb, 3 * g + kind + 1)
                if u >= 3:
                    pe.wait_ge(h_sb, u - 2)
                pe.matmul(bank[3 + u % 3][:, :], w1[:, c, :], fT[g][kind][:, :],
                          start=True, stop=True).then_inc(up_full, 1)

            def mlp_down(g, j):
                u = 12 * g + j
                pe.wait_ge(h_sb, u + 1)
                for b in range(GB):
                    mm = pe.matmul(bank[6 + g][:, b * P:(b + 1) * P], hT[u % 4][:, b * P:(b + 1) * P],
                                   w2[:, (j + 8) % 12, :], start=(j == 0 and b == 0), stop=(j == 11),
                                   skip_group_check=True)
                mm.then_inc(dn_done if j < 11 else acc_full, 1)

            def context_rows():
                pe.wait_ge(fT_sb, 5)
                for g in range(NG):
                    pe.wait_ge(cn_ready, 2 * g + 2)
                    for b in range(GB):
                        mm = pe.transpose(bank[g][:, b * P:(b + 1) * P], cn[:, g * GB + b, :], ident[:, :])
                    mm.then_inc(cnT_full, 1)

            def attention_rows(g):
                if g == 0:
                    pe.wait_ge(fT_sb, 6)
                pe.wait_ge(xh_ready, LN2 + g + 1)
                for b in range(GB):
                    mm = pe.transpose(bank[2][:, b * P:(b + 1) * P], xh[g][:, b, :], ident[:, :])
                mm.then_inc(x2T_full, 1)

            pe.wait_ge(x1_ready, NG)
            mlp_rows(0)
            pe.wait_ge(gw_sb, 9)
            pe.wait_ge(ld["w1"], 16)
            pe.wait_ge(ld["w2"], 16)
            for g in range(NG):
                for j in range(14):
                    if j < 12:
                        mlp_up(g, j)
                    if j == 7 and g == 0:
                        mlp_rows(1)
                    if j == 9 and g == 1:
                        attention_rows(0)
                    if j >= 2:
                        mlp_down(g, j - 2)
                if g == 0:
                    context_rows()

            def misc(name):
                if MISC.index(name):
                    pe.wait_ge(misc_read, MISC.index(name))

            def null_scores(g):
                misc(f"q0_{g}")
                pe.wait_ge(xnT_sb, g + 1)
                pe.matmul(bank[5][0:HEADS, :], wnull[:, :], xnT[g][:, :], start=True,
                          stop=True).then_inc(misc_full, 1)
                misc(f"s0_{g}")
                for b in range(GB):
                    mm = pe.transpose(bank[5][:, b * HEADS:(b + 1) * HEADS], q0T[:, b * P:(b + 1) * P],
                                      ident[0:HEADS, 0:HEADS])
                mm.then_inc(misc_full, 1)

            def fold_query(n):
                if n:
                    pe.wait_ge(t_sb, n)
                pe.wait_ge(xnT_sb, n // 16 + 1)
                if n == 16:
                    pe.wait_ge(xnT_sb, 2)
                pe.matmul(bank[2][:, :], G[:, n % 16, :], xnT[n // 16][:, :], start=True,
                          stop=True).then_inc(t_full, 1)

            def scores(s):
                g, hq, b = step(s)
                if s >= 2:
                    pe.wait_ge(exp_done, 4 * (s - 1))
                bb = g * GB + b
                pe.matmul(bank[s % 2][:, :], ones[:, :], rep(maskb[:, bb * P:(bb + 1) * P], 4),
                          start=True, stop=True)
                pe.wait_ge(t_sb, 4 * (s // 4) + 4)
                for i in range(4):
                    mm = pe.matmul(bank[s % 2][:, i * P:(i + 1) * P], tT[(s // 4) % 2][i][:, b * P:(b + 1) * P],
                                   cnT[:, bb * P:(bb + 1) * P], start=False, stop=True, skip_group_check=True)
                mm.then_inc(s_full, 1)

            def turn_probs(s):
                pe.wait_ge(pn_ready, s + 1)
                if s:
                    pe.wait_ge(pT_sb, s)
                for i in range(4):
                    mm = pe.transpose(bank[3][:, i * P:(i + 1) * P], pr[s % 3][:, i, :], ident[:, :])
                mm.then_inc(pT_full, 1)

            def gather_context(s):
                g, hq, b = step(s)
                pe.wait_ge(pT_sb, s + 1)
                if s:
                    pe.wait_ge(u_sb, s)
                pe.matmul(bank[4][:, :], cn[:, g * GB + b, :], pT[s % 2][:, :], start=True,
                          stop=True).then_inc(u_full, 1)

            def project(s):
                g, hq, b = step(s)
                pe.wait_ge(u_sb, s + 1)
                for i in range(4):
                    mm = pe.matmul(bank[6 + g][:, b * P:(b + 1) * P], uT[s % 2][:, i * P:(i + 1) * P],
                                   Wvo[:, 4 * hq + i, :], start=(s % 16 == 0 and i == 0), stop=False,
                                   skip_group_check=True)
                mm.then_inc(out_done, 1)

            def turn_null(g):
                misc(f"p0_{g}")
                pe.wait_ge(rr_ready, 16 * g + 16)
                for b in range(GB):
                    mm = pe.transpose(bank[5][0:HEADS, b * P:(b + 1) * P], p0n[:, g * GB + b, :], ident[:, :])
                mm.then_inc(misc_full, 1)

            def add_null(g):
                pe.wait_ge(misc_read, MISC.index(f"p0_{g}") + 1)
                for b in range(GB):
                    mm = pe.matmul(bank[6 + g][:, b * P:(b + 1) * P], p0T[:, b * P:(b + 1) * P], nw[:, :],
                                   start=False, stop=True, skip_group_check=True)
                mm.then_inc(o_full, 1)

            def moe_rows(g):
                misc(f"x3_{g}")
                pe.wait_ge(xh_ready, LNX + g + 1)
                for b in range(GB):
                    mm = pe.transpose(bank[5][:, b * P:(b + 1) * P], xh[g][:, b, :], ident[:, :])
                mm.then_inc(misc_full, 1)

            def moe_logits(g):
                misc(f"lg_{g}")
                pe.wait_ge(ld["small"], 48)
                for b in range(GB):
                    mm = pe.matmul(bank[5][:, b * EXPERTS:(b + 1) * EXPERTS], x3T[g][:, b * P:(b + 1) * P],
                                   gw[:, :], start=True, stop=True)
                mm.then_inc(misc_full, 1)

            def moe_weights(g):
                misc(f"cT_{g}")
                pe.wait_ge(comb_ready, g + 1)
                for b in range(GB):
                    mm = pe.transpose(bank[5][0:EXPERTS, b * P:(b + 1) * P], comb[g][:, b, :], ident[:, :])
                mm.then_inc(misc_full, 1)

            def moe_up(g, n):
                m, c = 9 * g + n, (n + 8) % 9
                if m >= 2:
                    pe.wait_ge(silu_done, m - 1)
                pe.matmul(bank[m % 2][:, :], we1[:, c, :], x3T[g][:, :], start=True,
                          stop=True).then_inc(h1_full, 1)
                if m >= 2:
                    pe.wait_ge(su_done, m - 1)
                pe.matmul(bank[2 + m % 2][:, :], we3[:, c, :], x3T[g][:, :], start=True,
                          stop=True).then_inc(h3_full, 1)
                if n:
                    k = 8 * g + n - 1
                    pe.wait_ge(c_ready, g + 1)
                    if k:
                        pe.wait_ge(hc_done, k)
                    pe.matmul(bank[4][:, :], selr[:, (n - 1) * P:n * P], cTs[g][:, :], start=True,
                              stop=True).then_inc(cb_full, 1)

            def moe_down(g, n):
                if n:
                    pe.wait_ge(hc_done, 8 * g + n)
                    src = hc[n % 2]
                else:
                    pe.wait_ge(su_done, 9 * g + 1)
                    src = su[(9 * g) % 2]
                for b in range(GB):
                    mm = pe.matmul(bank[6 + g][:, b * P:(b + 1) * P], src[:, b * P:(b + 1) * P],
                                   we2[:, (n + 8) % 9, :], start=(n == 0 and b == 0), stop=False,
                                   skip_group_check=True)
                mm.then_inc(dn1_done, 1)

            def moe_bias(g):
                for b in range(GB):
                    mm = pe.matmul(bank[6 + g][:, b * P:(b + 1) * P], cTf[g][:, b * P:(b + 1) * P], be2[:, :],
                                   start=False, stop=True, skip_group_check=True)
                mm.then_inc(y_full, 1)

            pe.wait_ge(h_sb, 24)
            pe.wait_ge(cnT_sb, NG)
            for n in range(4):
                if n == 0:
                    pe.wait_ge(xnT_sb, 1)
                fold_query(n)
                if n == 1:
                    null_scores(0)
            pe.wait_ge(prep, 10)
            for k in range(STEPS + 4):
                if k < STEPS:
                    scores(k)
                if k + 4 < STEPS:
                    if k == 3:
                        pe.wait_ge(t_sb, 7)
                        attention_rows(1)
                        pe.wait_ge(xnT_sb, 2)
                    fold_query(k + 4)
                if k == 4:
                    null_scores(1)
                if 2 <= k < STEPS + 2:
                    turn_probs(k - 2)
                if 3 <= k < STEPS + 3:
                    gather_context(k - 3)
                if k in (17, 33):
                    turn_null((k - 17) // 16)
                if k == 20:
                    pe.wait_ge(acc_full, 2)
                if k >= 4:
                    project(k - 4)
                if k in (19, 35):
                    add_null((k - 19) // 16)
                if k == 26:
                    moe_rows(0)
                if k == 28:
                    moe_logits(0)
                if k == 31:
                    moe_weights(0)
            pe.wait_ge(exp_done, 4 * STEPS)
            pe.wait_ge(t_sb, STEPS)
            pe.wait_ge(pT_sb, STEPS)
            pe.wait_ge(u_sb, STEPS)
            pe.wait_ge(ld["moe"], 48)
            for g in range(NG):
                pe.wait_ge(o_read, g + 1)
                pe.wait_ge(misc_read, MISC.index(f"x3_{g}") + 1)
                for n in range(10):
                    if n < 9:
                        moe_up(g, n)
                    if n >= 1:
                        moe_down(g, n - 1)
                    if g == 0 and n == 3:
                        moe_rows(1)
                    if g == 0 and n == 4:
                        moe_logits(1)
                    if g == 0 and n == 8:
                        moe_weights(1)
                moe_bias(g)

        @block.scalar
        def _(act):
            def copy(dst, src, **kw):
                return act.activation(dst, src, ACT.Copy, **kw)

            act.wait_ge(ld["cols"], 16)
            for g in range(NG):
                act.wait_ge(kr_full, g + 1)
                act.activation(krT[g][:, :], bank[g][:, :], ACT.Identity, bias=col(C_BRED)).then_inc(kr_sb, 1)
            act.wait_ge(ld["rows"], 16)
            act.activation(tg[:, :], rows[:, R_G:R_G + 4], ACT.Tanh).then_inc(tanh_done, 1)
            for g in range(NG):
                act.wait_ge(xT_full, g + 1)
                copy(xT[g][:, :], bank[2 + g][:, :]).then_inc(xT_sb, 1)
            act.wait_ge(consts, NCONST)
            for g in range(NG):
                act.wait_ge(sm_ready, g + 1)
                for b in range(GB):
                    act.activation(p0[g][:, b, :], sm[g][:, b, :], ACT.Exp, bias=nm0[:, g, b:b + 1],
                                   accum_out=rs0[:, g, b:b + 1]).then_inc(p0_ready, 1)
            for g in range(NG):
                act.wait_ge(pT0_full, g + 1)
                copy(pT0[g][:, :], bank[g][:, :]).then_inc(pT0_sb, 1)
            for n in range(8):
                act.wait_ge(gw_full, n + 1)
                dst = G if n < 4 else Wvo
                first = 8 * (n % 4 // 2) + n % 2
                copy(dst[:, first:first + 7:2, :], b4(4 + n % 4),
                     scale=HEADS ** -0.5 if n < 4 else 1.0).then_inc(gw_sb, 1)
            act.wait_ge(gw_full, 9)
            copy(wnull[:, :], bank[4][:, 0:HEADS], scale=HEADS ** -0.5)
            copy(nw[:, :], bank[4][0:HEADS, P:2 * P]).then_inc(gw_sb, 1)

            def rows_out(g):
                for k in range(3):
                    act.wait_ge(fT_full, 3 * g + k + 1)
                    copy(fT[g][k][:, :], bank[k][:, :]).then_inc(fT_sb, 1)

            def hidden(u):
                act.wait_ge(up_full, u + 1)
                if u >= 4:
                    v = u - 4
                    if v % 12 == 11:
                        act.wait_ge(acc_full, v // 12 + 1)
                    else:
                        act.wait_ge(dn_done, 11 * (v // 12) + v % 12 + 1)
                act.activation(hT[u % 4][:, :], bank[3 + u % 3][:, :], ACT.Relu,
                               bias=col(C_B1 + (u % 12 + 8) % 12)).then_inc(h_sb, 1)

            rows_out(0)
            for g in range(NG):
                for j in range(12):
                    hidden(12 * g + j)
                    if g == 0 and j == 7:
                        rows_out(1)
                    if g == 1 and j == 9:
                        act.wait_ge(x2T_full, 1)
                        act.activation(xnT[0][:, :], bank[2][:, :], ACT.Identity, bias=col(C_LN1B),
                                       scale=col(C_LN1S)).then_inc(xnT_sb, 1)
                if g == 0:
                    for c in range(NG):
                        act.wait_ge(cnT_full, c + 1)
                        copy(cnT[:, c * N:(c + 1) * N], bank[c][:, :]).then_inc(cnT_sb, 1)

            def t_copy(n):
                act.wait_ge(t_full, n + 1)
                if n >= 8:
                    act.wait_ge(s_full, 4 * (n // 4 - 1))
                copy(tT[(n // 4) % 2][n % 4][:, :], bank[2][:, :]).then_inc(t_sb, 1)

            def null_copies(g):
                act.wait_ge(misc_full, MISC.index(f"q0_{g}") + 1)
                copy(q0T[:, :], bank[5][0:HEADS, :]).then_inc(misc_read, 1)
                act.wait_ge(misc_full, MISC.index(f"s0_{g}") + 1)
                copy(ns0[:, GRP[g], :], bank[5][:, 0:GB * HEADS].rearrange("p (b h) -> p b h", b=GB),
                     scale=-1.0).then_inc(misc_read, 1)

            for n in range(4):
                t_copy(n)
                if n == 1:
                    null_copies(0)
            for k in range(STEPS + 3):
                if k + 4 < STEPS:
                    if k == 3:
                        act.wait_ge(x2T_full, 2)
                        act.activation(xnT[1][:, :], bank[2][:, :], ACT.Identity, bias=col(C_LN1B),
                                       scale=col(C_LN1S)).then_inc(xnT_sb, 1)
                    t_copy(k + 4)
                if k == 4:
                    null_copies(1)
                if k < STEPS:
                    act.wait_ge(nm_ready, k + 1)
                    if k >= 3:
                        act.wait_ge(pT_full, k - 2)
                    if k >= 2:
                        act.wait_ge(rr_ready, k - 1)
                    act.activation(pz[:, k % 2, :], d0[:, k % 2, :], ACT.Exp)
                    for i in range(4):
                        act.activation(pr[k % 3][:, i, :], bank[k % 2][:, i * P:(i + 1) * P], ACT.Exp,
                                       bias=nm[:, k % 2, i:i + 1],
                                       accum_out=rs[:, k % 2, i:i + 1]).then_inc(exp_done, 1)
                if k == 27:
                    act.wait_ge(misc_full, MISC.index("x3_0") + 1)
                    copy(x3T[0][:, :], bank[5][:, :]).then_inc(misc_read, 1)
                if k == 29:
                    act.wait_ge(sh_ready, 1)
                    act.activation(ex[:, :, :], sh[:, :, :], ACT.Exp).then_inc(ex_ready, 1)

            def high_part(g):
                act.wait_ge(misc_read, MISC.index(f"cT_{g}") + 1)
                act.wait_ge(prep, 10)
                copy(cTs[g][0:EXPERTS, :], cTf[g][:, :]).then_inc(chi_ready, 1)

            high_part(0)
            for g in range(NG):
                for n in range(9):
                    m = 9 * g + n
                    act.wait_ge(h1_full, m + 1)
                    if m >= 2:
                        act.wait_ge(su_done, m - 1)
                    act.activation(sa[m % 2][:, :], bank[m % 2][:, :], ACT.Silu,
                                   bias=col(C_BE1 + (n + 8) % 9)).then_inc(silu_done, 1)
                    if g == 0 and n == 3:
                        act.wait_ge(misc_full, MISC.index("x3_1") + 1)
                        copy(x3T[1][:, :], bank[5][:, :]).then_inc(misc_read, 1)
                    if g == 0 and n == 5:
                        act.wait_ge(sh_ready, 2)
                        act.activation(ex[:, :, :], sh[:, :, :], ACT.Exp).then_inc(ex_ready, 1)
                    if g == 0 and n == 8:
                        high_part(1)

        @block.vector
        def _(dve):
            links = 0

            def link(ins):
                nonlocal links
                links += 1
                ins.then_inc(dch, 1)
                dve.wait_ge(dch, links)

            norms = 0

            def norm(src, dst, event, scale, eps):
                nonlocal norms
                norms += 1
                for b in range(GB):
                    last = dve.bn_stats(stats[:, b, :], src(b))
                link(last)
                for b in range(GB):
                    last = dve.bn_aggr(mv[:, b, :], stats[:, b, :])
                link(last)
                dve.tensor_scalar(ve[:, :], mv[:, :, 1], scale, eps, op0=ALU.mult,
                                  op1=ALU.add).then_inc(var_ready, 1)
                dve.wait_ge(rstd_ready, norms)
                for b in range(GB):
                    last = dve.tensor_scalar(dst(b), src(b), mv[:, b, 0:1], rstd[:, b:b + 1],
                                             op0=ALU.subtract, op1=ALU.mult)
                last.then_inc(*event)

            def rows_of(g):
                return lambda b: xr[:, g * GB + b, :]

            dve.wait_ge(consts, 1)
            for g in range(NG):
                dve.wait_ge(ld[f"x{g}"], 16)
                norm(rows_of(g), lambda b: xh[g][:, b, :], (xh_ready, 1), 1.0, EPS0)

            dve.wait_ge(consts, NCONST)
            dve.wait_ge(ld["rows"], 16)
            dve.wait_ge(tanh_done, 1)

            for g in range(NG):
                dve.wait_ge(s0_full, g + 1)
                link(dve.tensor_tensor(sm[g][:, :, :], b4(4 + g), rep(band[:, :], GB), op=ALU.add))
                dve.tensor_reduce(nm0[:, g, :], sm[g][:, :, :], axis=AX.X, op=ALU.max,
                                  negate=True).then_inc(sm_ready, 1)
            dve.tensor_tensor(gwd[:, :], rows[:, R_GW:R_GW + P], rows[:, R_GW + P:R_GW + 2 * P],
                              op=ALU.subtract).then_inc(prep, 1)
            link(dve.tensor_tensor(b2bc[:, :], rows[:, R_B2:R_B2 + P], rows[:, R_B2 + P:R_B2 + 2 * P], op=ALU.add))
            dve.tensor_tensor(b2bc[:, :], b2bc[:, :], rows[:, R_B2 + 2 * P:R_B2 + 3 * P],
                              op=ALU.add).then_inc(prep, 1)
            dve.tensor_scalar(st[:, :], rows[:, R_LNOS:R_LNOS + P], tg[:, 1:2], None,
                              op0=ALU.mult).then_inc(prep, 1)
            dve.tensor_scalar(bt[:, :], rows[:, R_LNOB:R_LNOB + P], tg[:, 1:2], None,
                              op0=ALU.mult).then_inc(prep, 1)
            for r in range(2):
                half = slice(64 * r, 64 * r + 64)
                dve.tensor_copy(nvblk[half, :, :].rearrange("p c n -> p (c n)")[:, r:P:18],
                                cols[half, C_NV:C_NV + 1].to_broadcast([64, 8])).then_inc(prep, 1)
                dve.tensor_copy(nkblk[half, r:r + 1], cols[half, C_NK:C_NK + 1]).then_inc(prep, 1)
            for g in range(NG):
                dve.memset(cTs[g][:, :].bitcast(fp32), 0.0)

            def window_out(g):
                dve.wait_ge(o0_full, g + 1)
                dve.wait_ge(p0_ready, GB * (g + 1))
                link(dve.reciprocal(rr0[:, g, :], rs0[:, g, :]))
                link(dve.tensor_scalar(rr0[:, g, :], rr0[:, g, :], tg[:, 0:1], None, op0=ALU.mult))
                for b in range(GB):
                    last = dve.scalar_tensor_tensor(xr[:, g * GB + b, :], b4(2 + g)[:, b, :], rr0[:, g, b:b + 1],
                                                    xr[:, g * GB + b, :], op0=ALU.mult, op1=ALU.add)
                last.then_inc(x1_ready, 1)
                dve.wait_ge(x1_ready, g + 1)

            def mlp_input(g):
                norm(rows_of(g), lambda b: xh[g][:, b, :], (xh_ready, 1), 1.0, EPS0)
                dve.wait_ge(xh_ready, LN1 + g + 1)
                link(dve.tensor_tensor(gtmp[:, :, :], xh[g][:, :, :], rep(gwd[:, :], GB), op=ALU.mult))
                link(dve.tensor_reduce(gd[:, :], gtmp[:, :, :], axis=AX.X, op=ALU.add))
                link(dve.tensor_scalar(m0[:, :], gd[:, :], 0.0, None, op0=ALU.is_ge))
                link(dve.tensor_tensor(xm0[g][:, :, :], xh[g][:, :, :], bc(m0[:, :], P), op=ALU.mult))
                dve.tensor_tensor(xm1[g][:, :, :], xh[g][:, :, :], xm0[g][:, :, :],
                                  op=ALU.subtract).then_inc(fm_ready, 1)

            window_out(0)
            window_out(1)
            dve.wait_ge(prep, 8)
            mlp_input(0)
            mlp_input(1)
            dve.wait_ge(ld["small"], 48)
            link(dve.tensor_copy(maskf[:, :], mask8[:, :]))
            dve.tensor_scalar(maskb[:, :], maskf[:, :], -1.0, -MASKED, op0=ALU.add,
                              op1=ALU.mult).then_inc(prep, 1)
            dve.tensor_copy(selr[:, :], sel[:, :, :, :].rearrange("k c r m -> k (c r m)")).then_inc(prep, 1)
            dve.wait_ge(ld["ctx"], 16)
            for g in range(NG):
                norm(lambda b: ctx[:, g * GB + b, :], lambda b: cn[:, g * GB + b, :], (cn_raw, 1), 1.0, EPS1)

            def mlp_output(g):
                dve.wait_ge(acc_full, g + 1)
                link(dve.tensor_tensor(acc[:, :, :], b4(6 + g), rep(b2bc[:, :], GB), op=ALU.add))
                dve.scalar_tensor_tensor(xr[:, GRP[g], :], acc[:, :, :], tg[:, 2:3], xr[:, GRP[g], :],
                                         op0=ALU.mult, op1=ALU.add).then_inc(x2_ready, 1)
                dve.wait_ge(x2_ready, g + 1)
                norm(rows_of(g), lambda b: xh[g][:, b, :], (xh_ready, 1), 1.0 + EPS1, EPS0 * EPS1)

            mlp_output(0)
            mlp_output(1)

            def shift(s):
                g, hq, b = step(s)
                null = ns0[:, g * GB + b, 4 * hq:4 * hq + 4]
                dve.wait_ge(s_full, s + 1)
                if s == 0:
                    dve.wait_ge(misc_read, MISC.index("s0_0") + 1)
                if s == 16:
                    dve.wait_ge(misc_read, MISC.index("s0_1") + 1)
                if s >= 2:
                    dve.wait_ge(exp_done, 4 * (s - 1))
                link(dve.tensor_reduce(nmx[:, s % 2, :], b4(s % 2), axis=AX.X, op=ALU.max, negate=True))
                link(dve.tensor_tensor(nm[:, s % 2, :], nmx[:, s % 2, :], null, op=ALU.min))
                dve.tensor_tensor(d0[:, s % 2, :], nm[:, s % 2, :], null, op=ALU.subtract).then_inc(nm_ready, 1)

            def sums(s):
                g, hq, b = step(s)
                dve.wait_ge(exp_done, 4 * (s + 1))
                if s >= 2:
                    dve.wait_ge(pn_ready, s - 1)
                link(dve.tensor_tensor(rt[:, :], rs[:, s % 2, :], pz[:, s % 2, :], op=ALU.add))
                link(dve.reciprocal(rr[:, s % 2, :], rt[:, :]))
                dve.tensor_tensor(p0n[:, g * GB + b, 4 * hq:4 * hq + 4], pz[:, s % 2, :], rr[:, s % 2, :],
                                  op=ALU.mult).then_inc(rr_ready, 1)

            def probs_copy(s):
                dve.wait_ge(pT_full, s + 1)
                if s >= 2:
                    dve.wait_ge(u_full, s - 1)
                dve.tensor_copy(pT[s % 2][:, :], bank[3][:, :]).then_inc(pT_sb, 1)

            def gathered_copy(s):
                dve.wait_ge(u_full, s + 1)
                if s >= 2:
                    dve.wait_ge(out_done, s - 1)
                dve.tensor_copy(uT[s % 2][:, :], bank[4][:, :]).then_inc(u_sb, 1)

            def null_probs(g):
                dve.wait_ge(misc_full, MISC.index(f"p0_{g}") + 1)
                dve.tensor_copy(p0T[:, :], bank[5][0:HEADS, :]).then_inc(misc_read, 1)

            def attention_output(g):
                dve.wait_ge(o_full, g + 1)
                norm(lambda b: b4(6 + g)[:, b, :], lambda b: z[g][:, b, :], (o_read, 1), 1.0, EPS1)

            def moe_input(g):
                dve.wait_ge(x3_ready, g + 1)
                norm(rows_of(g), lambda b: xh[g][:, b, :], (xh_ready, 1), 1.0, EPS0)

            def two_largest(values, replaced):
                for b in range(GB):
                    last = dve.max(top8[:, b, :], values[:, b, :])
                link(last)
                link(dve.tensor_copy(want[:, :, 0:2], top8[:, :, 0:2]))
                for b in range(GB):
                    last = dve.match_replace(replaced[:, b, :], want[:, b, :], values[:, b, :], TAKEN)
                link(last)

            def gate_start(g):
                dve.wait_ge(misc_full, MISC.index(f"lg_{g}") + 1)
                lg = bank[5][:, 0:GB * EXPERTS].rearrange("p (b e) -> p b e", b=GB)
                link(dve.tensor_reduce(g4[:, :], lg, axis=AX.X, op=ALU.max))
                dve.tensor_tensor(sh[:, :, :], lg, bc(g4[:, :], EXPERTS), op=ALU.subtract).then_inc(sh_ready, 1)
                dve.wait_ge(sh_ready, g + 1)
                dve.sem_inc(misc_read, 1)

            def gate(g):
                dve.wait_ge(ex_ready, g + 1)
                link(dve.tensor_reduce(g4[:, :], ex[:, :, :], axis=AX.X, op=ALU.add))
                link(dve.reciprocal(g4r[:, :], g4[:, :]))
                link(dve.tensor_tensor(pb[:, :, :], ex[:, :, :], bc(g4r[:, :], EXPERTS), op=ALU.mult))
                link(dve.tensor_tensor(sc[:, :, :], pb[:, :, :], rep(rows[:, R_GB:R_GB + EXPERTS], GB), op=ALU.add))
                pairs = sc[:, :, :].rearrange("p b (g j k) -> p (b g) j k", g=4, j=2)
                dve.tensor_tensor(pmx[:, :, :], pairs[:, :, :, 0], pairs[:, :, :, 1], op=ALU.max)
                link(dve.tensor_tensor(pmn[:, :, :], pairs[:, :, :, 0], pairs[:, :, :, 1], op=ALU.min))
                dve.tensor_tensor(t1[:, :], pmx[:, :, 0], pmx[:, :, 1], op=ALU.max)
                dve.tensor_tensor(t2[:, :], pmx[:, :, 0], pmx[:, :, 1], op=ALU.min)
                link(dve.tensor_tensor(t3[:, :], pmn[:, :, 0], pmn[:, :, 1], op=ALU.max))
                link(dve.tensor_tensor(t2[:, :], t2[:, :], t3[:, :], op=ALU.max))
                link(dve.tensor_tensor(gsp[:, :, 0:4], t1[:, :].rearrange("p (b g) -> p b g", b=GB),
                                       t2[:, :].rearrange("p (b g) -> p b g", b=GB), op=ALU.add))
                two_largest(gsp, gsr)
                link(dve.tensor_scalar(keep[:, :, :], gsr[:, :, 0:4], TAKEN, None, op0=ALU.is_equal))
                link(dve.tensor_scalar(pen[:, :, :], keep[:, :, :], -1.0, -LOW, op0=ALU.add, op1=ALU.mult))
                flat = lambda t: t.rearrange("p b (g k) -> p (b g) k", g=4)
                kept = bc(keep[:, :, :].rearrange("p b g -> p (b g)"), 4)
                link(dve.tensor_tensor(flat(skp[:, :, :]), flat(sc[:, :, :]), kept, op=ALU.mult))
                for b in range(GB):
                    last = dve.tensor_tensor(msp[:, b, 0:EXPERTS].rearrange("p (g k) -> p g k", g=4),
                                             skp[:, b, :].rearrange("p (g k) -> p g k", g=4),
                                             bc(pen[:, b, :], 4), op=ALU.add)
                link(last)
                two_largest(msp, msr)
                dve.scalar_tensor_tensor(comb[g][:, :, :], msr[:, :, 0:EXPERTS], TAKEN, pb[:, :, :],
                                         op0=ALU.is_equal, op1=ALU.mult).then_inc(comb_ready, 1)

            def low_part(g):
                dve.wait_ge(misc_full, MISC.index(f"cT_{g}") + 1)
                dve.tensor_copy(cTf[g][:, :], bank[5][0:EXPERTS, :]).then_inc(misc_read, 1)
                dve.wait_ge(chi_ready, g + 1)
                dve.tensor_tensor(cTs[g][32:32 + EXPERTS, :], cTf[g][:, :],
                                  cTs[g][0:EXPERTS, :].bitcast(fp32), op=ALU.subtract).then_inc(c_ready, 1)

            def gated(g, n):
                m = 9 * g + n
                dve.wait_ge(silu_done, m + 1)
                dve.wait_ge(h3_full, m + 1)
                if n == 2 and g == 1:
                    dve.wait_ge(dn1_done, 10)
                if n == 2 and g == 0:
                    dve.wait_ge(dn1_done, 1)
                dve.scalar_tensor_tensor(su[m % 2][:, :], bank[2 + m % 2][:, :], col(C_BE3 + (n + 8) % 9),
                                         sa[m % 2][:, :], op0=ALU.add, op1=ALU.mult).then_inc(su_done, 1)
                if n:
                    k = 8 * g + n - 1
                    dve.wait_ge(cb_full, k + 1)
                    dve.wait_ge(su_done, m + 1)
                    if n > 2:
                        dve.wait_ge(dn1_done, 9 * g + n - 1)
                    elif g:
                        dve.wait_ge(dn1_done, 9)
                    dve.tensor_tensor(hc[n % 2][:, :], su[m % 2][:, :], bank[4][:, :],
                                      op=ALU.mult).then_inc(hc_done, 1)

            def moe_output(g):
                dve.wait_ge(y_full, g + 1)
                link(dve.tensor_tensor(acc[:, :, :], b4(6 + g), rep(rows[:, R_BS2:R_BS2 + P], GB), op=ALU.add))
                dve.scalar_tensor_tensor(xr[:, GRP[g], :], acc[:, :, :], tg[:, 3:4], xr[:, GRP[g], :],
                                         op0=ALU.mult, op1=ALU.add).then_inc(x4_ready, 1)

            for k in range(STEPS + 4):
                if 1 <= k <= STEPS:
                    sums(k - 1)
                if k < STEPS:
                    shift(k)
                if 2 <= k < STEPS + 2:
                    probs_copy(k - 2)
                if k in (17, 33):
                    null_probs((k - 17) // 16)
                if 3 <= k < STEPS + 3:
                    gathered_copy(k - 3)
                if k == 20:
                    attention_output(0)
                if k == 23:
                    moe_input(0)
                if k == 28:
                    gate_start(0)
                if k == 29:
                    gate(0)
                if k == 31:
                    low_part(0)
            attention_output(1)
            for n in range(9):
                gated(0, n)
                if n == 1:
                    moe_input(1)
                if n == 4:
                    gate_start(1)
                if n == 5:
                    gate(1)
            low_part(1)
            moe_output(0)
            for n in range(9):
                gated(1, n)
            moe_output(1)


def kernel(x, ctx_1024, mask_BxS2_bf1, g_xattn, g_ffn, L0_xattn_W_reduce, L0_xattn_b_reduce,
           L0_ffn_gate_w, L0_ffn_w1, L0_ffn_b1, L0_ffn_w2, L0_ffn_b2, L0_ffn_sw1, L0_ffn_sb1,
           L0_ffn_sw2, L0_ffn_sb2, L1_xattn_ln1_s, L1_xattn_ln1_b, L1_xattn_lnc_s, L1_xattn_lnc_b,
           L1_xattn_Wq, L1_xattn_Wkv, L1_xattn_null_kv, L1_xattn_Wo, L1_xattn_lno_s,
           L1_xattn_lno_b, L1_ffn_gate_w, L1_ffn_gate_b, L1_ffn_We1, L1_ffn_be1, L1_ffn_We2,
           L1_ffn_be2, L1_ffn_We3, L1_ffn_be3, L1_ffn_ws1, L1_ffn_bs1, L1_ffn_ws2, L1_ffn_bs2,
           L1_ffn_ws3, L1_ffn_bs3):
    import numpy as np
    import concourse.bacc as bacc
    from concourse.bass_utils import run_bass_kernel_spmd

    A = np.asarray
    x, ctx = A(x), A(ctx_1024)
    inner = HEADS * 64

    def by_partition(w):
        w = A(w)
        return w.reshape(-1, P, w.shape[-1]).transpose(1, 0, 2)

    def chunks(w):
        return A(w).reshape(P, -1, P)

    experts = lambda w: A(w).transpose(1, 0, 2).reshape(P, -1)
    wkv = A(L1_xattn_Wkv)
    cols = np.concatenate([
        A(L0_xattn_b_reduce)[None], A(L0_ffn_b1).reshape(-1, P), A(L0_ffn_sb1).reshape(-1, P),
        A(L1_xattn_ln1_s)[None], A(L1_xattn_ln1_b)[None],
        A(L1_ffn_be1).reshape(-1, P), A(L1_ffn_bs1)[None],
        A(L1_ffn_be3).reshape(-1, P), A(L1_ffn_bs3)[None],
        A(L1_xattn_null_kv)[[0, 0]].reshape(1, P), A(L1_xattn_null_kv)[[1, 1]].reshape(1, P)]).T
    rows = np.concatenate([A(a).reshape(-1) for a in (
        L0_ffn_gate_w, L0_ffn_b2, L0_ffn_sb2, L1_xattn_lnc_s, L1_xattn_lnc_b, L1_xattn_lno_s,
        L1_xattn_lno_b, L1_ffn_bs2, L1_ffn_gate_b, g_xattn, g_ffn)])
    w1 = np.concatenate([A(L0_ffn_w1).transpose(1, 0, 2).reshape(P, -1), A(L0_ffn_sw1)], 1)
    w2 = np.concatenate([A(L0_ffn_w2).reshape(-1, P), A(L0_ffn_sw2)])
    data = {
        "in_x": x.transpose(1, 0, 2),
        "in_ctx": ctx.transpose(1, 0, 2),
        "in_ctxT": ctx.reshape(-1, P).T,
        "in_wredT": A(L0_xattn_W_reduce).T,
        "in_cols": cols,
        "in_rows": rows,
        "in_w1": chunks(w1),
        "in_w2": by_partition(w2),
        "in_wqT": by_partition(A(L1_xattn_Wq).T),
        "in_wkT": by_partition(wkv[:, :inner].T),
        "in_wvT": by_partition(wkv[:, inner:].T),
        "in_wo": by_partition(L1_xattn_Wo),
        "in_gw": A(L1_ffn_gate_w).T,
        "in_we1": chunks(np.concatenate([experts(L1_ffn_We1), A(L1_ffn_ws1)], 1)),
        "in_we3": chunks(np.concatenate([experts(L1_ffn_We3), A(L1_ffn_ws3)], 1)),
        "in_we2": by_partition(np.concatenate([A(L1_ffn_We2).reshape(-1, P), A(L1_ffn_ws2)])),
        "in_be2": A(L1_ffn_be2),
        "in_mask": A(mask_BxS2_bf1).reshape(1, -1).view(np.uint8),
    }
    data = {k: np.ascontiguousarray(v) for k, v in data.items()}
    nc = bacc.Bacc("TRN2", target_bir_lowering=False, num_devices=1)
    args = [nc.dram_tensor(k, v.shape, mybir.dt.from_np(v.dtype), kind="ExternalInput").ap()
            for k, v in data.items()]
    out = nc.dram_tensor("out_x", (P, B, P), mybir.dt.float32, kind="ExternalOutput").ap()
    gated_layers(nc, *args, out)
    r = run_bass_kernel_spmd(nc, [data], core_ids=[0])
    return r.results[0]["out_x"].transpose(1, 0, 2)
```

```python
import concourse.bass as bass
from concourse import mybir
from contextlib import ExitStack

P = 128
B = 8
GB = 4
NG = B // GB
N = GB * P
HEADS = 16
QUADS = HEADS // 4
WINDOW = 20
FC = 4
EXPERTS = 16
EC = 8
STEPS = NG * QUADS * GB
NEG_BIG = -100000000.0
MASKED = -1e30
PAD = -2e38
LOW = -1e38
TAKEN = -3e38
EPS0, EPS1 = 1e-5, 1e-6

C_BRED, C_B1, C_LN1S, C_LN1B, C_BE1, C_BE3, C_NK, C_NV, NCOLS = 0, 1, 13, 14, 15, 24, 33, 34, 35
R_GW, R_B2, R_LNCS, R_LNCB, R_LNOS, R_LNOB, R_BS2, R_GB, R_G, NROWS = (
    0, 256, 640, 768, 896, 1024, 1152, 1280, 1296, 1300)
MISC = ["q0_0", "s0_0", "x2_1", "q0_1", "s0_1", "p0_0", "x3_0", "lg_0", "cT_0", "p0_1", "x3_1", "lg_1", "cT_1"]


def gated_layers(nc, x, ctx_in, ctxT_in, wredT_in, cols_in, rows_in, w1_in, w2_in, wqT_in, wkT_in,
                 wvT_in, wo_in, gw_in, we1_in, we3_in, we2_in, be2_in, mask_in, out):
    fp32, fp32r, bf16, u8 = mybir.dt.float32, mybir.dt.float32r, mybir.dt.bfloat16, mybir.dt.uint8
    ALU = mybir.AluOpType
    ACT = mybir.ActivationFunctionType
    AX = mybir.AxisListType

    with ExitStack() as stack:
        def sb(name, shape, dt=fp32):
            return stack.enter_context(nc.sbuf_tensor(name, shape, dt))

        def sem(name):
            return stack.enter_context(nc.semaphore(name))

        xr = sb("xr", [P, B, P])
        ctx = sb("ctx", [P, B, P])
        ctxT = sb("ctxT", [P, B * P])
        wredT = sb("wredT", [P, P])
        cols = sb("cols", [P, NCOLS])
        rows = sb("rows", [P, NROWS])
        w1 = sb("w1", [P, 3 * FC, P])
        w2 = sb("w2", [P, 3 * FC, P])
        gw = sb("gw", [P, EXPERTS])
        be2 = sb("be2", [EXPERTS, P])
        mask8 = sb("mask8", [1, B * P], u8)
        late = sb("late", [P, 3 * (EC + 1), P])
        wqT, wvT = late[:, 0:8, :], late[:, 8:16, :]
        we1, we3, we2 = (late[:, k * (EC + 1):(k + 1) * (EC + 1), :] for k in range(3))
        shared = sb("shared", [P, 10 * N])
        wkblk, woblk = (shared[:, k * 4 * N:(k + 1) * 4 * N].rearrange("p (c r n) -> p c r n", c=8, r=2)
                        for k in range(2))
        part = [shared[:, k * N:(k + 1) * N] for k in range(10)]
        ident = sb("ident", [P, P])
        band = sb("band", [P, P])
        mhalf = sb("mhalf", [P, GB])
        ones = sb("ones", [1, P], bf16)
        selr = sb("selr", [64, EC * P], fp32r)
        maskb = sb("maskb", [1, B * P], bf16)
        nvblk = sb("nvblk", [P, 8, 16])
        nkblk = sb("nkblk", [P, 2])
        gwd = sb("gwd", [P, P])
        b2bc = sb("b2bc", [P, P])
        tg = sb("tg", [P, 4])
        st = sb("st", [P, P])
        bt = sb("bt", [P, P])
        G = [sb(f"G{k}", [P, HEADS, P], fp32r) for k in range(2)]
        wnull = [sb(f"wnull{k}", [P, HEADS], fp32r) for k in range(2)]
        gws = [sb(f"gws{k}", [P, EXPERTS], fp32r) for k in range(2)]
        cns = [sb(f"cns{k}", [P, B, P], fp32r) for k in range(2)]
        ups = sb("ups", [P, 4 * (EC + 1), P], fp32r)
        w1s = [ups[:, k * 12:k * 12 + 12, :] for k in range(2)]
        we1s, we3s = ([ups[:, (2 * m + k) * (EC + 1):(2 * m + k + 1) * (EC + 1), :] for k in range(2)]
                      for m in range(2))
        turned = sb("turned", [P, 12 * N], fp32r)

        def pair(k):
            return [turned[:, (2 * k + i) * N:(2 * k + i + 1) * N] for i in range(2)]

        wnf = sb("wnf", [P, HEADS])
        Wvo = sb("Wvo", [P, HEADS, P])
        nw = sb("nw", [HEADS, P])
        stats = sb("stats", [P, GB, 6])
        mv = sb("mv", [P, 2, GB, 2])
        ve = sb("ve", [P, 2, GB])
        rstd = sb("rstd", [P, 2, GB])
        xh = [sb(f"xh{g}", [P, GB, P]) for g in range(NG)]
        xm0 = [sb(f"xma{g}", [P, GB, P]) for g in range(NG)]
        xm1 = [sb(f"xmb{g}", [P, GB, P]) for g in range(NG)]
        raw = [t[:, :, :].rearrange("p b n -> p (b n)") for t in xm1]
        gd = sb("gd", [P, GB])
        m0 = sb("m0", [P, GB])
        xT = [sb(f"xT{g}", [P, N]) for g in range(NG)]
        krT = [sb(f"krT{g}", [P, N]) for g in range(NG)]
        sm = [sb(f"sm{g}", [P, GB, P]) for g in range(NG)]
        nm0 = sb("nm0", [P, NG, GB])
        rs0 = sb("rs0", [P, NG, GB])
        rr0 = sb("rr0", [P, NG, GB])
        p0 = [sb(f"p0{g}", [P, GB, P]) for g in range(NG)]
        pT0 = [sb(f"pT0{g}", [P, N]) for g in range(NG)]
        fT = [[pair(3 * g + k) for k in range(3)] for g in range(NG)]
        hT = part[0:4]
        acc = sb("acc", [P, GB, P])
        gtmp = acc
        cnT = sb("cnT", [P, B * P])
        xnT = [pair(0), pair(1)]
        q0T = sb("q0T", [HEADS, N])
        ns0 = sb("ns0", [P, B, HEADS])
        tT = [[t[:, :] for t in (xT[0], xT[1], krT[0], krT[1])],
              [t[:, :, :].rearrange("p b n -> p (b n)") for t in (sm[0], sm[1], p0[0], p0[1])]]
        nmx = sb("nmx", [P, 2, 4])
        nm = sb("nm", [P, 2, 4])
        d0 = sb("d0", [P, 2, 4])
        pr = [part[4 + k].rearrange("p (i n) -> p i n", i=4) for k in range(3)]
        rs = sb("rs", [P, 2, 4])
        pz = sb("pz", [P, 2, 4])
        rt = sb("rt", [P, 4])
        rr = sb("rr", [P, 2, 4])
        p0n = sb("p0n", [P, B, HEADS])
        p0T = part[9][0:HEADS, :]
        pT = [pair(2), pair(3)]
        uT = part[7:9]
        z = [pT0[g][:, :].rearrange("p (b n) -> p b n", b=GB) for g in range(NG)]
        xb = xm0
        x3T = [pair(4), pair(5)]
        sh = sb("sh", [P, GB, EXPERTS])
        ex = sb("ex", [P, GB, EXPERTS])
        pb = sb("pb", [P, GB, EXPERTS])
        sc = sb("sc", [P, GB, EXPERTS])
        g4 = sb("g4", [P, GB])
        g4r = sb("g4r", [P, GB])
        pmx = sb("pmx", [P, 16, 2])
        pmn = sb("pmn", [P, 16, 2])
        t1 = sb("t1", [P, 16])
        t2 = sb("t2", [P, 16])
        t3 = sb("t3", [P, 16])
        gsp = sb("gsp", [P, GB, 12])
        gsr = sb("gsr", [P, GB, 12])
        top8 = sb("top8", [P, GB, 8])
        want = sb("want", [P, GB, 8])
        keep = sb("keep", [P, GB, 4])
        pen = sb("pen", [P, GB, 4])
        skp = sb("skp", [P, GB, EXPERTS])
        msp = sb("msp", [P, GB, 24])
        msr = sb("msr", [P, GB, 24])
        comb = [sb(f"comb{g}", [P, GB, EXPERTS]) for g in range(NG)]
        cTf = [sb(f"cTf{g}", [EXPERTS, N]) for g in range(NG)]
        cTs = [sb(f"cTs{g}", [64, N], fp32r) for g in range(NG)]
        sa, su, hc = hT[0:2], hT[2:4], [t[:, :] for t in (xT[0], xT[1])]
        bank = [stack.enter_context(nc.psum_tensor(f"bank{k}", [P, N], fp32)) for k in range(8)]

        ld = {n: sem("ld_" + n) for n in
              ["x0", "x1", "ctx", "ctxT", "wredT", "cols", "rows", "w1", "w2", "wqk", "wvo", "moe", "small"]}
        consts = sem("consts")
        prep = sem("prep")
        tanh_done = sem("tanh_done")
        var_ready = sem("var_ready")
        rstd_ready = sem("rstd_ready")
        dch = sem("dve_chain")
        xh_ready = sem("xh_ready")
        kr_full, kr_sb = sem("kr_full"), sem("kr_sb")
        xT_full, xT_sb = sem("xT_full"), sem("xT_sb")
        s0_full, sm_ready = sem("s0_full"), sem("sm_ready")
        p0_ready = sem("p0_ready")
        pT0_full, pT0_sb = sem("pT0_full"), sem("pT0_sb")
        o0_full, x1_ready = sem("o0_full"), sem("x1_ready")
        blk_clear = sem("blk_clear")
        blk_clear2 = sem("blk_clear2")
        gw_full, gw_sb = sem("gw_full"), sem("gw_sb")
        gw_lo = sem("gw_lo")
        w1_hi, w1_lo = sem("w1_hi"), sem("w1_lo")
        we_hi, we_lo = sem("we_hi"), sem("we_lo")
        cn_hi, cn_lo = sem("cn_hi"), sem("cn_lo")
        fT_hi, xn_raw, xn_hi = sem("fT_hi"), sem("xn_raw"), sem("xn_hi")
        pT_hi, x3_hi, x3T_sb = sem("pT_hi"), sem("x3_hi"), sem("x3T_sb")
        fm_ready = sem("fm_ready")
        fT_full, fT_sb = sem("fT_full"), sem("fT_sb")
        up_full, h_sb, dn_done = sem("up_full"), sem("h_sb"), sem("dn_done")
        acc_full, x2_ready = sem("acc_full"), sem("x2_ready")
        cn_raw, cn_ready = sem("cn_raw"), sem("cn_ready")
        cnT_full, cnT_sb = sem("cnT_full"), sem("cnT_sb")
        x2T_full, xnT_sb = sem("x2T_full"), sem("xnT_sb")
        misc_full, misc_read = sem("misc_full"), sem("misc_read")
        t_full, t_sb = sem("t_full"), sem("t_sb")
        s_full, nm_ready, exp_done = sem("s_full"), sem("nm_ready"), sem("exp_done")
        rr_ready, pn_ready = sem("rr_ready"), sem("pn_ready")
        pT_full, pT_sb = sem("pT_full"), sem("pT_sb")
        u_full, u_sb = sem("u_full"), sem("u_sb")
        out_done, o_full, o_read = sem("out_done"), sem("o_full"), sem("o_read")
        xb_ready, x3_ready = sem("xb_ready"), sem("x3_ready")
        sh_ready, ex_ready, comb_ready = sem("sh_ready"), sem("ex_ready"), sem("comb_ready")
        chi_ready, c_ready = sem("chi_ready"), sem("c_ready")
        h1_full, h3_full, cb_full = sem("h1_full"), sem("h3_full"), sem("cb_full")
        silu_done, su_done, hc_done = sem("silu_done"), sem("su_done"), sem("hc_done")
        dn1_done, y_full = sem("dn1_done"), sem("y_full")
        x4_ready, stored = sem("x4_ready"), sem("stored")

        NCONST = 16
        LN0, LN1, LN2, LNX = 0, 2, 4, 6
        GRP = [slice(g * GB, (g + 1) * GB) for g in range(NG)]

        def bc(ap, n):
            return ap.unsqueeze(2).to_broadcast([ap.shape[0], ap.shape[1], n])

        def rep(ap, n):
            return ap.unsqueeze(1).to_broadcast([ap.shape[0], n, ap.shape[1]])

        def b4(k):
            return bank[k][:, :].rearrange("p (b n) -> p b n", b=GB)

        def col(k):
            return cols[:, k:k + 1]

        def misc_uses(name):
            return MISC.index(name) + 1 - (MISC.index(name) > MISC.index("x2_1"))

        def t_bank(n):
            return 2 + n if n < 3 else 2

        def step(s):
            return s // 16, (s // 4) % 4, s % 4

        block = stack.enter_context(nc.Block())

        @block.sync
        def _(sp):
            sp.dma_start(xr[:, GRP[0], :], x[:, GRP[0], :]).then_inc(ld["x0"], 16)
            sp.dma_start(wredT[:, :], wredT_in).then_inc(ld["wredT"], 16)
            sp.dma_start(ctxT[:, :], ctxT_in).then_inc(ld["ctxT"], 16)
            sp.dma_start(cols[:, :], cols_in).then_inc(ld["cols"], 16)
            sp.dma_start(xr[:, GRP[1], :], x[:, GRP[1], :]).then_inc(ld["x1"], 16)
            sp.dma_start(wqT, wqT_in).then_inc(ld["wqk"], 16)
            sp.wait_ge(blk_clear, 1)
            for r in range(2):
                half = slice(64 * r, 64 * r + 64)
                sp.dma_start(wkblk[half, :, r, :], wkT_in[half, :, :]).then_inc(ld["wqk"], 16)
            sp.dma_start(rows[:, :], rows_in.partition_broadcast(P)).then_inc(ld["rows"], 16)
            sp.dma_start(ctx[:, :, :], ctx_in).then_inc(ld["ctx"], 16)
            sp.dma_start(wvT, wvT_in).then_inc(ld["wvo"], 16)
            sp.wait_ge(blk_clear2, 1)
            for r in range(2):
                half = slice(64 * r, 64 * r + 64)
                sp.dma_start(woblk[half, :, r, :], wo_in[half, :, :]).then_inc(ld["wvo"], 16)
            sp.dma_start(w1[:, :, :], w1_in).then_inc(ld["w1"], 16)
            sp.dma_start(w2[:, :, :], w2_in).then_inc(ld["w2"], 16)
            sp.dma_start(mask8[:, :], mask_in).then_inc(ld["small"], 16)
            sp.dma_start(gw[:, :], gw_in).then_inc(ld["small"], 16)
            sp.dma_start(be2[:, :], be2_in).then_inc(ld["small"], 16)
            sp.wait_ge(gw_full, 9)
            sp.dma_start(we1, we1_in).then_inc(ld["moe"], 16)
            sp.dma_start(we3, we3_in).then_inc(ld["moe"], 16)
            sp.dma_start(we2, we2_in).then_inc(ld["moe"], 16)
            for g in range(NG):
                sp.wait_ge(x4_ready, g + 1)
                sp.dma_start(out[:, GRP[g], :], xr[:, GRP[g], :]).then_inc(stored, 16)
            sp.wait_ge(stored, 16 * NG)

        @block.gpsimd
        def _(pool):
            done = 0

            def put(ins, wait=False):
                nonlocal done
                done += 1
                ins.then_inc(consts, 1)
                if wait:
                    pool.wait_ge(consts, done)

            put(pool.memset(mhalf[:, :], -0.5))
            put(pool.memset(ident[:, :], 0.0), True)
            put(pool.affine_select(out=ident[:, :], in_=ident[:, :], compare_op=ALU.not_equal, fill=1.0,
                                   base=0, pattern=[[-1, P]], channel_multiplier=1))
            put(pool.memset(band[:, :], 0.0), True)
            put(pool.affine_select(out=band[:, :], in_=band[:, :], compare_op=ALU.is_ge, fill=NEG_BIG,
                                   base=WINDOW, pattern=[[-1, P]], channel_multiplier=1), True)
            put(pool.affine_select(out=band[:, :], in_=band[:, :], compare_op=ALU.is_ge, fill=NEG_BIG,
                                   base=WINDOW, pattern=[[1, P]], channel_multiplier=-1))
            put(pool.memset(ones[:, :], 1.0))
            put(pool.memset(selr[:, :].bitcast(fp32), 0.0), True)
            for half in range(2):
                put(pool.affine_select(out=selr[:, :].rearrange("k (c r m) -> k c r m", c=EC, r=2),
                                       in_=selr[:, :].bitcast(fp32).rearrange("k (c r m) -> k c r m", c=EC, r=2),
                                       compare_op=ALU.not_equal, fill=1.0, base=-32 * half, pattern=[[-2, EC], [-1, 2], [0, 64]],
                                       channel_multiplier=1), True)
            put(pool.memset(nvblk[:, :, :], 0.0))
            put(pool.memset(nkblk[:, :], 0.0))
            put(pool.memset(gsp[:, :, :], PAD))
            put(pool.memset(msp[:, :, :], PAD))
            put(pool.memset(want[:, :, :], PAD))
            put(pool.memset(rs0[:, :, :], 0.0))
            pool.memset(shared[:, 4 * N:8 * N], 0.0).then_inc(blk_clear2, 1)
            assert done == NCONST

            n_ln = 0

            def power():
                nonlocal n_ln
                n_ln += 1
                pool.wait_ge(var_ready, n_ln)
                k = (n_ln - 1) % 2
                pool.tensor_tensor(rstd[:, k, :], ve[:, k, :], mhalf[:, :], op=ALU.pow).then_inc(rstd_ready, 1)

            power()
            power()
            for n in range(4):
                pool.wait_ge(gw_sb, n + 1)
                pool.tensor_tensor(G[1][:, 4 * n:4 * n + 4, :],
                                   raw[n % 2].rearrange("p (i n) -> p i n", i=4),
                                   G[0][:, 4 * n:4 * n + 4, :].bitcast(fp32),
                                   op=ALU.subtract).then_inc(gw_lo, 1)
            power()
            pool.wait_ge(gw_sb, 9)
            pool.tensor_tensor(wnull[1][:, :], wnf[:, :], wnull[0][:, :].bitcast(fp32),
                               op=ALU.subtract).then_inc(gw_lo, 1)
            for n, k in enumerate((2, 0, 1)):
                pool.wait_ge(w1_hi, n + 1)
                pool.tensor_tensor(w1s[1][:, 4 * k:4 * k + 4, :], w1[:, 4 * k:4 * k + 4, :],
                                   w1s[0][:, 4 * k:4 * k + 4, :].bitcast(fp32),
                                   op=ALU.subtract).then_inc(w1_lo, 1)
            power()
            for g in range(NG):
                power()
                pool.wait_ge(cn_raw, g + 1)
                pool.tensor_tensor(ctx[:, GRP[g], :], ctx[:, GRP[g], :], rep(rows[:, R_LNCS:R_LNCS + P], GB),
                                   op=ALU.mult).then_inc(cn_ready, 1)
                pool.wait_ge(cn_ready, 2 * g + 1)
                pool.tensor_tensor(ctx[:, GRP[g], :], ctx[:, GRP[g], :], rep(rows[:, R_LNCB:R_LNCB + P], GB),
                                   op=ALU.add).then_inc(cn_ready, 1)

            def context_low(g):
                pool.wait_ge(cn_hi, g + 1)
                pool.tensor_tensor(cns[1][:, GRP[g], :], ctx[:, GRP[g], :],
                                   cns[0][:, GRP[g], :].bitcast(fp32), op=ALU.subtract).then_inc(cn_lo, 1)

            def attention_input(g):
                power()
                pool.wait_ge(x2_ready, g + 1)
                pool.wait_ge(prep, 10)
                pool.tensor_tensor(xb[g][:, :, :], xr[:, GRP[g], :], rep(bt[:, :], GB),
                                   op=ALU.add).then_inc(xb_ready, 1)

            def normalise(s):
                pool.wait_ge(rr_ready, s + 1)
                pool.tensor_tensor(pr[s % 3][:, :, :], pr[s % 3][:, :, :], bc(rr[:, s % 2, :], P),
                                   op=ALU.mult).then_inc(pn_ready, 1)

            def output_gain(g):
                pool.wait_ge(o_read, g + 1)
                pool.tensor_tensor(z[g][:, :, :], z[g][:, :, :], rep(st[:, :], GB),
                                   op=ALU.mult).then_inc(xb_ready, 1)

            def output_add(g):
                pool.wait_ge(xb_ready, NG + g + 1)
                pool.tensor_tensor(xr[:, GRP[g], :], z[g][:, :, :], xb[g][:, :, :],
                                   op=ALU.add).then_inc(x3_ready, 1)

            context_low(0)
            context_low(1)
            attention_input(0)
            attention_input(1)
            for k in range(STEPS + 8):
                if 1 <= k <= STEPS:
                    normalise(k - 1)
                if k in (20, 36, 23, 39):
                    power()
                if k in (21, 37):
                    output_gain((k - 21) // 16)
                if k in (22, 38):
                    output_add((k - 22) // 16)
                if 8 <= k < 14:
                    m, third = divmod(k - 8, 3)
                    cut = slice(3 * third, 3 * third + 3)
                    pool.wait_ge(we_hi, k - 7)
                    pool.tensor_tensor((we1s, we3s)[m][1][:, cut, :], (we1, we3)[m][:, cut, :],
                                       (we1s, we3s)[m][0][:, cut, :].bitcast(fp32),
                                       op=ALU.subtract).then_inc(we_lo, 1)

        @block.tensor
        def _(pe):
            def product(dst, a, b, start=True):
                pe.matmul(dst, a[0], b[0], start=start, stop=False)
                pe.matmul(dst, a[0], b[1], start=False, stop=False)
                return pe.matmul(dst, a[1], b[0], start=False, stop=True)

            def window_keys(g):
                pe.matmul(bank[g][:, :], wredT[:, :], ctxT[:, g * N:(g + 1) * N],
                          start=True, stop=True).then_inc(kr_full, 1)

            def window_rows(g):
                pe.wait_ge(xh_ready, LN0 + g + 1)
                for b in range(GB):
                    mm = pe.transpose(bank[2 + g][:, b * P:(b + 1) * P], xh[g][:, b, :], ident[:, :])
                mm.then_inc(xT_full, 1)

            def window_scores(g):
                pe.wait_ge(kr_sb, g + 1)
                pe.wait_ge(xT_sb, g + 1)
                for b in range(GB):
                    mm = pe.matmul(bank[4 + g][:, b * P:(b + 1) * P], xT[g][:, b * P:(b + 1) * P],
                                   krT[g][:, b * P:(b + 1) * P], start=True, stop=True)
                mm.then_inc(s0_full, 1)

            def window_turn(g):
                pe.wait_ge(p0_ready, GB * (g + 1))
                for b in range(GB):
                    mm = pe.transpose(bank[g][:, b * P:(b + 1) * P], p0[g][:, b, :], ident[:, :])
                mm.then_inc(pT0_full, 1)

            def window_values(g):
                pe.wait_ge(pT0_sb, g + 1)
                pe.wait_ge(ld["ctx"], 16)
                for b in range(GB):
                    mm = pe.matmul(bank[2 + g][:, b * P:(b + 1) * P], pT0[g][:, b * P:(b + 1) * P],
                                   ctx[:, g * GB + b, :], start=True, stop=True)
                mm.then_inc(o0_full, 1)

            def fold(n):
                pe.wait_ge(ld["wqk" if n < 4 else "wvo"], 48)
                if n >= 2:
                    pe.wait_ge(gw_sb, n - 1)
                left, right = (wqT, wkblk) if n < 4 else (wvT, woblk)
                for i in range(2):
                    c = 2 * (n % 4) + i
                    mm = pe.matmul(bank[6 + n % 2][:, 2 * i * P:2 * (i + 1) * P], left[:, c, :],
                                   right[:, c, :, :], start=True, stop=True)
                mm.then_inc(gw_full, 1)

            def fold_null():
                pe.wait_ge(gw_sb, 7)
                pe.wait_ge(prep, 8)
                for c in range(8):
                    pe.matmul(bank[6][:, 2 * c:2 * c + 2], wqT[:, c, :], nkblk[:, :], start=True, stop=True)
                for c in range(8):
                    for r in range(2):
                        mm = pe.matmul(bank[6][0:HEADS, P:2 * P], nvblk[:, c, :], woblk[:, c, r, :],
                                       start=(c == r == 0), stop=(c == 7 and r == 1))
                mm.then_inc(gw_full, 1)

            pe.wait_ge(ld["wredT"], 16)
            pe.wait_ge(ld["ctxT"], 16)
            window_keys(0)
            window_keys(1)
            pe.wait_ge(consts, NCONST)
            window_rows(0)
            fold(0)
            window_rows(1)
            window_scores(0)
            window_scores(1)
            fold(1)
            fold(2)
            window_turn(0)
            fold(3)
            window_turn(1)
            window_values(0)
            fold(4)
            window_values(1)
            fold(5)
            fold(6)
            fold(7)
            fold_null()

            def misc(name):
                if MISC.index(name):
                    pe.wait_ge(misc_read, MISC.index(name))

            def mlp_rows(g):
                if g:
                    pe.wait_ge(fT_sb, 3 * g)
                pe.wait_ge(fm_ready, g + 1)
                for k, src in enumerate((xh[g], xm0[g], xm1[g])):
                    for b in range(GB):
                        mm = pe.transpose(bank[k][:, b * P:(b + 1) * P], src[:, b, :], ident[:, :])
                    mm.then_inc(fT_full, 1)

            def mlp_up(g, j):
                u = 12 * g + j
                kind, c = j // FC, (j + 8) % 12
                pe.wait_ge(fT_sb, 3 * g + kind + 1)
                if u >= 3:
                    pe.wait_ge(h_sb, u - 2)
                if g == 0:
                    pe.wait_ge(w1_lo, kind + 1)
                product(bank[3 + u % 3][:, :], [w[:, c, :] for w in w1s], fT[g][kind]).then_inc(up_full, 1)

            def mlp_down(g, j):
                u = 12 * g + j
                pe.wait_ge(h_sb, u + 1)
                for b in range(GB):
                    mm = pe.matmul(bank[6 + g][:, b * P:(b + 1) * P], hT[u % 4][:, b * P:(b + 1) * P],
                                   w2[:, (j + 8) % 12, :], start=(j == 0 and b == 0), stop=(j == 11),
                                   skip_group_check=True)
                mm.then_inc(dn_done if j < 11 else acc_full, 1)

            def context_rows(g):
                pe.wait_ge(fT_sb, 5)
                pe.wait_ge(cn_ready, 2 * g + 2)
                for b in range(GB):
                    mm = pe.transpose(bank[g][:, b * P:(b + 1) * P], ctx[:, g * GB + b, :], ident[:, :])
                mm.then_inc(cnT_full, 1)

            def attention_rows(g):
                if g == 0:
                    pe.wait_ge(fT_sb, 6)
                else:
                    misc("x2_1")
                pe.wait_ge(xh_ready, LN2 + g + 1)
                for b in range(GB):
                    mm = pe.transpose(bank[2 + 3 * g][:, b * P:(b + 1) * P], xh[g][:, b, :], ident[:, :])
                mm.then_inc(x2T_full, 1)

            mlp_rows(0)
            pe.wait_ge(x1_ready, NG)
            pe.wait_ge(gw_sb, 9)
            pe.wait_ge(ld["w2"], 16)
            for g in range(NG):
                for j in range(14):
                    if j < 12:
                        mlp_up(g, j)
                    if j == 7 and g == 0:
                        mlp_rows(1)
                    if j in (1, 4) and g == 1:
                        context_rows(j // 4)
                    if j == 9 and g == 1:
                        attention_rows(0)
                    if j >= 2:
                        mlp_down(g, j - 2)

            def null_scores(g):
                misc(f"q0_{g}")
                pe.wait_ge(xnT_sb, g + 1)
                product(bank[5][0:HEADS, :], [w[:, :] for w in wnull], xnT[g]).then_inc(misc_full, 1)

            def turn_null_scores(g):
                misc(f"s0_{g}")
                for b in range(GB):
                    mm = pe.transpose(bank[5][:, b * HEADS:(b + 1) * HEADS], q0T[:, b * P:(b + 1) * P],
                                      ident[0:HEADS, 0:HEADS])
                mm.then_inc(misc_full, 1)

            def fold_query(n):
                if n > 3:
                    pe.wait_ge(t_sb, n)
                elif n == 3:
                    pe.wait_ge(t_sb, 1)
                pe.wait_ge(xnT_sb, n // 16 + 1)
                product(bank[t_bank(n)][:, :], [w[:, n % 16, :] for w in G], xnT[n // 16]).then_inc(t_full, 1)

            def scores(s):
                g, hq, b = step(s)
                if s >= 2:
                    pe.wait_ge(exp_done, 4 * (s - 1))
                bb = g * GB + b
                pe.matmul(bank[s % 2][:, :], ones[:, :], rep(maskb[:, bb * P:(bb + 1) * P], 4),
                          start=True, stop=True)
                pe.wait_ge(t_sb, 4 * (s // 4) + 4)
                for i in range(4):
                    mm = pe.matmul(bank[s % 2][:, i * P:(i + 1) * P], tT[(s // 4) % 2][i][:, b * P:(b + 1) * P],
                                   cnT[:, bb * P:(bb + 1) * P], start=False, stop=True, skip_group_check=True)
                mm.then_inc(s_full, 1)

            def turn_probs(s):
                pe.wait_ge(pn_ready, s + 1)
                if s:
                    pe.wait_ge(pT_sb, s)
                for i in range(4):
                    mm = pe.transpose(bank[3][:, i * P:(i + 1) * P], pr[s % 3][:, i, :], ident[:, :])
                mm.then_inc(pT_full, 1)

            def gather_context(s):
                g, hq, b = step(s)
                pe.wait_ge(pT_sb, s + 1)
                if s:
                    pe.wait_ge(u_sb, s)
                product(bank[4][:, :], [c[:, g * GB + b, :] for c in cns], pT[s % 2]).then_inc(u_full, 1)

            def project(s):
                g, hq, b = step(s)
                pe.wait_ge(u_sb, s + 1)
                for i in range(4):
                    mm = pe.matmul(bank[6 + g][:, b * P:(b + 1) * P], uT[s % 2][:, i * P:(i + 1) * P],
                                   Wvo[:, 4 * hq + i, :], start=(s % 16 == 0 and i == 0), stop=False,
                                   skip_group_check=True)
                mm.then_inc(out_done, 1)

            def turn_null(g):
                misc(f"p0_{g}")
                pe.wait_ge(rr_ready, 16 * g + 16)
                for b in range(GB):
                    mm = pe.transpose(bank[5][0:HEADS, b * P:(b + 1) * P], p0n[:, g * GB + b, :], ident[:, :])
                mm.then_inc(misc_full, 1)

            def add_null(g):
                pe.wait_ge(misc_read, MISC.index(f"p0_{g}") + 1)
                for b in range(GB):
                    mm = pe.matmul(bank[6 + g][:, b * P:(b + 1) * P], p0T[:, b * P:(b + 1) * P], nw[:, :],
                                   start=False, stop=True, skip_group_check=True)
                mm.then_inc(o_full, 1)

            def moe_rows(g):
                misc(f"x3_{g}")
                pe.wait_ge(xh_ready, LNX + g + 1)
                for b in range(GB):
                    mm = pe.transpose(bank[5][:, b * P:(b + 1) * P], xh[g][:, b, :], ident[:, :])
                mm.then_inc(misc_full, 1)

            def moe_logits(g):
                misc(f"lg_{g}")
                pe.wait_ge(x3T_sb, g + 1)
                for b in range(GB):
                    mm = product(bank[5][:, b * EXPERTS:(b + 1) * EXPERTS],
                                 [t[:, b * P:(b + 1) * P] for t in x3T[g]], [w[:, :] for w in gws])
                mm.then_inc(misc_full, 1)

            def moe_weights(g):
                misc(f"cT_{g}")
                pe.wait_ge(comb_ready, g + 1)
                for b in range(GB):
                    mm = pe.transpose(bank[5][0:EXPERTS, b * P:(b + 1) * P], comb[g][:, b, :], ident[:, :])
                mm.then_inc(misc_full, 1)

            def moe_up(g, n):
                m, c = 9 * g + n, (n + 8) % 9
                if m >= 2:
                    pe.wait_ge(silu_done, m - 1)
                product(bank[m % 2][:, :], [w[:, c, :] for w in we1s], x3T[g]).then_inc(h1_full, 1)
                if m >= 2:
                    pe.wait_ge(su_done, m - 1)
                product(bank[2 + m % 2][:, :], [w[:, c, :] for w in we3s], x3T[g]).then_inc(h3_full, 1)

            def moe_spread_weights(g, n):
                if n:
                    k = 8 * g + n - 1
                    pe.wait_ge(c_ready, g + 1)
                    if k:
                        pe.wait_ge(hc_done, k)
                    pe.matmul(bank[4][:, :], selr[:, (n - 1) * P:n * P], cTs[g][:, :], start=True,
                              stop=True).then_inc(cb_full, 1)

            def moe_down(g, n):
                if n:
                    pe.wait_ge(hc_done, 8 * g + n)
                    src = hc[n % 2]
                else:
                    pe.wait_ge(su_done, 9 * g + 1)
                    src = su[(9 * g) % 2]
                for b in range(GB):
                    mm = pe.matmul(bank[6 + g][:, b * P:(b + 1) * P], src[:, b * P:(b + 1) * P],
                                   we2[:, (n + 8) % 9, :], start=(n == 0 and b == 0), stop=False,
                                   skip_group_check=True)
                mm.then_inc(dn1_done, 1)

            def moe_bias(g):
                for b in range(GB):
                    mm = pe.matmul(bank[6 + g][:, b * P:(b + 1) * P], cTf[g][:, b * P:(b + 1) * P], be2[:, :],
                                   start=False, stop=True, skip_group_check=True)
                mm.then_inc(y_full, 1)

            pe.wait_ge(h_sb, 24)
            pe.wait_ge(cnT_sb, NG)
            for n in range(4):
                fold_query(n)
                if n == 1:
                    null_scores(0)
            turn_null_scores(0)
            pe.wait_ge(prep, 10)
            pe.wait_ge(cn_lo, NG)
            for k in range(STEPS + 4):
                if k < STEPS:
                    scores(k)
                if k + 4 < STEPS:
                    if k == 7:
                        attention_rows(1)
                    fold_query(k + 4)
                if k == 9:
                    null_scores(1)
                if k == 10:
                    turn_null_scores(1)
                if k == 32:
                    pe.wait_ge(ld["moe"], 48)
                    pe.wait_ge(we_lo, 6)
                    pe.wait_ge(exp_done, 4 * (STEPS - 1))
                    pe.wait_ge(t_sb, STEPS)
                    moe_up(0, 0)
                if k == 34:
                    pe.wait_ge(exp_done, 4 * STEPS)
                    pe.wait_ge(pT_sb, STEPS)
                    moe_up(0, 1)
                if 2 <= k < STEPS + 2:
                    turn_probs(k - 2)
                if 3 <= k < STEPS + 3:
                    gather_context(k - 3)
                if k in (17, 33):
                    turn_null((k - 17) // 16)
                if k == 20:
                    pe.wait_ge(acc_full, 2)
                if k >= 4:
                    project(k - 4)
                if k in (19, 35):
                    add_null((k - 19) // 16)
                if k == 25:
                    moe_rows(0)
                if k == 27:
                    moe_logits(0)
                if k == 31:
                    moe_weights(0)
            for g in range(NG):
                pe.wait_ge(o_read, g + 1)
                for n in range(10):
                    if n < 9:
                        if (g, n) > (0, 1):
                            moe_up(g, n)
                        if n:
                            moe_spread_weights(g, n)
                    if n >= 1:
                        moe_down(g, n - 1)
                    if g == 0 and n == 3:
                        moe_rows(1)
                    if g == 0 and n == 4:
                        moe_logits(1)
                    if g == 0 and n == 8:
                        moe_weights(1)
                moe_bias(g)

        @block.scalar
        def _(act):
            def copy(dst, src, **kw):
                return act.activation(dst, src, ACT.Copy, **kw)

            act.wait_ge(ld["cols"], 16)
            for g in range(NG):
                act.wait_ge(kr_full, g + 1)
                act.activation(krT[g][:, :], bank[g][:, :], ACT.Identity, bias=col(C_BRED)).then_inc(kr_sb, 1)
            act.wait_ge(ld["rows"], 16)
            act.activation(tg[:, :], rows[:, R_G:R_G + 4], ACT.Tanh).then_inc(tanh_done, 1)
            for g in range(NG):
                act.wait_ge(xT_full, g + 1)
                copy(xT[g][:, :], bank[2 + g][:, :]).then_inc(xT_sb, 1)
            act.wait_ge(consts, NCONST)

            def window_exp(g):
                act.wait_ge(sm_ready, g + 1)
                for b in range(GB):
                    act.activation(p0[g][:, b, :], sm[g][:, b, :], ACT.Exp, bias=nm0[:, g, b:b + 1],
                                   accum_out=rs0[:, g, b:b + 1]).then_inc(p0_ready, 1)

            def window_probs(g):
                act.wait_ge(pT0_full, g + 1)
                copy(pT0[g][:, :], bank[g][:, :]).then_inc(pT0_sb, 1)

            def folded(n):
                act.wait_ge(gw_full, n + 1)
                dst = slice(4 * (n % 4), 4 * (n % 4) + 4)
                if n >= 4:
                    copy(Wvo[:, dst, :], b4(6 + n % 2)).then_inc(gw_sb, 1)
                    return
                if n >= 2:
                    act.wait_ge(gw_lo, n - 1)
                scale = HEADS ** -0.5
                copy(raw[n % 2], bank[6 + n % 2][:, :], scale=scale)
                copy(G[0][:, dst, :], b4(6 + n % 2), scale=scale).then_inc(gw_sb, 1)

            folded(0)
            window_exp(0)
            folded(1)
            window_exp(1)
            folded(2)
            window_probs(0)
            folded(3)
            window_probs(1)
            for n in range(4, 8):
                folded(n)
            act.wait_ge(gw_full, 9)
            copy(wnf[:, :], bank[6][:, 0:HEADS], scale=HEADS ** -0.5)
            copy(wnull[0][:, :], bank[6][:, 0:HEADS], scale=HEADS ** -0.5)
            copy(nw[:, :], bank[6][0:HEADS, P:2 * P]).then_inc(gw_sb, 1)
            act.wait_ge(ld["w1"], 16)
            for k in (2, 0, 1):
                copy(w1s[0][:, 4 * k:4 * k + 4, :], w1[:, 4 * k:4 * k + 4, :]).then_inc(w1_hi, 1)

            def rows_out(g):
                for k in range(3):
                    act.wait_ge(fT_full, 3 * g + k + 1)
                    copy(fT[g][k][0], bank[k][:, :]).then_inc(fT_hi, 1)

            def hidden(u):
                act.wait_ge(up_full, u + 1)
                if u >= 4:
                    v = u - 4
                    if v % 12 == 11:
                        act.wait_ge(acc_full, v // 12 + 1)
                    else:
                        act.wait_ge(dn_done, 11 * (v // 12) + v % 12 + 1)
                act.activation(hT[u % 4], bank[3 + u % 3][:, :], ACT.Relu,
                               bias=col(C_B1 + (u % 12 + 8) % 12)).then_inc(h_sb, 1)

            def attention_rows(g):
                act.wait_ge(x2T_full, g + 1)
                copied = (xn_raw, 1) if g == 0 else (misc_read, MISC.index("x2_1") + 1)
                act.activation(raw[g], bank[2 + 3 * g][:, :], ACT.Identity, bias=col(C_LN1B),
                               scale=col(C_LN1S)).then_inc(copied[0], 1)
                act.wait_ge(*copied)
                copy(xnT[g][0], raw[g]).then_inc(xn_hi, 1)

            rows_out(0)
            for g in range(NG):
                for j in range(12):
                    hidden(12 * g + j)
                    if g == 0 and j == 7:
                        rows_out(1)
                    if g == 1 and j == 9:
                        attention_rows(0)
                    if g == 1 and j in (1, 4):
                        c = j // 4
                        act.wait_ge(cnT_full, c + 1)
                        copy(cnT[:, c * N:(c + 1) * N], bank[c][:, :]).then_inc(cnT_sb, 1)
                        copy(cns[0][:, GRP[c], :], ctx[:, GRP[c], :]).then_inc(cn_hi, 1)

            def t_copy(n):
                act.wait_ge(t_full, n + 1)
                if n >= 8:
                    act.wait_ge(s_full, 4 * (n // 4 - 1))
                copy(tT[(n // 4) % 2][n % 4], bank[t_bank(n)][:, :]).then_inc(t_sb, 1)

            def null_copies(g):
                act.wait_ge(misc_full, misc_uses(f"q0_{g}"))
                copy(q0T[:, :], bank[5][0:HEADS, :]).then_inc(misc_read, 1)

            def null_score_copy(g):
                act.wait_ge(misc_full, misc_uses(f"s0_{g}"))
                copy(ns0[:, GRP[g], :], bank[5][:, 0:GB * HEADS].rearrange("p (b h) -> p b h", b=GB),
                     scale=-1.0).then_inc(misc_read, 1)

            def probs_high(s):
                act.wait_ge(pT_full, s + 1)
                if s >= 2:
                    act.wait_ge(u_full, s - 1)
                copy(pT[s % 2][0], bank[3][:, :]).then_inc(pT_hi, 1)

            def silu(g, n):
                m = 9 * g + n
                act.wait_ge(h1_full, m + 1)
                if m >= 2:
                    act.wait_ge(su_done, m - 1)
                act.activation(sa[m % 2], bank[m % 2][:, :], ACT.Silu,
                               bias=col(C_BE1 + (n + 8) % 9)).then_inc(silu_done, 1)

            def high_part(g):
                act.wait_ge(misc_read, MISC.index(f"cT_{g}") + 1)
                copy(cTs[g][0:EXPERTS, :], cTf[g][:, :]).then_inc(chi_ready, 1)

            act.wait_ge(prep, 10)
            for n in range(4):
                t_copy(n)
                if n == 1:
                    null_copies(0)
            null_score_copy(0)
            for k in range(STEPS + 3):
                if k + 4 < STEPS:
                    t_copy(k + 4)
                    if k == 7:
                        attention_rows(1)
                if 2 <= k < STEPS + 2:
                    probs_high(k - 2)
                if k == 9:
                    null_copies(1)
                if k == 10:
                    null_score_copy(1)
                if 8 <= k < 14:
                    m, third = divmod(k - 8, 3)
                    cut = slice(3 * third, 3 * third + 3)
                    act.wait_ge(ld["moe"], 48)
                    copy((we1s, we3s)[m][0][:, cut, :], (we1, we3)[m][:, cut, :]).then_inc(we_hi, 1)
                if k < STEPS:
                    act.wait_ge(nm_ready, k + 1)
                    if k >= 3:
                        act.wait_ge(pT_full, k - 2)
                    if k >= 2:
                        act.wait_ge(rr_ready, k - 1)
                    act.activation(pz[:, k % 2, :], d0[:, k % 2, :], ACT.Exp)
                    for i in range(4):
                        act.activation(pr[k % 3][:, i, :], bank[k % 2][:, i * P:(i + 1) * P], ACT.Exp,
                                       bias=nm[:, k % 2, i:i + 1],
                                       accum_out=rs[:, k % 2, i:i + 1]).then_inc(exp_done, 1)
                if k == 25:
                    act.wait_ge(misc_full, misc_uses("x3_0"))
                    copy(x3T[0][0], bank[5][:, :]).then_inc(x3_hi, 1)
                if k == 27:
                    act.wait_ge(sh_ready, 1)
                    act.activation(ex[:, :, :], sh[:, :, :], ACT.Exp).then_inc(ex_ready, 1)
                if k == 32:
                    high_part(0)
            silu(0, 0)

            for g in range(NG):
                for n in range(9):
                    if (g, n) != (0, 0):
                        silu(g, n)
                    if g == 0 and n == 3:
                        act.wait_ge(misc_full, misc_uses("x3_1"))
                        copy(x3T[1][0], bank[5][:, :]).then_inc(x3_hi, 1)
                    if g == 0 and n == 5:
                        act.wait_ge(sh_ready, 2)
                        act.activation(ex[:, :, :], sh[:, :, :], ACT.Exp).then_inc(ex_ready, 1)
                    if g == 0 and n == 8:
                        high_part(1)

        @block.vector
        def _(dve):
            links = 0

            def link(ins):
                nonlocal links
                links += 1
                ins.then_inc(dch, 1)
                dve.wait_ge(dch, links)

            norms = [0, 0]

            def spread(src, scale, eps):
                for b in range(GB):
                    last = dve.bn_stats(stats[:, b, :], src(b))
                link(last)
                for b in range(GB):
                    last = dve.bn_aggr(mv[:, norms[0] % 2, b, :], stats[:, b, :])
                link(last)
                dve.tensor_scalar(ve[:, norms[0] % 2, :], mv[:, norms[0] % 2, :, 1], scale, eps, op0=ALU.mult,
                                  op1=ALU.add).then_inc(var_ready, 1)
                norms[0] += 1

            def scaled(src, dst, event):
                k = norms[1] % 2
                norms[1] += 1
                dve.wait_ge(rstd_ready, norms[1])
                for b in range(GB):
                    last = dve.tensor_scalar(dst(b), src(b), mv[:, k, b, 0:1], rstd[:, k, b:b + 1],
                                             op0=ALU.subtract, op1=ALU.mult)
                last.then_inc(*event)

            def norm(src, dst, event, scale, eps):
                spread(src, scale, eps)
                scaled(src, dst, event)

            def rows_of(g):
                return lambda b: xr[:, g * GB + b, :]

            dve.memset(shared[:, 0:4 * N], 0.0).then_inc(blk_clear, 1)
            for g in range(NG):
                dve.wait_ge(ld[f"x{g}"], 16)
                spread(rows_of(g), 1.0, EPS0)
            for g in range(NG):
                scaled(rows_of(g), lambda b: xh[g][:, b, :], (xh_ready, 1))

            dve.wait_ge(consts, NCONST)
            dve.wait_ge(ld["rows"], 16)
            dve.wait_ge(tanh_done, 1)

            for g in range(NG):
                dve.wait_ge(s0_full, g + 1)
                link(dve.tensor_tensor(sm[g][:, :, :], b4(4 + g), rep(band[:, :], GB), op=ALU.add))
                dve.tensor_reduce(nm0[:, g, :], sm[g][:, :, :], axis=AX.X, op=ALU.max,
                                  negate=True).then_inc(sm_ready, 1)
            dve.tensor_tensor(gwd[:, :], rows[:, R_GW:R_GW + P], rows[:, R_GW + P:R_GW + 2 * P],
                              op=ALU.subtract).then_inc(prep, 1)
            link(dve.tensor_tensor(b2bc[:, :], rows[:, R_B2:R_B2 + P], rows[:, R_B2 + P:R_B2 + 2 * P], op=ALU.add))
            dve.tensor_tensor(b2bc[:, :], b2bc[:, :], rows[:, R_B2 + 2 * P:R_B2 + 3 * P],
                              op=ALU.add).then_inc(prep, 1)
            dve.tensor_scalar(st[:, :], rows[:, R_LNOS:R_LNOS + P], tg[:, 1:2], None,
                              op0=ALU.mult).then_inc(prep, 1)
            dve.tensor_scalar(bt[:, :], rows[:, R_LNOB:R_LNOB + P], tg[:, 1:2], None,
                              op0=ALU.mult).then_inc(prep, 1)
            for r in range(2):
                half = slice(64 * r, 64 * r + 64)
                dve.tensor_copy(nvblk[half, :, :].rearrange("p c n -> p (c n)")[:, r:P:18],
                                cols[half, C_NV:C_NV + 1].to_broadcast([64, 8])).then_inc(prep, 1)
                dve.tensor_copy(nkblk[half, r:r + 1], cols[half, C_NK:C_NK + 1]).then_inc(prep, 1)
            for g in range(NG):
                dve.memset(cTs[g][:, :].bitcast(fp32), 0.0)

            def window_out(g):
                dve.wait_ge(o0_full, g + 1)
                dve.wait_ge(p0_ready, GB * (g + 1))
                link(dve.reciprocal(rr0[:, g, :], rs0[:, g, :]))
                link(dve.tensor_scalar(rr0[:, g, :], rr0[:, g, :], tg[:, 0:1], None, op0=ALU.mult))
                for b in range(GB):
                    last = dve.scalar_tensor_tensor(xr[:, g * GB + b, :], b4(2 + g)[:, b, :], rr0[:, g, b:b + 1],
                                                    xr[:, g * GB + b, :], op0=ALU.mult, op1=ALU.add)
                last.then_inc(x1_ready, 1)
                dve.wait_ge(x1_ready, g + 1)

            def mlp_input(g):
                norm(rows_of(g), lambda b: xh[g][:, b, :], (xh_ready, 1), 1.0, EPS0)
                dve.wait_ge(xh_ready, LN1 + g + 1)
                link(dve.tensor_tensor(gtmp[:, :, :], xh[g][:, :, :], rep(gwd[:, :], GB), op=ALU.mult))
                link(dve.tensor_reduce(gd[:, :], gtmp[:, :, :], axis=AX.X, op=ALU.add))
                link(dve.tensor_scalar(m0[:, :], gd[:, :], 0.0, None, op0=ALU.is_ge))
                link(dve.tensor_tensor(xm0[g][:, :, :], xh[g][:, :, :], bc(m0[:, :], P), op=ALU.mult))
                dve.tensor_tensor(xm1[g][:, :, :], xh[g][:, :, :], xm0[g][:, :, :],
                                  op=ALU.subtract).then_inc(fm_ready, 1)

            def rows_low(g):
                for k in range(3):
                    dve.wait_ge(fT_hi, 3 * g + k + 1)
                    dve.tensor_tensor(fT[g][k][1], bank[k][:, :], fT[g][k][0].bitcast(fp32),
                                      op=ALU.subtract).then_inc(fT_sb, 1)

            window_out(0)
            dve.wait_ge(prep, 8)
            dve.wait_ge(gw_lo, 4)
            mlp_input(0)
            window_out(1)
            dve.wait_ge(ld["small"], 48)
            dve.tensor_scalar(maskb[:, :], mask8[:, :], -1.0, -MASKED, op0=ALU.add,
                              op1=ALU.mult).then_inc(prep, 1)
            link(dve.tensor_copy(gws[0][:, :], gw[:, :]))
            dve.tensor_tensor(gws[1][:, :], gw[:, :], gws[0][:, :].bitcast(fp32), op=ALU.subtract).then_inc(prep, 1)
            rows_low(0)
            mlp_input(1)
            for g in range(NG):
                norm(lambda b: ctx[:, g * GB + b, :], lambda b: ctx[:, g * GB + b, :], (cn_raw, 1), 1.0, EPS1)
                if g == 0:
                    rows_low(1)

            def mlp_output(g):
                dve.wait_ge(acc_full, g + 1)
                link(dve.tensor_tensor(acc[:, :, :], b4(6 + g), rep(b2bc[:, :], GB), op=ALU.add))
                dve.scalar_tensor_tensor(xr[:, GRP[g], :], acc[:, :, :], tg[:, 2:3], xr[:, GRP[g], :],
                                         op0=ALU.mult, op1=ALU.add).then_inc(x2_ready, 1)
                dve.wait_ge(x2_ready, g + 1)
                norm(rows_of(g), lambda b: xh[g][:, b, :], (xh_ready, 1), 1.0 + EPS1, EPS0 * EPS1)

            def attention_rows(g):
                dve.wait_ge(xn_hi, g + 1)
                dve.tensor_tensor(xnT[g][1], raw[g], xnT[g][0].bitcast(fp32), op=ALU.subtract).then_inc(xnT_sb, 1)

            mlp_output(0)
            attention_rows(0)
            mlp_output(1)

            def shift(s):
                g, hq, b = step(s)
                null = ns0[:, g * GB + b, 4 * hq:4 * hq + 4]
                dve.wait_ge(s_full, s + 1)
                if s == 0:
                    dve.wait_ge(misc_read, MISC.index("s0_0") + 1)
                if s == 16:
                    dve.wait_ge(misc_read, MISC.index("s0_1") + 1)
                if s >= 2:
                    dve.wait_ge(exp_done, 4 * (s - 1))
                link(dve.tensor_reduce(nmx[:, s % 2, :], b4(s % 2), axis=AX.X, op=ALU.max, negate=True))
                link(dve.tensor_tensor(nm[:, s % 2, :], nmx[:, s % 2, :], null, op=ALU.min))
                dve.tensor_tensor(d0[:, s % 2, :], nm[:, s % 2, :], null, op=ALU.subtract).then_inc(nm_ready, 1)

            def sums(s):
                g, hq, b = step(s)
                dve.wait_ge(exp_done, 4 * (s + 1))
                if s >= 2:
                    dve.wait_ge(pn_ready, s - 1)
                link(dve.tensor_tensor(rt[:, :], rs[:, s % 2, :], pz[:, s % 2, :], op=ALU.add))
                link(dve.reciprocal(rr[:, s % 2, :], rt[:, :]))
                dve.tensor_tensor(p0n[:, g * GB + b, 4 * hq:4 * hq + 4], pz[:, s % 2, :], rr[:, s % 2, :],
                                  op=ALU.mult).then_inc(rr_ready, 1)

            def probs_copy(s):
                dve.wait_ge(pT_hi, s + 1)
                dve.tensor_tensor(pT[s % 2][1], bank[3][:, :], pT[s % 2][0].bitcast(fp32),
                                  op=ALU.subtract).then_inc(pT_sb, 1)

            def gathered_copy(s):
                dve.wait_ge(u_full, s + 1)
                if s >= 2:
                    dve.wait_ge(out_done, s - 1)
                dve.tensor_copy(uT[s % 2], bank[4][:, :]).then_inc(u_sb, 1)

            def null_probs(g):
                dve.wait_ge(misc_full, misc_uses(f"p0_{g}"))
                dve.tensor_copy(p0T, bank[5][0:HEADS, :]).then_inc(misc_read, 1)

            def output_of(g):
                return lambda b: b4(6 + g)[:, b, :]

            def output_spread(g):
                dve.wait_ge(o_full, g + 1)
                spread(output_of(g), 1.0, EPS1)

            def output_scaled(g):
                scaled(output_of(g), lambda b: z[g][:, b, :], (o_read, 1))

            def moe_spread(g):
                dve.wait_ge(x3_ready, g + 1)
                spread(rows_of(g), 1.0, EPS0)

            def moe_scaled(g):
                scaled(rows_of(g), lambda b: xh[g][:, b, :], (xh_ready, 1))

            def two_largest(values, replaced):
                for b in range(GB):
                    last = dve.max(top8[:, b, :], values[:, b, :])
                link(last)
                link(dve.tensor_copy(want[:, :, 0:2], top8[:, :, 0:2]))
                for b in range(GB):
                    last = dve.match_replace(replaced[:, b, :], want[:, b, :], values[:, b, :], TAKEN)
                link(last)

            def gate_start(g):
                dve.wait_ge(misc_full, misc_uses(f"lg_{g}"))
                lg = bank[5][:, 0:GB * EXPERTS].rearrange("p (b e) -> p b e", b=GB)
                link(dve.tensor_reduce(g4[:, :], lg, axis=AX.X, op=ALU.max))
                dve.tensor_tensor(sh[:, :, :], lg, bc(g4[:, :], EXPERTS), op=ALU.subtract).then_inc(sh_ready, 1)
                dve.wait_ge(sh_ready, g + 1)
                dve.sem_inc(misc_read, 1)

            def gate_probs(g):
                dve.wait_ge(ex_ready, g + 1)
                link(dve.tensor_reduce(g4[:, :], ex[:, :, :], axis=AX.X, op=ALU.add))
                link(dve.reciprocal(g4r[:, :], g4[:, :]))
                link(dve.tensor_tensor(pb[:, :, :], ex[:, :, :], bc(g4r[:, :], EXPERTS), op=ALU.mult))
                link(dve.tensor_tensor(sc[:, :, :], pb[:, :, :], rep(rows[:, R_GB:R_GB + EXPERTS], GB), op=ALU.add))
                pairs = sc[:, :, :].rearrange("p b (g j k) -> p (b g) j k", g=4, j=2)
                dve.tensor_tensor(pmx[:, :, :], pairs[:, :, :, 0], pairs[:, :, :, 1], op=ALU.max)
                link(dve.tensor_tensor(pmn[:, :, :], pairs[:, :, :, 0], pairs[:, :, :, 1], op=ALU.min))
                dve.tensor_tensor(t1[:, :], pmx[:, :, 0], pmx[:, :, 1], op=ALU.max)
                dve.tensor_tensor(t2[:, :], pmx[:, :, 0], pmx[:, :, 1], op=ALU.min)
                link(dve.tensor_tensor(t3[:, :], pmn[:, :, 0], pmn[:, :, 1], op=ALU.max))
                link(dve.tensor_tensor(t2[:, :], t2[:, :], t3[:, :], op=ALU.max))
                link(dve.tensor_tensor(gsp[:, :, 0:4], t1[:, :].rearrange("p (b g) -> p b g", b=GB),
                                       t2[:, :].rearrange("p (b g) -> p b g", b=GB), op=ALU.add))

            def gate_groups(g):
                two_largest(gsp, gsr)
                link(dve.tensor_scalar(keep[:, :, :], gsr[:, :, 0:4], TAKEN, None, op0=ALU.is_equal))
                link(dve.tensor_scalar(pen[:, :, :], keep[:, :, :], -1.0, -LOW, op0=ALU.add, op1=ALU.mult))
                flat = lambda t: t.rearrange("p b (g k) -> p (b g) k", g=4)
                kept = bc(keep[:, :, :].rearrange("p b g -> p (b g)"), 4)
                link(dve.tensor_tensor(flat(skp[:, :, :]), flat(sc[:, :, :]), kept, op=ALU.mult))
                for b in range(GB):
                    last = dve.tensor_tensor(msp[:, b, 0:EXPERTS].rearrange("p (g k) -> p g k", g=4),
                                             skp[:, b, :].rearrange("p (g k) -> p g k", g=4),
                                             bc(pen[:, b, :], 4), op=ALU.add)
                link(last)

            def gate_experts(g):
                two_largest(msp, msr)
                dve.scalar_tensor_tensor(comb[g][:, :, :], msr[:, :, 0:EXPERTS], TAKEN, pb[:, :, :],
                                         op0=ALU.is_equal, op1=ALU.mult).then_inc(comb_ready, 1)

            def low_part(g):
                dve.wait_ge(misc_full, misc_uses(f"cT_{g}"))
                dve.tensor_copy(cTf[g][:, :], bank[5][0:EXPERTS, :]).then_inc(misc_read, 1)
                dve.wait_ge(chi_ready, g + 1)
                dve.tensor_tensor(cTs[g][32:32 + EXPERTS, :], cTf[g][:, :],
                                  cTs[g][0:EXPERTS, :].bitcast(fp32), op=ALU.subtract).then_inc(c_ready, 1)

            def gated(g, n):
                m = 9 * g + n
                dve.wait_ge(silu_done, m + 1)
                dve.wait_ge(h3_full, m + 1)
                if n == 2 and g == 1:
                    dve.wait_ge(dn1_done, 10)
                if n == 2 and g == 0:
                    dve.wait_ge(dn1_done, 1)
                dve.scalar_tensor_tensor(su[m % 2], bank[2 + m % 2][:, :], col(C_BE3 + (n + 8) % 9),
                                         sa[m % 2], op0=ALU.add, op1=ALU.mult).then_inc(su_done, 1)
                if n:
                    k = 8 * g + n - 1
                    dve.wait_ge(cb_full, k + 1)
                    dve.wait_ge(su_done, m + 1)
                    if n > 2:
                        dve.wait_ge(dn1_done, 9 * g + n - 1)
                    elif g:
                        dve.wait_ge(dn1_done, 9)
                    dve.tensor_tensor(hc[n % 2], su[m % 2], bank[4][:, :],
                                      op=ALU.mult).then_inc(hc_done, 1)

            def moe_output(g):
                dve.wait_ge(y_full, g + 1)
                link(dve.tensor_tensor(acc[:, :, :], b4(6 + g), rep(rows[:, R_BS2:R_BS2 + P], GB), op=ALU.add))
                dve.scalar_tensor_tensor(xr[:, GRP[g], :], acc[:, :, :], tg[:, 3:4], xr[:, GRP[g], :],
                                         op0=ALU.mult, op1=ALU.add).then_inc(x4_ready, 1)

            def moe_rows(g):
                dve.wait_ge(x3_hi, g + 1)
                link(dve.tensor_tensor(x3T[g][1], bank[5][:, :], x3T[g][0].bitcast(fp32), op=ALU.subtract))
                dve.sem_inc(misc_read, 1)
                dve.sem_inc(x3T_sb, 1)

            for k in range(STEPS + 4):
                if 1 <= k <= STEPS:
                    sums(k - 1)
                if k < STEPS:
                    shift(k)
                if 2 <= k < STEPS + 2:
                    probs_copy(k - 2)
                if k in (17, 33):
                    null_probs((k - 17) // 16)
                if 3 <= k < STEPS + 3:
                    gathered_copy(k - 3)
                if k == 20:
                    output_spread(0)
                if k == 21:
                    output_scaled(0)
                if k == 23:
                    moe_spread(0)
                if k == 24:
                    moe_scaled(0)
                if k == 8:
                    attention_rows(1)
                if k == 26:
                    moe_rows(0)
                if k == 27:
                    gate_start(0)
                if k == 28:
                    gate_probs(0)
                if k == 29:
                    gate_groups(0)
                if k == 30:
                    gate_experts(0)
                if k == 32:
                    low_part(0)
                if k == 35:
                    gated(0, 0)
            output_spread(1)
            output_scaled(1)
            for n in range(1, 9):
                gated(0, n)
                if n == 1:
                    moe_spread(1)
                if n == 2:
                    moe_scaled(1)
                if n == 3:
                    moe_rows(1)
                if n == 4:
                    gate_start(1)
                if n == 5:
                    gate_probs(1)
                if n == 6:
                    gate_groups(1)
                if n == 7:
                    gate_experts(1)
            low_part(1)
            moe_output(0)
            for n in range(9):
                gated(1, n)
            moe_output(1)


def kernel(x, ctx_1024, mask_BxS2_bf1, g_xattn, g_ffn, L0_xattn_W_reduce, L0_xattn_b_reduce,
           L0_ffn_gate_w, L0_ffn_w1, L0_ffn_b1, L0_ffn_w2, L0_ffn_b2, L0_ffn_sw1, L0_ffn_sb1,
           L0_ffn_sw2, L0_ffn_sb2, L1_xattn_ln1_s, L1_xattn_ln1_b, L1_xattn_lnc_s, L1_xattn_lnc_b,
           L1_xattn_Wq, L1_xattn_Wkv, L1_xattn_null_kv, L1_xattn_Wo, L1_xattn_lno_s,
           L1_xattn_lno_b, L1_ffn_gate_w, L1_ffn_gate_b, L1_ffn_We1, L1_ffn_be1, L1_ffn_We2,
           L1_ffn_be2, L1_ffn_We3, L1_ffn_be3, L1_ffn_ws1, L1_ffn_bs1, L1_ffn_ws2, L1_ffn_bs2,
           L1_ffn_ws3, L1_ffn_bs3):
    import numpy as np
    import concourse.bacc as bacc
    from concourse.bass_utils import run_bass_kernel_spmd

    A = np.asarray
    x, ctx = A(x), A(ctx_1024)
    inner = HEADS * 64

    def by_partition(w):
        w = A(w)
        return w.reshape(-1, P, w.shape[-1]).transpose(1, 0, 2)

    def chunks(w):
        return A(w).reshape(P, -1, P)

    experts = lambda w: A(w).transpose(1, 0, 2).reshape(P, -1)
    wkv = A(L1_xattn_Wkv)
    cols = np.concatenate([
        A(L0_xattn_b_reduce)[None], A(L0_ffn_b1).reshape(-1, P), A(L0_ffn_sb1).reshape(-1, P),
        A(L1_xattn_ln1_s)[None], A(L1_xattn_ln1_b)[None],
        A(L1_ffn_be1).reshape(-1, P), A(L1_ffn_bs1)[None],
        A(L1_ffn_be3).reshape(-1, P), A(L1_ffn_bs3)[None],
        A(L1_xattn_null_kv)[[0, 0]].reshape(1, P), A(L1_xattn_null_kv)[[1, 1]].reshape(1, P)]).T
    rows = np.concatenate([A(a).reshape(-1) for a in (
        L0_ffn_gate_w, L0_ffn_b2, L0_ffn_sb2, L1_xattn_lnc_s, L1_xattn_lnc_b, L1_xattn_lno_s,
        L1_xattn_lno_b, L1_ffn_bs2, L1_ffn_gate_b, g_xattn, g_ffn)])
    w1 = np.concatenate([A(L0_ffn_w1).transpose(1, 0, 2).reshape(P, -1), A(L0_ffn_sw1)], 1)
    w2 = np.concatenate([A(L0_ffn_w2).reshape(-1, P), A(L0_ffn_sw2)])
    data = {
        "in_x": x.transpose(1, 0, 2),
        "in_ctx": ctx.transpose(1, 0, 2),
        "in_ctxT": ctx.reshape(-1, P).T,
        "in_wredT": A(L0_xattn_W_reduce).T,
        "in_cols": cols,
        "in_rows": rows,
        "in_w1": chunks(w1),
        "in_w2": by_partition(w2),
        "in_wqT": by_partition(A(L1_xattn_Wq).T),
        "in_wkT": by_partition(wkv[:, :inner].T),
        "in_wvT": by_partition(wkv[:, inner:].T),
        "in_wo": by_partition(L1_xattn_Wo),
        "in_gw": A(L1_ffn_gate_w).T,
        "in_we1": chunks(np.concatenate([experts(L1_ffn_We1), A(L1_ffn_ws1)], 1)),
        "in_we3": chunks(np.concatenate([experts(L1_ffn_We3), A(L1_ffn_ws3)], 1)),
        "in_we2": by_partition(np.concatenate([A(L1_ffn_We2).reshape(-1, P), A(L1_ffn_ws2)])),
        "in_be2": A(L1_ffn_be2),
        "in_mask": A(mask_BxS2_bf1).reshape(1, -1).view(np.uint8),
    }
    data = {k: np.ascontiguousarray(v) for k, v in data.items()}
    nc = bacc.Bacc("TRN2", target_bir_lowering=False, num_devices=1)
    args = [nc.dram_tensor(k, v.shape, mybir.dt.from_np(v.dtype), kind="ExternalInput").ap()
            for k, v in data.items()]
    out = nc.dram_tensor("out_x", (P, B, P), mybir.dt.float32, kind="ExternalOutput").ap()
    gated_layers(nc, *args, out)
    r = run_bass_kernel_spmd(nc, [data], core_ids=[0])
    return r.results[0]["out_x"].transpose(1, 0, 2)
```

```python
import concourse.bass as bass
from concourse import mybir
from contextlib import ExitStack

P = 128
B = 8
GB = 4
NG = B // GB
N = GB * P
HEADS = 16
PAIRS = HEADS // 2
WINDOW = 20
FC = 4
EXPERTS = 16
EC = 8
STEPS = NG * PAIRS * GB // 2
LAG = 3
NEG_BIG = -100000000.0
MASKED = -1e30
PAD = -2e38
LOW = -1e38
TAKEN = -3e38
EPS0, EPS1 = 1e-5, 1e-6

C_BRED, C_B1, C_LN1S, C_LN1B, C_BE1, C_BE3, C_NK, C_NV, C_B2, C_BS2, NCOLS = (
    0, 1, 13, 14, 15, 24, 33, 34, 35, 38, 39)
R_GW, R_LNCS, R_LNCB, R_LNOS, R_LNOB, R_GB, R_G, NROWS = 0, 256, 384, 512, 640, 768, 784, 788
DVE_LOW = [14, 15, 17]
MISC = ["q0_0", "s0_0", "x2_1", "q0_1", "s0_1", "p0_0", "x3_0", "lg_0", "p0_1", "cT_0", "x3_1", "lg_1", "cT_1"]


def gated_layers(nc, x, ctx_in, ctxT_in, wredT_in, cols_in, rows_in, w1_in, w2_in, wqT_in, wkT_in,
                 wvT_in, wo_in, gw_in, we1_in, we3_in, we2_in, be2_in, mask_in, out):
    fp32, fp32r, bf16, u8 = mybir.dt.float32, mybir.dt.float32r, mybir.dt.bfloat16, mybir.dt.uint8
    ALU = mybir.AluOpType
    ACT = mybir.ActivationFunctionType
    AX = mybir.AxisListType

    with ExitStack() as stack:
        def sb(name, shape, dt=fp32):
            return stack.enter_context(nc.sbuf_tensor(name, shape, dt))

        def both(name, shape):
            with nc.sbuf_tensor(name + "_raw", shape, fp32) as plain:
                pass
            return plain, sb(name, shape, fp32r)

        def sem(name):
            return stack.enter_context(nc.semaphore(name))

        xr = sb("xr", [P, B, P])
        ctx = sb("ctx", [P, B, P])
        ctxT = sb("ctxT", [P, B * P])
        wredT = sb("wredT", [P, P])
        cols = sb("cols", [P, NCOLS])
        rows = sb("rows", [P, NROWS])
        gw = sb("gw", [P, EXPERTS])
        be2 = sb("be2", [EXPERTS, P])
        mask8 = sb("mask8", [1, B * P], u8)
        late_raw, late = both("late", [P, 2 * (EC + 1), P])
        wqT, wvT = late_raw[:, 0:8, :], late_raw[:, 8:16, :]
        shared, shared_r = both("shared", [P, 10 * N])
        wkblk, woblk = (shared[:, k * 4 * N:(k + 1) * 4 * N].rearrange("p (c r n) -> p c r n", c=8, r=2)
                        for k in range(2))
        part = [shared[:, k * N:(k + 1) * N] for k in range(10)]
        ident = sb("ident", [P, P])
        band = sb("band", [P, P])
        mhalf = sb("mhalf", [P, GB])
        warm = sb("warm", [P, GB])
        selr = sb("selr", [64, EC * P], fp32r)
        ones = sb("ones", [1, P], bf16)
        maskb = sb("maskb", [1, B * P], bf16)
        nvblk = sb("nvblk", [P, 8, 16])
        nkblk = sb("nkblk", [P, 2])
        gwd = sb("gwd", [P, P])
        b2sum = sb("b2sum", [P, 2])
        tg = sb("tg", [P, 4])
        st = sb("st", [P, P])
        bt = sb("bt", [P, P])
        Graw, G1 = both("G1", [P, HEADS, P])
        G = [sb("G0", [P, HEADS, P], fp32r), G1]
        wnull = [sb(f"wnull{k}", [P, HEADS], fp32r) for k in range(2)]
        gws = [sb(f"gws{k}", [P, EXPERTS], fp32r) for k in range(2)]
        cns = [sb(f"cns{k}", [P, B, P], fp32r) for k in range(2)]
        ups_raw, ups = both("ups", [P, 4 * (EC + 1), P])
        w1s = [ups[:, k * 12:k * 12 + 12, :] for k in range(2)]
        we1s, we3s = ([ups[:, (2 * m + k) * (EC + 1):(2 * m + k + 1) * (EC + 1), :] for k in range(2)]
                      for m in range(2))
        we2s = [late[:, k * (EC + 1):(k + 1) * (EC + 1), :] for k in range(2)]
        w2raw, w2low = both("w2low", [P, 3 * FC, P])
        w2s = [sb("w2high", [P, 3 * FC, P], fp32r), w2low]
        Wvo_raw, Wvo1 = (t[:, 0:4 * N].rearrange("p (h n) -> p h n", h=HEADS) for t in (shared, shared_r))
        Wvo = [sb("Wvo", [P, HEADS, P], fp32r), Wvo1]
        w1raw, we1raw, we3raw = ups_raw[:, 12:24, :], ups_raw[:, 9:18, :], ups_raw[:, 27:36, :]
        we2raw = late_raw[:, EC + 1:2 * (EC + 1), :]
        turned = sb("turned", [P, 12 * N], fp32r)

        def pair(k):
            return [turned[:, (2 * k + i) * N:(2 * k + i + 1) * N] for i in range(2)]

        wnf = sb("wnf", [P, HEADS])
        nw = sb("nw", [HEADS, P])
        stats = sb("stats", [P, GB, 6])
        mv = sb("mv", [P, 2, GB, 2])
        ve = sb("ve", [P, 2, GB])
        rstd = sb("rstd", [P, 2, GB])
        xh = [sb(f"xh{g}", [P, GB, P]) for g in range(NG)]
        xm0 = [sb(f"xma{g}", [P, GB, P]) for g in range(NG)]
        xm1 = [sb(f"xmb{g}", [P, GB, P]) for g in range(NG)]
        raw = [t[:, :, :].rearrange("p b n -> p (b n)") for t in xm1]
        gd = sb("gd", [P, GB])
        m0 = sb("m0", [P, GB])
        tiles, tiles_r = both("tiles", [P, 8 * N])
        free, free_r = ([t[:, k * N:(k + 1) * N] for k in range(8)] for t in (tiles, tiles_r))
        xT, krT = free[0:2], free[2:4]
        sm, p0 = ([t.rearrange("p (b n) -> p b n", b=GB) for t in free[k:k + 2]] for k in (4, 6))
        nm0 = sb("nm0", [P, NG, GB])
        rs0 = sb("rs0", [P, NG, GB])
        rr0 = sb("rr0", [P, NG, GB])
        p0 = [sb(f"p0{g}", [P, GB, P]) for g in range(NG)]
        pT0 = [sb(f"pT0{g}", [P, N]) for g in range(NG)]
        fT = [[pair(3 * g + k) for k in range(3)] for g in range(NG)]
        hraw = free[0:2] + part[4:6]
        hT = [[free_r[2 + k], free_r[5 + k]] for k in range(3)]
        accT = sb("accT", [P, N])
        gtmp = accT[:, :].rearrange("p (b n) -> p b n", b=GB)
        cn = sb("cn", [P, B, P])
        cnT = sb("cnT", [P, B * P])
        xnT = [pair(0), pair(1)]
        q0T = sb("q0T", [HEADS, N])
        ns0 = sb("ns0", [P, B, HEADS])
        tT = free[0:4]
        uT = [free_r[4 + 2 * k:6 + 2 * k] for k in range(2)]
        nmx = sb("nmx", [P, 2, 4])
        nm = sb("nm", [P, 2, 4])
        d0 = sb("d0", [P, 2, 4])
        pr = [part[4 + k].rearrange("p (i n) -> p i n", i=4) for k in range(3)]
        rs = sb("rs", [P, 2, 4])
        pz = sb("pz", [P, 2, 4])
        rt = sb("rt", [P, 4])
        rr = sb("rr", [P, 2, 4])
        p0n = sb("p0n", [P, B, HEADS])
        p0T = part[9][0:HEADS, :]
        pT = [pair(2), pair(3)]
        z = [pT0[g][:, :].rearrange("p (b n) -> p b n", b=GB) for g in range(NG)]
        xb = xm0
        x3T = [pair(4), pair(5)]
        sh = sb("sh", [P, GB, EXPERTS])
        ex = sb("ex", [P, GB, EXPERTS])
        pb = sb("pb", [P, GB, EXPERTS])
        sc = sb("sc", [P, GB, EXPERTS])
        g4 = sb("g4", [P, GB])
        g4r = sb("g4r", [P, GB])
        pmx = sb("pmx", [P, 16, 2])
        pmn = sb("pmn", [P, 16, 2])
        t1 = sb("t1", [P, 16])
        t2 = sb("t2", [P, 16])
        t3 = sb("t3", [P, 16])
        gsp = sb("gsp", [P, GB, 12])
        gsr = sb("gsr", [P, GB, 12])
        top8 = sb("top8", [P, GB, 8])
        want = sb("want", [P, GB, 8])
        keep = sb("keep", [P, GB, 4])
        pen = sb("pen", [P, GB, 4])
        skp = sb("skp", [P, GB, EXPERTS])
        msp = sb("msp", [P, GB, 24])
        msr = sb("msr", [P, GB, 24])
        comb = [sb(f"comb{g}", [P, GB, EXPERTS]) for g in range(NG)]
        cTf = [sb(f"cTf{g}", [EXPERTS, N]) for g in range(NG)]
        cTs = [sb(f"cTs{g}", [64, N], fp32r) for g in range(NG)]
        sa, su, graw = free[0:2], free[2:4], part[4:7]
        gT = uT + [[shared_r[:, k * N:(k + 1) * N] for k in range(2)]]
        bank = [stack.enter_context(nc.psum_tensor(f"bank{k}", [P, N], fp32)) for k in range(8)]

        ld = {n: sem("ld_" + n) for n in
              ["x0", "x1", "ctx", "ctxT", "wredT", "cols", "rows", "w1", "w2", "wqk", "wvo", "moe", "small"]}
        consts = sem("consts")
        late_consts = sem("late_consts")
        prep = sem("prep")
        tanh_done = sem("tanh_done")
        var_ready = sem("var_ready")
        rstd_ready = sem("rstd_ready")
        dch = sem("dve_chain")
        xh_ready = sem("xh_ready")
        kr_full, kr_sb = sem("kr_full"), sem("kr_sb")
        xT_full, xT_sb = sem("xT_full"), sem("xT_sb")
        s0_full, sm_ready = sem("s0_full"), sem("sm_ready")
        p0_ready = sem("p0_ready")
        pT0_full, pT0_sb = sem("pT0_full"), sem("pT0_sb")
        o0_full, x1_ready = sem("o0_full"), sem("x1_ready")
        blk_clear = sem("blk_clear")
        blk_clear2 = sem("blk_clear2")
        gw_full, gw_sb = sem("gw_full"), sem("gw_sb")
        gw_hi, gw_lo, wvo_lo = sem("gw_hi"), sem("gw_lo"), sem("wvo_lo")
        w1_hi, w1_lo = sem("w1_hi"), sem("w1_lo")
        w2_hi, w2_lo = sem("w2_hi"), sem("w2_lo")
        we_hi, we_lo = sem("we_hi"), sem("we_lo")
        cn_hi, cn_lo = sem("cn_hi"), sem("cn_lo")
        fT_hi, xn_raw, xn_hi = sem("fT_hi"), sem("xn_raw"), sem("xn_hi")
        pT_hi, x3_hi = sem("pT_hi"), sem("x3_hi")
        fm_ready = sem("fm_ready")
        fT_full, fT_sb = sem("fT_full"), sem("fT_sb")
        up_full, h_raw, h_hi = sem("up_full"), sem("h_raw"), sem("h_hi")
        h_hi_dve = sem("h_hi_dve")
        h_lo = [sem("h_lo_even"), sem("h_lo_odd")]
        dn_done = sem("dn_done")
        accT_sb, acc_full, x2_ready = sem("accT_sb"), sem("acc_full"), sem("x2_ready")
        cn_raw, cn_ready = sem("cn_raw"), sem("cn_ready")
        cnT_full, cnT_sb = sem("cnT_full"), sem("cnT_sb")
        x2T_full, xnT_sb = sem("x2T_full"), sem("xnT_sb")
        misc_full, misc_read = sem("misc_full"), sem("misc_read")
        t_full, t_sb = sem("t_full"), sem("t_sb")
        s_full, nm_ready, exp_done = sem("s_full"), sem("nm_ready"), sem("exp_done")
        d0_ready, pz_ready, p0n_ready = sem("d0_ready"), sem("pz_ready"), sem("p0n_ready")
        rr_ready, pn_ready = sem("rr_ready"), sem("pn_ready")
        pT_full, pT_sb = sem("pT_full"), sem("pT_sb")
        u_full, u_hi, u_sb = sem("u_full"), sem("u_hi"), sem("u_sb")
        out_done, o_full, o_read = sem("out_done"), sem("o_full"), sem("o_read")
        oT_full, oT_sb = sem("oT_full"), sem("oT_sb")
        xb_ready, x3_ready = sem("xb_ready"), sem("x3_ready")
        ex_ready, comb_ready = sem("ex_ready"), sem("comb_ready")
        chi_ready, c_ready = sem("chi_ready"), sem("c_ready")
        h1_full, h3_full, cb_full = sem("h1_full"), sem("h3_full"), sem("cb_full")
        silu_done, su_done, g_raw = sem("silu_done"), sem("su_done"), sem("g_raw")
        g_lo_dve = sem("g_lo_dve")
        g_hi, g_lo, dn1_done = sem("g_hi"), sem("g_lo"), sem("dn1_done")
        yT_sb, y_full = sem("yT_sb"), sem("y_full")
        x4_ready, stored = sem("x4_ready"), sem("stored")

        NCONST, NLATE = 7, 11
        LN0, LN1, LN2, LNX = 0, 2, 4, 6
        GRP = [slice(g * GB, (g + 1) * GB) for g in range(NG)]

        def bc(ap, n):
            return ap.unsqueeze(2).to_broadcast([ap.shape[0], ap.shape[1], n])

        def rep(ap, n):
            return ap.unsqueeze(1).to_broadcast([ap.shape[0], n, ap.shape[1]])

        def b4(k):
            return bank[k][:, :].rearrange("p (b n) -> p b n", b=GB)

        def col(k):
            return cols[:, k:k + 1]

        def misc_uses(name):
            return MISC.index(name) + 1 - (MISC.index(name) > MISC.index("x2_1"))

        def wait_gated(engine, m):
            dve_done = sum(c <= m for c in DVE_LOW)
            engine.wait_ge(g_lo, m + 1 - dve_done)
            if dve_done:
                engine.wait_ge(g_lo_dve, dve_done)

        def up_bank(u):
            return 3 + (u + 1) % 3

        def step(s):
            return s // 16, (s // 2) % 8, s % 2

        def by_head(t, s):
            g, hp, bp = step(s)
            first = g * GB + 2 * bp
            return t[:, first:first + 2, 2 * hp:2 * hp + 2].rearrange("p b h -> p h b")

        def two(ap):
            return ap.rearrange("p (h b) -> p h b", h=2)

        block = stack.enter_context(nc.Block())

        @block.sync
        def _(sp):
            sp.dma_start(xr[:, GRP[0], :], x[:, GRP[0], :]).then_inc(ld["x0"], 16)
            sp.dma_start(wredT[:, :], wredT_in).then_inc(ld["wredT"], 16)
            sp.dma_start(ctxT[:, :], ctxT_in).then_inc(ld["ctxT"], 16)
            sp.dma_start(cols[:, :], cols_in).then_inc(ld["cols"], 16)
            sp.dma_start(xr[:, GRP[1], :], x[:, GRP[1], :]).then_inc(ld["x1"], 16)
            sp.dma_start(wqT, wqT_in).then_inc(ld["wqk"], 16)
            sp.wait_ge(blk_clear, 1)
            for r in range(2):
                half = slice(64 * r, 64 * r + 64)
                sp.dma_start(wkblk[half, :, r, :], wkT_in[half, :, :]).then_inc(ld["wqk"], 16)
            sp.dma_start(rows[:, :], rows_in.partition_broadcast(P)).then_inc(ld["rows"], 16)
            sp.dma_start(ctx[:, :, :], ctx_in).then_inc(ld["ctx"], 16)
            sp.dma_start(wvT, wvT_in).then_inc(ld["wvo"], 16)
            sp.wait_ge(blk_clear2, 1)
            for r in range(2):
                half = slice(64 * r, 64 * r + 64)
                sp.dma_start(woblk[half, :, r, :], wo_in[half, :, :]).then_inc(ld["wvo"], 16)
            sp.dma_start(w1raw, w1_in).then_inc(ld["w1"], 16)
            sp.dma_start(w2raw[:, :, :], w2_in).then_inc(ld["w2"], 16)
            sp.dma_start(mask8[:, :], mask_in).then_inc(ld["small"], 16)
            sp.dma_start(gw[:, :], gw_in).then_inc(ld["small"], 16)
            sp.dma_start(be2[:, :], be2_in).then_inc(ld["small"], 16)
            sp.wait_ge(gw_full, 9)
            sp.dma_start(we2raw, we2_in).then_inc(ld["moe"], 16)
            sp.wait_ge(up_full, 24)
            sp.dma_start(we1raw, we1_in).then_inc(ld["moe"], 16)
            sp.dma_start(we3raw, we3_in).then_inc(ld["moe"], 16)
            for n, batches in enumerate((slice(0, GB), slice(GB, GB + 2), slice(GB + 2, B))):
                sp.wait_ge(x4_ready, n + 1)
                sp.dma_start(out[:, batches, :], xr[:, batches, :]).then_inc(stored, 16)
            sp.wait_ge(stored, 16 * 3)

        @block.gpsimd
        def _(pool):
            done = {consts: 0, late_consts: 0}

            def put(ins, wait=False, event=consts):
                done[event] += 1
                ins.then_inc(event, 1)
                if wait:
                    pool.wait_ge(event, done[event])

            n_ln = 0

            def power():
                nonlocal n_ln
                n_ln += 1
                pool.wait_ge(var_ready, n_ln)
                k = (n_ln - 1) % 2
                pool.tensor_tensor(rstd[:, k, :], ve[:, k, :], mhalf[:, :], op=ALU.pow).then_inc(rstd_ready, 1)

            put(pool.memset(mhalf[:, :], -0.5))
            put(pool.memset(ident[:, :], 0.0), True)
            put(pool.affine_select(out=ident[:, :], in_=ident[:, :], compare_op=ALU.not_equal, fill=1.0,
                                   base=0, pattern=[[-1, P]], channel_multiplier=1))
            put(pool.memset(band[:, :], 0.0), True)
            put(pool.affine_select(out=band[:, :], in_=band[:, :], compare_op=ALU.is_ge, fill=NEG_BIG,
                                   base=WINDOW, pattern=[[-1, P]], channel_multiplier=1), True)
            put(pool.affine_select(out=band[:, :], in_=band[:, :], compare_op=ALU.is_ge, fill=NEG_BIG,
                                   base=WINDOW, pattern=[[1, P]], channel_multiplier=-1))
            put(pool.memset(rs0[:, :, :], 0.0))
            assert done[consts] == NCONST
            power()
            power()
            pool.memset(shared[:, 4 * N:8 * N], 0.0).then_inc(blk_clear2, 1)
            put(pool.memset(nvblk[:, :, :], 0.0), False, late_consts)
            put(pool.memset(nkblk[:, :], 0.0), False, late_consts)
            put(pool.memset(selr[:, :].bitcast(fp32), 0.0), True, late_consts)
            for half in range(2):
                put(pool.affine_select(out=selr[:, :].rearrange("k (c r m) -> k c r m", c=EC, r=2),
                                       in_=selr[:, :].bitcast(fp32).rearrange("k (c r m) -> k c r m", c=EC, r=2),
                                       compare_op=ALU.not_equal, fill=1.0, base=-32 * half,
                                       pattern=[[-2, EC], [-1, 2], [0, 64]], channel_multiplier=1),
                    True, late_consts)
            put(pool.memset(ones[:, :], 1.0), False, late_consts)
            put(pool.memset(gsp[:, :, :], PAD), False, late_consts)
            put(pool.memset(msp[:, :, :], PAD), False, late_consts)
            put(pool.memset(want[:, :, :], PAD), False, late_consts)
            for g in range(NG):
                put(pool.memset(cTs[g][:, :].bitcast(fp32), 0.0), False, late_consts)

            assert done[late_consts] == NLATE

            def context_affine(g):
                pool.wait_ge(cn_raw, g + 1)
                pool.tensor_tensor(cn[:, GRP[g], :], cn[:, GRP[g], :], rep(rows[:, R_LNCS:R_LNCS + P], GB),
                                   op=ALU.mult).then_inc(cn_ready, 1)
                pool.wait_ge(cn_ready, 2 * g + 1)
                pool.tensor_tensor(cn[:, GRP[g], :], cn[:, GRP[g], :], rep(rows[:, R_LNCB:R_LNCB + P], GB),
                                   op=ALU.add).then_inc(cn_ready, 1)

            power()
            power()
            context_affine(0)
            power()

            def low(pair, whole, chunks, event):
                pool.tensor_tensor(pair[1][:, chunks, :], whole[:, chunks, :],
                                   pair[0][:, chunks, :].bitcast(fp32), op=ALU.subtract).then_inc(*event)

            def folded_low(n):
                pool.wait_ge(gw_hi, n + 6)
                low(Wvo, Wvo_raw, slice(4 * n, 4 * n + 4), (wvo_lo, 1))

            for n, k in enumerate((2, 0, 1)):
                pool.wait_ge(w1_hi, n + 1)
                low(w1s, w1raw, slice(4 * k, 4 * k + 4), (w1_lo, 1))
                if n == 0:
                    pool.wait_ge(w2_hi, 1)
                    low(w2s, w2raw, slice(8, 12), (w2_lo, 1))

            def hidden_low(u):
                pool.wait_ge(h_hi_dve, u // 2 + 1)
                pool.tensor_tensor(hT[u % 3][1], hraw[u % 4], hT[u % 3][0].bitcast(fp32),
                                   op=ALU.subtract).then_inc(h_lo[1], 1)

            def context_low(g):
                pool.wait_ge(cn_hi, g + 1)
                pool.tensor_tensor(cns[1][:, GRP[g], :], cn[:, GRP[g], :],
                                   cns[0][:, GRP[g], :].bitcast(fp32), op=ALU.subtract).then_inc(cn_lo, 1)

            def attention_input(g):
                pool.wait_ge(x2_ready, g + 1)
                pool.wait_ge(prep, 10)
                pool.tensor_tensor(xb[g][:, :, :], xr[:, GRP[g], :], rep(bt[:, :], GB),
                                   op=ALU.add).then_inc(xb_ready, 1)

            def normalise(s):
                pool.wait_ge(rr_ready, s + 1)
                pool.tensor_tensor(pr[s % 3][:, :, :], pr[s % 3][:, :, :], bc(rr[:, s % 2, :], P),
                                   op=ALU.mult).then_inc(pn_ready, 1)

            def output_gain(g):
                pool.wait_ge(o_read, g + 1)
                pool.tensor_tensor(z[g][:, :, :], z[g][:, :, :], rep(st[:, :], GB),
                                   op=ALU.mult).then_inc(xb_ready, 1)

            def output_add(g):
                pool.wait_ge(xb_ready, NG + g + 1)
                pool.tensor_tensor(xr[:, GRP[g], :], z[g][:, :, :], xb[g][:, :, :],
                                   op=ALU.add).then_inc(x3_ready, 1)

            for u in range(1, 24, 2):
                if u == 1:
                    power()
                if u == 17:
                    power()
                hidden_low(u)
                if u in (3, 7):
                    k = (u - 3) // 4
                    pool.wait_ge(w2_hi, 2 + k)
                    low(w2s, w2raw, slice(4 * k, 4 * k + 4), (w2_lo, 1))
                if u == 5:
                    context_affine(1)
                if u in (11, 13):
                    context_low((u - 11) // 2)
                if u == 19:
                    attention_input(0)
                if u in (15, 21, 23):
                    folded_low((15, 21, 23).index(u))

            def null_shift(s):
                pool.wait_ge(nm_ready, s + 1)
                pool.tensor_tensor(two(d0[:, s % 2, :]), two(nm[:, s % 2, :]), by_head(ns0, s),
                                   op=ALU.subtract).then_inc(d0_ready, 1)

            def null_prob(s):
                pool.tensor_tensor(by_head(p0n, s), two(pz[:, s % 2, :]), two(rr[:, s % 2, :]),
                                   op=ALU.mult).then_inc(p0n_ready, 1)

            for k in range(STEPS + 1):
                if k:
                    normalise(k - 1)
                    null_prob(k - 1)
                if k < STEPS:
                    null_shift(k)
                if k == 0:
                    folded_low(3)
                if k == 4:
                    power()
                    attention_input(1)
                if k in (21, 24):
                    power()
                if k == 22:
                    output_gain(0)
                if k == 23:
                    output_add(0)
                if 8 <= k < 17:
                    m, third = divmod(k - 8, 3)
                    pool.wait_ge(we_hi, k - 7)
                    low((we1s, we3s, we2s)[m], (we1raw, we3raw, we2raw)[m], slice(3 * third, 3 * third + 3), (we_lo, 1))

            def gated_low(m):
                pool.wait_ge(g_hi, m + 1)
                pool.tensor_tensor(gT[m % 3][1], graw[m % 3], gT[m % 3][0].bitcast(fp32),
                                   op=ALU.subtract).then_inc(g_lo, 1)

            power()
            gated_low(0)
            output_gain(1)
            output_add(1)
            gated_low(1)
            power()
            for m in range(2, 18):
                if m not in DVE_LOW:
                    gated_low(m)

        @block.tensor
        def _(pe):
            def product(dst, a, b, start=True, stop=True):
                pe.matmul(dst, a[0], b[0], start=start, stop=False, skip_group_check=True)
                pe.matmul(dst, a[0], b[1], start=False, stop=False, skip_group_check=True)
                return pe.matmul(dst, a[1], b[0], start=False, stop=stop, skip_group_check=True)

            def turn_back(k, event):
                for b in range(GB):
                    mm = pe.transpose(bank[k][:, b * P:(b + 1) * P], accT[:, b * P:(b + 1) * P], ident[:, :])
                mm.then_inc(event, 1)

            def window_keys(g):
                pe.matmul(bank[g][:, :], wredT[:, :], ctxT[:, g * N:(g + 1) * N],
                          start=True, stop=True).then_inc(kr_full, 1)

            def window_rows(g):
                pe.wait_ge(xh_ready, LN0 + g + 1)
                for b in range(GB):
                    mm = pe.transpose(bank[2 + g][:, b * P:(b + 1) * P], xh[g][:, b, :], ident[:, :])
                mm.then_inc(xT_full, 1)

            def window_scores(g):
                pe.wait_ge(kr_sb, g + 1)
                pe.wait_ge(xT_sb, g + 1)
                for b in range(GB):
                    mm = pe.matmul(bank[4 + g][:, b * P:(b + 1) * P], xT[g][:, b * P:(b + 1) * P],
                                   krT[g][:, b * P:(b + 1) * P], start=True, stop=True)
                mm.then_inc(s0_full, 1)

            def window_turn(g):
                pe.wait_ge(p0_ready, GB * (g + 1))
                for b in range(GB):
                    mm = pe.transpose(bank[g][:, b * P:(b + 1) * P], p0[g][:, b, :], ident[:, :])
                mm.then_inc(pT0_full, 1)

            def window_values(g):
                pe.wait_ge(pT0_sb, g + 1)
                pe.wait_ge(ld["ctx"], 16)
                for b in range(GB):
                    mm = pe.matmul(bank[2 + g][:, b * P:(b + 1) * P], pT0[g][:, b * P:(b + 1) * P],
                                   ctx[:, g * GB + b, :], start=True, stop=True)
                mm.then_inc(o0_full, 1)

            def fold(n):
                pe.wait_ge(ld["wqk" if n < 4 else "wvo"], 48)
                if n >= 2:
                    pe.wait_ge(gw_sb, n - 1)
                left, right = (wqT, wkblk) if n < 4 else (wvT, woblk)
                for i in range(2):
                    c = 2 * (n % 4) + i
                    mm = pe.matmul(bank[6 + n % 2][:, 2 * i * P:2 * (i + 1) * P], left[:, c, :],
                                   right[:, c, :, :], start=True, stop=True)
                mm.then_inc(gw_full, 1)

            def fold_null_key():
                pe.wait_ge(gw_sb, 7)
                pe.wait_ge(prep, 8)
                for c in range(8):
                    pe.matmul(bank[6][:, 2 * c:2 * c + 2], wqT[:, c, :], nkblk[:, :], start=True, stop=True)

            def fold_null_value(chunks):
                for c in chunks:
                    for r in range(2):
                        mm = pe.matmul(bank[6][0:HEADS, P:2 * P], nvblk[:, c, :], woblk[:, c, r, :],
                                       start=(c == r == 0), stop=(c == 7 and r == 1))
                return mm

            pe.wait_ge(ld["wredT"], 16)
            pe.wait_ge(ld["ctxT"], 16)
            window_keys(0)
            window_keys(1)
            pe.wait_ge(consts, NCONST)
            window_rows(0)
            fold(0)
            window_rows(1)
            window_scores(0)
            window_scores(1)
            fold(1)
            fold(2)
            window_turn(0)
            fold(3)
            window_turn(1)
            window_values(0)
            fold(4)
            window_values(1)
            fold(5)
            fold(6)
            fold(7)
            fold_null_key()
            fold_null_value(range(0, 3))

            def misc(name):
                if MISC.index(name):
                    pe.wait_ge(misc_read, MISC.index(name))

            def mlp_rows(g, k):
                if g:
                    pe.wait_ge(fT_sb, k + 1)
                if k == 0:
                    pe.wait_ge(xh_ready, LN1 + g + 1)
                else:
                    pe.wait_ge(fm_ready, g + 1)
                src = (xh[g], xm0[g], xm1[g])[k]
                for b in range(GB):
                    mm = pe.transpose(bank[k][:, b * P:(b + 1) * P], src[:, b, :], ident[:, :])
                mm.then_inc(fT_full, 1)

            def mlp_up(u):
                g, j = divmod(u, 12)
                kind, c = j // FC, (j + 8) % 12
                pe.wait_ge(fT_sb, 3 * g + kind + 1)
                if u >= 3:
                    pe.wait_ge(h_raw, u - 2)
                if g == 0:
                    pe.wait_ge(w1_lo, kind + 1)
                product(bank[up_bank(u)][:, :], [w[:, c, :] for w in w1s], fT[g][kind]).then_inc(up_full, 1)

            def mlp_down(u):
                g, j = divmod(u, 12)
                pe.wait_ge(h_lo[u % 2], u // 2 + 1)
                if g == 0:
                    pe.wait_ge(w2_lo, j // FC + 1)
                product(bank[6 + g][:, :], [w[:, (j + 8) % 12, :] for w in w2s], hT[u % 3],
                        start=(j == 0), stop=(j == 11)).then_inc(dn_done, 1)

            def mlp_turn(g):
                pe.wait_ge(accT_sb, g + 1)
                turn_back(6 + g, acc_full)

            def context_rows(g):
                pe.wait_ge(fT_sb, 4 + g)
                pe.wait_ge(cn_ready, 2 * g + 2)
                for b in range(GB):
                    mm = pe.transpose(bank[g][:, b * P:(b + 1) * P], cn[:, g * GB + b, :], ident[:, :])
                mm.then_inc(cnT_full, 1)

            def attention_rows(g):
                if g == 0:
                    pe.wait_ge(fT_sb, 6)
                else:
                    misc("x2_1")
                pe.wait_ge(xh_ready, LN2 + g + 1)
                for b in range(GB):
                    mm = pe.transpose(bank[2 + 3 * g][:, b * P:(b + 1) * P], xh[g][:, b, :], ident[:, :])
                mm.then_inc(x2T_full, 1)

            def null_scores(g):
                misc(f"q0_{g}")
                pe.wait_ge(xnT_sb, g + 1)
                product(bank[5][0:HEADS, :], [w[:, :] for w in wnull], xnT[g]).then_inc(misc_full, 1)

            def fold_query(n):
                if n:
                    pe.wait_ge(t_sb, n)
                pe.wait_ge(xnT_sb, n // 16 + 1)
                product(bank[2][:, :], [w[:, n % 16, :] for w in G], xnT[n // 16]).then_inc(t_full, 1)

            pe.wait_ge(p0_ready, 2 * GB)
            mlp_rows(0, 0)
            fold_null_value(range(3, 8)).then_inc(gw_full, 1)
            pe.wait_ge(sm_ready, NG)
            for u in range(24 + LAG):
                if u == 2:
                    mlp_rows(0, 1)
                    mlp_rows(0, 2)
                    pe.wait_ge(x1_ready, NG)
                if u < 24:
                    mlp_up(u)
                if u == 7:
                    mlp_rows(1, 0)
                if u == 9:
                    mlp_rows(1, 1)
                    mlp_rows(1, 2)
                if u in (13, 17):
                    context_rows((u - 13) // 4)
                if u == 19:
                    attention_rows(0)
                if u == LAG:
                    pe.wait_ge(gw_sb, 9)
                if u >= LAG:
                    mlp_down(u - LAG)
                if u == 12 + LAG:
                    mlp_turn(0)
                if u == 24:
                    pe.wait_ge(gw_lo, 5)
                    fold_query(0)
                if u == 25:
                    pe.wait_ge(h_raw, 24)
                    null_scores(0)
                    fold_query(1)

            def turn_null_scores(g):
                misc(f"s0_{g}")
                for b in range(GB):
                    mm = pe.transpose(bank[5][:, b * HEADS:(b + 1) * HEADS], q0T[:, b * P:(b + 1) * P],
                                      ident[0:HEADS, 0:HEADS])
                mm.then_inc(misc_full, 1)

            def scores(s):
                g, hp, bp = step(s)
                if s >= 2:
                    pe.wait_ge(exp_done, 4 * (s - 1))
                first = (g * GB + 2 * bp) * P
                pe.matmul(bank[s % 2][:, :].rearrange("p (h n) -> p h n", h=2), ones[:, :],
                          rep(maskb[:, first:first + 2 * P], 2), start=True, stop=True)
                pe.wait_ge(t_sb, 2 * (s // 2) + 2)
                for i in range(4):
                    b = 2 * bp + i % 2
                    mm = pe.matmul(bank[s % 2][:, i * P:(i + 1) * P],
                                   tT[2 * (s // 2 % 2) + i // 2][:, b * P:(b + 1) * P],
                                   cnT[:, (g * GB + b) * P:(g * GB + b + 1) * P],
                                   start=False, stop=True, skip_group_check=True)
                mm.then_inc(s_full, 1)

            def turn_probs(s):
                pe.wait_ge(pn_ready, s + 1)
                if s:
                    pe.wait_ge(pT_sb, s)
                for i in range(4):
                    mm = pe.transpose(bank[3][:, i * P:(i + 1) * P], pr[s % 3][:, i, :], ident[:, :])
                mm.then_inc(pT_full, 1)

            def gather_context(s):
                g, hp, bp = step(s)
                pe.wait_ge(pT_sb, s + 1)
                if s:
                    pe.wait_ge(u_sb, s)
                for i in range(2):
                    def batch(t):
                        return t.rearrange("p (h b n) -> p h b n", h=2, b=2)[:, :, i, :]
                    mm = product(batch(bank[4][:, :]), [c[:, g * GB + 2 * bp + i, :] for c in cns],
                                 [batch(t) for t in pT[s % 2]])
                mm.then_inc(u_full, 1)

            def project(s):
                g, hp, bp = step(s)
                pe.wait_ge(u_sb, s + 1)
                if g == 0:
                    pe.wait_ge(wvo_lo, hp // 2 + 1)
                for i in range(2):
                    mm = product(bank[6 + g][:, bp * 2 * P:(bp + 1) * 2 * P], [w[:, 2 * hp + i, :] for w in Wvo],
                                 [t[:, i * 2 * P:(i + 1) * 2 * P] for t in uT[s % 2]],
                                 start=(s % 16 == 0 and i == 0), stop=False)
                mm.then_inc(out_done, 1)

            def turn_null(g):
                misc(f"p0_{g}")
                pe.wait_ge(p0n_ready, 16 * g + 16)
                for b in range(GB):
                    mm = pe.transpose(bank[5][0:HEADS, b * P:(b + 1) * P], p0n[:, g * GB + b, :], ident[:, :])
                mm.then_inc(misc_full, 1)

            def add_null(g):
                pe.wait_ge(misc_read, MISC.index(f"p0_{g}") + 1)
                pe.matmul(bank[6 + g][:, :], nw[:, :], p0T, start=False, stop=True,
                          skip_group_check=True).then_inc(oT_full, 1)

            def turn_output(g):
                pe.wait_ge(oT_sb, g + 1)
                turn_back(6 + g, o_full)

            def moe_rows(g):
                misc(f"x3_{g}")
                pe.wait_ge(xh_ready, LNX + g + 1)
                for b in range(GB):
                    mm = pe.transpose(bank[5][:, b * P:(b + 1) * P], xh[g][:, b, :], ident[:, :])
                mm.then_inc(misc_full, 1)

            def moe_logits(g):
                misc(f"lg_{g}")
                for b in range(GB):
                    mm = product(bank[5][:, b * EXPERTS:(b + 1) * EXPERTS],
                                 [t[:, b * P:(b + 1) * P] for t in x3T[g]], [w[:, :] for w in gws])
                mm.then_inc(misc_full, 1)

            def moe_weights(g):
                misc(f"cT_{g}")
                pe.wait_ge(comb_ready, g + 1)
                for b in range(GB):
                    mm = pe.transpose(bank[5][0:EXPERTS, b * P:(b + 1) * P], comb[g][:, b, :], ident[:, :])
                mm.then_inc(misc_full, 1)

            def moe_up(m):
                g, n = divmod(m, 9)
                c = (n + 8) % 9
                if m >= 2:
                    pe.wait_ge(silu_done, m - 1)
                product(bank[m % 2][:, :], [w[:, c, :] for w in we1s], x3T[g]).then_inc(h1_full, 1)
                if m >= 2:
                    pe.wait_ge(su_done, m - 1)
                product(bank[2 + m % 2][:, :], [w[:, c, :] for w in we3s], x3T[g]).then_inc(h3_full, 1)

            def moe_spread_weights(m):
                g, n = divmod(m, 9)
                if n:
                    k = 8 * g + n - 1
                    pe.wait_ge(c_ready, g + 1)
                    if k:
                        pe.wait_ge(g_raw, k)
                    pe.matmul(bank[4][:, :], selr[:, (n - 1) * P:n * P], cTs[g][:, :], start=True,
                              stop=True).then_inc(cb_full, 1)

            def moe_down(m):
                g, n = divmod(m, 9)
                wait_gated(pe, m)
                product(bank[6 + g][:, :], [w[:, (n + 8) % 9, :] for w in we2s], gT[m % 3],
                        start=(n == 0), stop=(n == 8)).then_inc(dn1_done, 1)

            def moe_bias(g):
                pe.matmul(bank[6 + g][:, :], be2[:, :], cTf[g][:, :], start=False, stop=False,
                          skip_group_check=True)

            def moe_turn(g):
                pe.wait_ge(yT_sb, g + 1)
                turn_back(6 + g, y_full)

            def moe_turn_last():
                for half in range(2):
                    pe.wait_ge(yT_sb, half + 2)
                    for b in (2 * half, 2 * half + 1):
                        mm = pe.transpose(bank[half][:, b * P:(b + 1) * P], accT[:, b * P:(b + 1) * P],
                                          ident[:, :])
                    mm.then_inc(y_full, 1)

            turn_null_scores(0)
            fold_query(2)
            pe.wait_ge(cn_lo, NG)
            pe.wait_ge(prep, 10)
            pe.wait_ge(late_consts, NLATE)
            pe.wait_ge(cnT_sb, NG)
            for k in range(STEPS + 4):
                if k < STEPS:
                    scores(k)
                if 3 <= k < STEPS + 3:
                    gather_context(k - 3)
                if k in (4, 20):
                    pe.wait_ge(x2_ready, 1 + k // 20)
                if k >= 4:
                    project(k - 4)
                if k + 3 < STEPS:
                    fold_query(k + 3)
                if k == 2:
                    mlp_turn(1)
                if k == 7:
                    attention_rows(1)
                if k == 9:
                    null_scores(1)
                if k == 10:
                    turn_null_scores(1)
                if k == 32:
                    pe.wait_ge(we_lo, 9)
                    pe.wait_ge(exp_done, 4 * (STEPS - 1))
                    pe.wait_ge(t_sb, STEPS)
                    moe_up(0)
                if k == 34:
                    pe.wait_ge(exp_done, 4 * STEPS)
                    pe.wait_ge(pT_sb, STEPS)
                    moe_up(1)
                if 1 <= k <= STEPS:
                    turn_probs(k - 1)
                if k in (17, 33):
                    turn_null((k - 17) // 16)
                if k in (19, 35):
                    add_null((k - 19) // 16)
                if k == 20:
                    turn_output(0)
                if k == 26:
                    moe_rows(0)
                if k == 28:
                    moe_logits(0)
                if k == 34:
                    moe_weights(0)
            for m in range(1, 20):
                if 3 <= m < 18:
                    moe_up(m)
                if m == 1:
                    moe_up(2)
                    turn_output(1)
                if m == 10:
                    moe_weights(1)
                    moe_down(8)
                if m < 18:
                    moe_spread_weights(m)
                if m in (2, 11):
                    pe.wait_ge(o_read, 1 + m // 11)
                if m >= 2 and m != 10:
                    moe_down(m - 2)
                if m == 4:
                    moe_rows(1)
                if m == 5:
                    moe_logits(1)
                if m in (4, 13):
                    moe_bias(m // 13)
                if m == 12:
                    moe_turn(0)
            pe.wait_ge(silu_done, 18)
            moe_turn_last()

        @block.scalar
        def _(act):
            def copy(dst, src, **kw):
                return act.activation(dst, src, ACT.Copy, **kw)

            act.wait_ge(consts, 1)
            act.activation(warm[:, :], mhalf[:, :], ACT.Exp)
            act.wait_ge(ld["cols"], 16)
            for g in range(NG):
                act.wait_ge(kr_full, g + 1)
                act.activation(krT[g][:, :], bank[g][:, :], ACT.Identity, bias=col(C_BRED)).then_inc(kr_sb, 1)
            act.wait_ge(ld["rows"], 16)
            act.activation(tg[:, :], rows[:, R_G:R_G + 4], ACT.Tanh).then_inc(tanh_done, 1)
            for g in range(NG):
                act.wait_ge(xT_full, g + 1)
                copy(xT[g][:, :], bank[2 + g][:, :]).then_inc(xT_sb, 1)
            act.wait_ge(consts, NCONST)

            def window_exp(g):
                act.wait_ge(sm_ready, g + 1)
                for b in range(GB):
                    act.activation(p0[g][:, b, :], sm[g][:, b, :], ACT.Exp, bias=nm0[:, g, b:b + 1],
                                   accum_out=rs0[:, g, b:b + 1]).then_inc(p0_ready, 1)

            def window_probs(g):
                act.wait_ge(pT0_full, g + 1)
                copy(pT0[g][:, :], bank[g][:, :]).then_inc(pT0_sb, 1)

            def folded(n):
                act.wait_ge(gw_full, n + 1)
                whole, scale = (Graw, HEADS ** -0.5) if n < 4 else (Wvo_raw, 1.0)
                copy(whole[:, 4 * (n % 4):4 * (n % 4) + 4, :], b4(6 + n % 2), scale=scale).then_inc(gw_sb, 1)

            def high(pair, whole, chunks, event):
                copy(pair[0][:, chunks, :], whole[:, chunks, :]).then_inc(*event)

            def folded_high(n):
                w, whole = (G, Graw) if n < 4 else (Wvo, Wvo_raw)
                act.wait_ge(gw_sb, n + 1)
                high(w, whole, slice(4 * (n % 4), 4 * (n % 4) + 4), (gw_hi, 1))

            folded(0)
            window_exp(0)
            folded(1)
            window_exp(1)
            folded(2)
            window_probs(0)
            folded(3)
            window_probs(1)
            for n in range(4, 8):
                folded(n)
            def first_high(pair, whole, k, event):
                high(pair, whole, slice(4 * k, 4 * k + 4), event)

            folded_high(0)
            folded_high(1)
            act.wait_ge(ld["w1"], 16)
            act.wait_ge(ld["w2"], 16)
            first_high(w1s, w1raw, 2, (w1_hi, 1))
            first_high(w2s, w2raw, 2, (w2_hi, 1))

            def rows_out(g, k):
                act.wait_ge(fT_full, 3 * g + k + 1)
                copy(fT[g][k][0], bank[k][:, :]).then_inc(fT_hi, 1)

            def hidden(u):
                act.wait_ge(up_full, u + 1)
                if u >= 4:
                    act.wait_ge(h_lo[u % 2], u // 2 - 1)
                act.activation(hraw[u % 4], bank[up_bank(u)][:, :], ACT.Relu,
                               bias=col(C_B1 + (u % 12 + 8) % 12)).then_inc(h_raw, 1)
                if u % 2:
                    return
                act.wait_ge(h_raw, u + 1)
                if u >= 3:
                    act.wait_ge(dn_done, u - 2)
                copy(hT[u % 3][0], hraw[u % 4]).then_inc(h_hi, 1)

            def mlp_output(g):
                act.wait_ge(dn_done, 12 * (g + 1))
                act.activation(accT[:, :], bank[6 + g][:, :], ACT.Identity, bias=b2sum[:, 1:2]).then_inc(accT_sb, 1)

            def attention_rows(g):
                act.wait_ge(x2T_full, g + 1)
                copied, value = (xn_raw, 1) if g == 0 else (misc_read, MISC.index("x2_1") + 1)
                act.activation(raw[g], bank[2 + 3 * g][:, :], ACT.Identity, bias=col(C_LN1B),
                               scale=col(C_LN1S)).then_inc(copied, 1)
                act.wait_ge(copied, value)
                copy(xnT[g][0], raw[g]).then_inc(xn_hi, 1)

            rows_out(0, 0)
            first_high(w1s, w1raw, 0, (w1_hi, 1))
            first_high(w1s, w1raw, 1, (w1_hi, 1))
            act.wait_ge(gw_full, 9)
            copy(wnf[:, :], bank[6][:, 0:HEADS], scale=HEADS ** -0.5)
            copy(nw[:, :], bank[6][0:HEADS, P:2 * P]).then_inc(gw_sb, 1)
            for u in range(24):
                hidden(u)
                if u == 1:
                    rows_out(0, 1)
                    rows_out(0, 2)
                if u in (3, 6):
                    first_high(w2s, w2raw, u // 3 - 1, (w2_hi, 1))
                if u == 5:
                    folded_high(2)
                if u == 7:
                    rows_out(1, 0)
                    folded_high(3)
                if u == 9:
                    rows_out(1, 1)
                    rows_out(1, 2)
                if u == 9:
                    act.wait_ge(gw_sb, 9)
                    copy(wnull[0][:, :], wnf[:, :]).then_inc(gw_hi, 1)
                if u in (9, 11):
                    c = (u - 9) // 2
                    act.wait_ge(cn_ready, 2 * c + 2)
                    copy(cns[0][:, GRP[c], :], cn[:, GRP[c], :]).then_inc(cn_hi, 1)
                if u in (13, 17):
                    c = (u - 13) // 4
                    act.wait_ge(cnT_full, c + 1)
                    copy(cnT[:, c * N:(c + 1) * N], bank[c][:, :]).then_inc(cnT_sb, 1)
                if u == 14:
                    act.wait_ge(prep, 8)
                    mlp_output(0)
                if u in (13, 17, 21):
                    folded_high(4 + (u - 13) // 4)
                if u == 19:
                    attention_rows(0)

            def t_copy(n):
                act.wait_ge(t_full, n + 1)
                if n >= 4:
                    act.wait_ge(s_full, 2 * ((n - 4) // 2) + 2)
                copy(tT[n % 4], bank[2][:, :]).then_inc(t_sb, 1)

            def null_copies(g):
                act.wait_ge(misc_full, misc_uses(f"q0_{g}"))
                copy(q0T[:, :], bank[5][0:HEADS, :]).then_inc(misc_read, 1)

            def null_score_copy(g):
                act.wait_ge(misc_full, misc_uses(f"s0_{g}"))
                copy(ns0[:, GRP[g], :], bank[5][:, 0:GB * HEADS].rearrange("p (b h) -> p b h", b=GB),
                     scale=-1.0).then_inc(misc_read, 1)

            def probs_high(s):
                act.wait_ge(pT_full, s + 1)
                if s >= 2:
                    act.wait_ge(u_full, s - 1)
                copy(pT[s % 2][0], bank[3][:, :]).then_inc(pT_hi, 1)

            def gathered_high(s):
                act.wait_ge(u_full, s + 1)
                if s >= 2:
                    act.wait_ge(out_done, s - 1)
                copy(uT[s % 2][0], bank[4][:, :]).then_inc(u_hi, 1)

            def output_copy(g):
                act.wait_ge(oT_full, g + 1)
                copy(accT[:, :], bank[6 + g][:, :]).then_inc(oT_sb, 1)

            def silu(m):
                act.wait_ge(h1_full, m + 1)
                if m >= 2:
                    act.wait_ge(su_done, m - 1)
                act.activation(sa[m % 2], bank[m % 2][:, :], ACT.Silu,
                               bias=col(C_BE1 + (m + 8) % 9)).then_inc(silu_done, 1)

            def gated_high(m):
                g, n = divmod(m, 9)
                if n:
                    act.wait_ge(g_raw, 8 * g + n)
                else:
                    act.wait_ge(su_done, m + 1)
                if m >= 3:
                    act.wait_ge(dn1_done, m - 2)
                copy(gT[m % 3][0], graw[m % 3]).then_inc(g_hi, 1)

            def moe_output(g):
                act.wait_ge(dn1_done, 9 * (g + 1))
                act.activation(accT[:, :], bank[6 + g][:, :], ACT.Identity, bias=col(C_BS2)).then_inc(yT_sb, 1)

            def high_part(g):
                act.wait_ge(misc_full, misc_uses(f"cT_{g}"))
                copy(cTf[g][:, :], bank[5][0:EXPERTS, :]).then_inc(misc_read, 1)
                act.wait_ge(misc_read, MISC.index(f"cT_{g}") + 1)
                copy(cTs[g][0:EXPERTS, :], cTf[g][:, :]).then_inc(chi_ready, 1)

            t_copy(0)
            null_copies(0)
            t_copy(1)
            null_score_copy(0)
            for k in range(STEPS + 3):
                if 2 <= k < STEPS + 2:
                    probs_high(k - 2)
                if k == 20:
                    output_copy(0)
                if k + 2 < STEPS:
                    t_copy(k + 2)
                if k == 8:
                    attention_rows(1)
                if k == 10:
                    null_copies(1)
                if k == 11:
                    null_score_copy(1)
                if k >= 3:
                    gathered_high(k - 3)
                if 8 <= k < 17:
                    m, third = divmod(k - 8, 3)
                    act.wait_ge(ld["moe"], 48)
                    high((we1s, we3s, we2s)[m], (we1raw, we3raw, we2raw)[m], slice(3 * third, 3 * third + 3), (we_hi, 1))
                if k == 0:
                    folded_high(7)
                if k == 1:
                    mlp_output(1)
                if k < STEPS:
                    act.wait_ge(nm_ready, k + 1)
                    if k >= 3:
                        act.wait_ge(pT_full, k - 2)
                    if k >= 2:
                        act.wait_ge(rr_ready, k - 1)
                    for i in range(4):
                        act.activation(pr[k % 3][:, i, :], bank[k % 2][:, i * P:(i + 1) * P], ACT.Exp,
                                       bias=nm[:, k % 2, i:i + 1],
                                       accum_out=rs[:, k % 2, i:i + 1]).then_inc(exp_done, 1)
                    act.wait_ge(d0_ready, k + 1)
                    if k >= 2:
                        act.wait_ge(p0n_ready, k - 1)
                    act.activation(pz[:, k % 2, :], d0[:, k % 2, :], ACT.Exp).then_inc(pz_ready, 1)
                if k == 26:
                    act.wait_ge(misc_full, misc_uses("x3_0"))
                    copy(x3T[0][0], bank[5][:, :]).then_inc(x3_hi, 1)
                if k == 28:
                    act.wait_ge(misc_read, MISC.index("lg_0") + 1)
                    act.activation(ex[:, :, :], sh[:, :, :], ACT.Exp).then_inc(ex_ready, 1)
                if k == 33:
                    silu(0)
                if k == 34:
                    high_part(0)
            silu(1)
            output_copy(1)
            act.wait_ge(out_done, STEPS)
            gated_high(0)
            for m in range(1, 18):
                if 2 <= m < 18:
                    silu(m)
                if 1 < m < 18:
                    gated_high(m - 1)
                if m == 4:
                    act.wait_ge(misc_full, misc_uses("x3_1"))
                    copy(x3T[1][0], bank[5][:, :]).then_inc(x3_hi, 1)
                if m == 6:
                    act.wait_ge(misc_read, MISC.index("lg_1") + 1)
                    act.activation(ex[:, :, :], sh[:, :, :], ACT.Exp).then_inc(ex_ready, 1)
                if m == 10:
                    high_part(1)
                if m == 11:
                    moe_output(0)
            act.wait_ge(dn1_done, 18)
            for half in range(2):
                cut = slice(2 * half * P, (2 * half + 2) * P)
                act.activation(accT[:, cut], bank[7][:, cut], ACT.Identity, bias=col(C_BS2)).then_inc(yT_sb, 1)

        @block.vector
        def _(dve):
            links = 0

            def link(ins):
                nonlocal links
                links += 1
                ins.then_inc(dch, 1)
                dve.wait_ge(dch, links)

            norms = [0, 0]

            def spread(src, scale, eps):
                for b in range(GB):
                    last = dve.bn_stats(stats[:, b, :], src(b))
                link(last)
                for b in range(GB):
                    last = dve.bn_aggr(mv[:, norms[0] % 2, b, :], stats[:, b, :])
                link(last)
                dve.tensor_scalar(ve[:, norms[0] % 2, :], mv[:, norms[0] % 2, :, 1], scale, eps, op0=ALU.mult,
                                  op1=ALU.add).then_inc(var_ready, 1)
                norms[0] += 1

            def scaled(src, dst, event):
                k = norms[1] % 2
                norms[1] += 1
                dve.wait_ge(rstd_ready, norms[1])
                for b in range(GB):
                    last = dve.tensor_scalar(dst(b), src(b), mv[:, k, b, 0:1], rstd[:, k, b:b + 1],
                                             op0=ALU.subtract, op1=ALU.mult)
                last.then_inc(*event)

            def norm(src, dst, event, scale, eps):
                spread(src, scale, eps)
                scaled(src, dst, event)

            def rows_of(g):
                return lambda b: xr[:, g * GB + b, :]

            dve.memset(shared[:, 0:4 * N], 0.0).then_inc(blk_clear, 1)
            for g in range(NG):
                dve.wait_ge(ld[f"x{g}"], 16)
                spread(rows_of(g), 1.0, EPS0)
            for g in range(NG):
                scaled(rows_of(g), lambda b: xh[g][:, b, :], (xh_ready, 1))

            dve.wait_ge(consts, NCONST)

            def ctx_of(g):
                return lambda b: ctx[:, g * GB + b, :]

            def cn_of(g):
                return lambda b: cn[:, g * GB + b, :]

            for g in range(NG):
                dve.wait_ge(s0_full, g + 1)
                link(dve.tensor_tensor(sm[g][:, :, :], b4(4 + g), rep(band[:, :], GB), op=ALU.add))
                dve.tensor_reduce(nm0[:, g, :], sm[g][:, :, :], axis=AX.X, op=ALU.max,
                                  negate=True).then_inc(sm_ready, 1)
            dve.wait_ge(ld["ctx"], 16)
            for g in range(NG):
                spread(ctx_of(g), 1.0, EPS1)
            dve.wait_ge(ld["rows"], 16)
            dve.wait_ge(tanh_done, 1)
            dve.wait_ge(late_consts, NLATE)
            dve.tensor_tensor(gwd[:, :], rows[:, R_GW:R_GW + P], rows[:, R_GW + P:R_GW + 2 * P],
                              op=ALU.subtract).then_inc(prep, 1)
            link(dve.tensor_tensor(b2sum[:, 0:1], cols[:, C_B2:C_B2 + 1], cols[:, C_B2 + 1:C_B2 + 2], op=ALU.add))
            dve.tensor_tensor(b2sum[:, 1:2], b2sum[:, 0:1], cols[:, C_B2 + 2:C_B2 + 3],
                              op=ALU.add).then_inc(prep, 1)
            dve.tensor_scalar(st[:, :], rows[:, R_LNOS:R_LNOS + P], tg[:, 1:2], None,
                              op0=ALU.mult).then_inc(prep, 1)
            dve.tensor_scalar(bt[:, :], rows[:, R_LNOB:R_LNOB + P], tg[:, 1:2], None,
                              op0=ALU.mult).then_inc(prep, 1)
            for r in range(2):
                half = slice(64 * r, 64 * r + 64)
                dve.tensor_copy(nvblk[half, :, :].rearrange("p c n -> p (c n)")[:, r:P:18],
                                cols[half, C_NV:C_NV + 1].to_broadcast([64, 8])).then_inc(prep, 1)
                dve.tensor_copy(nkblk[half, r:r + 1], cols[half, C_NK:C_NK + 1]).then_inc(prep, 1)
            for g in range(NG):
                scaled(ctx_of(g), cn_of(g), (cn_raw, 1))

            def window_out(g):
                dve.wait_ge(o0_full, g + 1)
                dve.wait_ge(p0_ready, GB * (g + 1))
                link(dve.reciprocal(rr0[:, g, :], rs0[:, g, :]))
                link(dve.tensor_scalar(rr0[:, g, :], rr0[:, g, :], tg[:, 0:1], None, op0=ALU.mult))
                for b in range(GB):
                    last = dve.scalar_tensor_tensor(xr[:, g * GB + b, :], b4(2 + g)[:, b, :], rr0[:, g, b:b + 1],
                                                    xr[:, g * GB + b, :], op0=ALU.mult, op1=ALU.add)
                last.then_inc(x1_ready, 1)
                dve.wait_ge(x1_ready, g + 1)

            def mlp_choice(g):
                scaled(rows_of(g), lambda b: xh[g][:, b, :], (xh_ready, 1))
                dve.wait_ge(xh_ready, LN1 + g + 1)
                link(dve.tensor_tensor(gtmp, xh[g][:, :, :], rep(gwd[:, :], GB), op=ALU.mult))
                link(dve.tensor_reduce(gd[:, :], gtmp, axis=AX.X, op=ALU.add))

            def mlp_masks(g):
                link(dve.tensor_scalar(m0[:, :], gd[:, :], 0.0, None, op0=ALU.is_ge))
                link(dve.tensor_tensor(xm0[g][:, :, :], xh[g][:, :, :], bc(m0[:, :], P), op=ALU.mult))
                dve.tensor_tensor(xm1[g][:, :, :], xh[g][:, :, :], xm0[g][:, :, :],
                                  op=ALU.subtract).then_inc(fm_ready, 1)

            def rows_low(g, k):
                dve.wait_ge(fT_hi, 3 * g + k + 1)
                dve.tensor_tensor(fT[g][k][1], bank[k][:, :], fT[g][k][0].bitcast(fp32),
                                  op=ALU.subtract).then_inc(fT_sb, 1)

            window_out(0)
            dve.wait_ge(prep, 8)
            spread(rows_of(0), 1.0, EPS0)
            mlp_choice(0)
            rows_low(0, 0)
            mlp_masks(0)
            window_out(1)
            spread(rows_of(1), 1.0, EPS0)
            def hidden_low(u):
                dve.wait_ge(h_hi, u // 2 + 1)
                dve.tensor_tensor(hT[u % 3][1], hraw[u % 4], hT[u % 3][0].bitcast(fp32),
                                  op=ALU.subtract).then_inc(h_lo[0], 1)

            def mlp_output(g):
                dve.wait_ge(acc_full, g + 1)
                dve.scalar_tensor_tensor(xr[:, GRP[g], :], b4(6 + g), tg[:, 2:3], xr[:, GRP[g], :],
                                         op0=ALU.mult, op1=ALU.add).then_inc(x2_ready, 1)
                dve.wait_ge(x2_ready, g + 1)
                spread(rows_of(g), 1.0 + EPS1, EPS0 * EPS1)

            def attention_norm(g):
                scaled(rows_of(g), lambda b: xh[g][:, b, :], (xh_ready, 1))

            def attention_rows(g):
                dve.wait_ge(xn_hi, g + 1)
                dve.tensor_tensor(xnT[g][1], raw[g], xnT[g][0].bitcast(fp32), op=ALU.subtract).then_inc(xnT_sb, 1)

            def hidden_high(u):
                dve.wait_ge(h_raw, u + 1)
                if u >= 3:
                    dve.wait_ge(dn_done, u - 2)
                dve.tensor_copy(hT[u % 3][0], hraw[u % 4]).then_inc(h_hi_dve, 1)

            def folded_low(n):
                dst = slice(4 * n, 4 * n + 4)
                dve.wait_ge(gw_hi, n + 1)
                dve.tensor_tensor(G[1][:, dst, :], Graw[:, dst, :], G[0][:, dst, :].bitcast(fp32),
                                  op=ALU.subtract).then_inc(gw_lo, 1)

            for u in range(0, 24, 2):
                hidden_low(u)
                hidden_high(u + 1)
                if u == 0:
                    rows_low(0, 1)
                    rows_low(0, 2)
                if u == 2:
                    mlp_choice(1)
                if u == 4:
                    mlp_masks(1)
                if u in (4, 6, 10, 12):
                    folded_low((4, 6, 10, 12).index(u))
                if u == 12:
                    dve.wait_ge(gw_hi, 5)
                    dve.tensor_tensor(wnull[1][:, :], wnf[:, :], wnull[0][:, :].bitcast(fp32),
                                      op=ALU.subtract).then_inc(gw_lo, 1)
                if u == 6:
                    dve.wait_ge(ld["small"], 48)
                    link(dve.tensor_copy(gws[0][:, :], gw[:, :]))
                    dve.tensor_tensor(gws[1][:, :], gw[:, :], gws[0][:, :].bitcast(fp32), op=ALU.subtract).then_inc(prep, 1)
                    dve.tensor_scalar(maskb[:, :], mask8[:, :], -1.0, -MASKED, op0=ALU.add,
                                      op1=ALU.mult).then_inc(prep, 1)
                if u == 8:
                    rows_low(1, 0)
                if u == 10:
                    rows_low(1, 1)
                    rows_low(1, 2)
                if u == 14:
                    mlp_output(0)
                if u == 16:
                    attention_norm(0)
                if u == 20:
                    attention_rows(0)

            def shift(s):
                null = by_head(ns0, s)
                dve.wait_ge(s_full, s + 1)
                if s == 0:
                    dve.wait_ge(misc_read, MISC.index("s0_0") + 1)
                if s == 16:
                    dve.wait_ge(misc_read, MISC.index("s0_1") + 1)
                if s >= 2:
                    dve.wait_ge(exp_done, 4 * (s - 1))
                    dve.wait_ge(d0_ready, s - 1)
                link(dve.tensor_reduce(nmx[:, s % 2, :], b4(s % 2), axis=AX.X, op=ALU.max, negate=True))
                dve.tensor_tensor(two(nm[:, s % 2, :]), two(nmx[:, s % 2, :]), null, op=ALU.min).then_inc(nm_ready, 1)

            def sums(s):
                dve.wait_ge(pz_ready, s + 1)
                if s >= 2:
                    dve.wait_ge(p0n_ready, s - 1)
                link(dve.tensor_tensor(rt[:, :], rs[:, s % 2, :], pz[:, s % 2, :], op=ALU.add))
                dve.reciprocal(rr[:, s % 2, :], rt[:, :]).then_inc(rr_ready, 1)

            def probs_copy(s):
                dve.wait_ge(pT_hi, s + 1)
                dve.tensor_tensor(pT[s % 2][1], bank[3][:, :], pT[s % 2][0].bitcast(fp32),
                                  op=ALU.subtract).then_inc(pT_sb, 1)

            def gathered_low(s):
                dve.wait_ge(u_hi, s + 1)
                dve.tensor_tensor(uT[s % 2][1], bank[4][:, :], uT[s % 2][0].bitcast(fp32),
                                  op=ALU.subtract).then_inc(u_sb, 1)

            def null_probs(g):
                dve.wait_ge(misc_full, misc_uses(f"p0_{g}"))
                dve.tensor_copy(p0T, bank[5][0:HEADS, :]).then_inc(misc_read, 1)

            def output_of(g):
                return lambda b: b4(6 + g)[:, b, :]

            def output_spread(g):
                dve.wait_ge(o_full, g + 1)
                spread(output_of(g), 1.0, EPS1)

            def output_scaled(g):
                scaled(output_of(g), lambda b: z[g][:, b, :], (o_read, 1))

            def moe_spread(g):
                dve.wait_ge(x3_ready, g + 1)
                spread(rows_of(g), 1.0, EPS0)

            def moe_scaled(g):
                scaled(rows_of(g), lambda b: xh[g][:, b, :], (xh_ready, 1))

            def two_largest(values, replaced):
                for b in range(GB):
                    last = dve.max(top8[:, b, :], values[:, b, :])
                link(last)
                link(dve.tensor_copy(want[:, :, 0:2], top8[:, :, 0:2]))
                for b in range(GB):
                    last = dve.match_replace(replaced[:, b, :], want[:, b, :], values[:, b, :], TAKEN)
                link(last)

            def gate_start(g):
                dve.wait_ge(misc_full, misc_uses(f"lg_{g}"))
                lg = bank[5][:, 0:GB * EXPERTS].rearrange("p (b e) -> p b e", b=GB)
                link(dve.tensor_reduce(g4[:, :], lg, axis=AX.X, op=ALU.max))
                dve.tensor_tensor(sh[:, :, :], lg, bc(g4[:, :], EXPERTS), op=ALU.subtract).then_inc(misc_read, 1)

            def gate_probs(g):
                dve.wait_ge(ex_ready, g + 1)
                link(dve.tensor_reduce(g4[:, :], ex[:, :, :], axis=AX.X, op=ALU.add))
                link(dve.reciprocal(g4r[:, :], g4[:, :]))
                link(dve.tensor_tensor(pb[:, :, :], ex[:, :, :], bc(g4r[:, :], EXPERTS), op=ALU.mult))
                link(dve.tensor_tensor(sc[:, :, :], pb[:, :, :], rep(rows[:, R_GB:R_GB + EXPERTS], GB), op=ALU.add))

            def gate_pairs(g):
                pairs = sc[:, :, :].rearrange("p b (g j k) -> p (b g) j k", g=4, j=2)
                dve.tensor_tensor(pmx[:, :, :], pairs[:, :, :, 0], pairs[:, :, :, 1], op=ALU.max)
                link(dve.tensor_tensor(pmn[:, :, :], pairs[:, :, :, 0], pairs[:, :, :, 1], op=ALU.min))
                dve.tensor_tensor(t1[:, :], pmx[:, :, 0], pmx[:, :, 1], op=ALU.max)
                dve.tensor_tensor(t2[:, :], pmx[:, :, 0], pmx[:, :, 1], op=ALU.min)
                link(dve.tensor_tensor(t3[:, :], pmn[:, :, 0], pmn[:, :, 1], op=ALU.max))
                link(dve.tensor_tensor(t2[:, :], t2[:, :], t3[:, :], op=ALU.max))
                link(dve.tensor_tensor(gsp[:, :, 0:4], t1[:, :].rearrange("p (b g) -> p b g", b=GB),
                                       t2[:, :].rearrange("p (b g) -> p b g", b=GB), op=ALU.add))

            def gate_groups(g):
                two_largest(gsp, gsr)

            def gate_lower(g):
                link(dve.tensor_scalar(keep[:, :, :], gsr[:, :, 0:4], TAKEN, None, op0=ALU.is_equal))
                link(dve.tensor_scalar(pen[:, :, :], keep[:, :, :], -1.0, -LOW, op0=ALU.add, op1=ALU.mult))
                flat = lambda t: t.rearrange("p b (g k) -> p (b g) k", g=4)
                kept = bc(keep[:, :, :].rearrange("p b g -> p (b g)"), 4)
                link(dve.tensor_tensor(flat(skp[:, :, :]), flat(sc[:, :, :]), kept, op=ALU.mult))
                for b in range(GB):
                    last = dve.tensor_tensor(msp[:, b, 0:EXPERTS].rearrange("p (g k) -> p g k", g=4),
                                             skp[:, b, :].rearrange("p (g k) -> p g k", g=4),
                                             bc(pen[:, b, :], 4), op=ALU.add)
                link(last)

            def gate_experts(g):
                two_largest(msp, msr)
                dve.scalar_tensor_tensor(comb[g][:, :, :], msr[:, :, 0:EXPERTS], TAKEN, pb[:, :, :],
                                         op0=ALU.is_equal, op1=ALU.mult).then_inc(comb_ready, 1)

            def low_part(g):
                dve.wait_ge(chi_ready, g + 1)
                dve.tensor_tensor(cTs[g][32:32 + EXPERTS, :], cTf[g][:, :],
                                  cTs[g][0:EXPERTS, :].bitcast(fp32), op=ALU.subtract).then_inc(c_ready, 1)

            def gated(m):
                g, n = divmod(m, 9)
                dve.wait_ge(silu_done, m + 1)
                dve.wait_ge(h3_full, m + 1)
                if m >= 3:
                    wait_gated(dve, m - 3)
                dve.scalar_tensor_tensor(su[m % 2] if n else graw[m % 3], bank[2 + m % 2][:, :],
                                         col(C_BE3 + (n + 8) % 9), sa[m % 2], op0=ALU.add,
                                         op1=ALU.mult).then_inc(su_done, 1)
                if n:
                    dve.wait_ge(cb_full, 8 * g + n)
                    dve.wait_ge(su_done, m + 1)
                    dve.tensor_tensor(graw[m % 3], su[m % 2], bank[4][:, :], op=ALU.mult).then_inc(g_raw, 1)

            def gated_low(m):
                if m < 17:
                    dve.wait_ge(g_hi, m + 1)
                else:
                    dve.wait_ge(g_raw, 16)
                    link(dve.tensor_copy(gT[m % 3][0], graw[m % 3]))
                dve.tensor_tensor(gT[m % 3][1], graw[m % 3], gT[m % 3][0].bitcast(fp32),
                                  op=ALU.subtract).then_inc(g_lo_dve, 1)

            def moe_output(g):
                dve.wait_ge(y_full, g + 1)
                dve.scalar_tensor_tensor(xr[:, GRP[g], :], b4(6 + g), tg[:, 3:4], xr[:, GRP[g], :],
                                         op0=ALU.mult, op1=ALU.add).then_inc(x4_ready, 1)

            def moe_rows(g):
                dve.wait_ge(x3_hi, g + 1)
                dve.tensor_tensor(x3T[g][1], bank[5][:, :], x3T[g][0].bitcast(fp32),
                                  op=ALU.subtract).then_inc(misc_read, 1)

            for k in range(STEPS + 4):
                if 1 <= k <= STEPS:
                    sums(k - 1)
                if k < STEPS:
                    shift(k)
                if 2 <= k < STEPS + 2:
                    probs_copy(k - 2)
                if 3 <= k < STEPS + 3:
                    gathered_low(k - 3)
                if k in (17, 33):
                    null_probs((k - 17) // 16)
                if k == 8:
                    attention_rows(1)
                if k == 21:
                    output_spread(0)
                if k == 22:
                    output_scaled(0)
                if k == 24:
                    moe_spread(0)
                if k == 25:
                    moe_scaled(0)
                if k == 27:
                    moe_rows(0)
                if k == 28:
                    gate_start(0)
                if k == 3:
                    mlp_output(1)
                if k == 4:
                    attention_norm(1)
                if 29 <= k < 34:
                    (gate_probs, gate_pairs, gate_groups, gate_lower, gate_experts)[k - 29](0)
                if k == 34:
                    gated(0)
                if k == 35:
                    low_part(0)
            output_spread(1)
            for m in range(1, 18):
                gated(m)
                if m == 1:
                    output_scaled(1)
                if m == 2:
                    moe_spread(1)
                if m == 3:
                    moe_scaled(1)
                if m == 4:
                    moe_rows(1)
                if m == 5:
                    gate_start(1)
                if m == 6:
                    gate_probs(1)
                    gate_pairs(1)
                if m == 7:
                    gate_groups(1)
                    gate_lower(1)
                if m == 8:
                    gate_experts(1)
                if m == 9:
                    low_part(1)
                if m == 12:
                    moe_output(0)
                if m - 1 in DVE_LOW:
                    gated_low(m - 1)
            gated_low(17)
            for half in range(2):
                dve.wait_ge(y_full, half + 2)
                pair_of = slice(2 * half, 2 * half + 2)
                rows_half = xr[:, GB + 2 * half:GB + 2 * half + 2, :]
                dve.scalar_tensor_tensor(rows_half, b4(half)[:, pair_of, :], tg[:, 3:4], rows_half,
                                         op0=ALU.mult, op1=ALU.add).then_inc(x4_ready, 1)


def kernel(x, ctx_1024, mask_BxS2_bf1, g_xattn, g_ffn, L0_xattn_W_reduce, L0_xattn_b_reduce,
           L0_ffn_gate_w, L0_ffn_w1, L0_ffn_b1, L0_ffn_w2, L0_ffn_b2, L0_ffn_sw1, L0_ffn_sb1,
           L0_ffn_sw2, L0_ffn_sb2, L1_xattn_ln1_s, L1_xattn_ln1_b, L1_xattn_lnc_s, L1_xattn_lnc_b,
           L1_xattn_Wq, L1_xattn_Wkv, L1_xattn_null_kv, L1_xattn_Wo, L1_xattn_lno_s,
           L1_xattn_lno_b, L1_ffn_gate_w, L1_ffn_gate_b, L1_ffn_We1, L1_ffn_be1, L1_ffn_We2,
           L1_ffn_be2, L1_ffn_We3, L1_ffn_be3, L1_ffn_ws1, L1_ffn_bs1, L1_ffn_ws2, L1_ffn_bs2,
           L1_ffn_ws3, L1_ffn_bs3):
    import numpy as np
    import concourse.bacc as bacc
    from concourse.bass_utils import run_bass_kernel_spmd

    A = np.asarray
    x, ctx = A(x), A(ctx_1024)
    inner = HEADS * 64

    def by_partition(w):
        w = A(w)
        return w.reshape(-1, P, w.shape[-1]).transpose(1, 0, 2)

    def chunks(w):
        return A(w).reshape(P, -1, P)

    experts = lambda w: A(w).transpose(1, 0, 2).reshape(P, -1)
    wkv = A(L1_xattn_Wkv)
    cols = np.concatenate([
        A(L0_xattn_b_reduce)[None], A(L0_ffn_b1).reshape(-1, P), A(L0_ffn_sb1).reshape(-1, P),
        A(L1_xattn_ln1_s)[None], A(L1_xattn_ln1_b)[None],
        A(L1_ffn_be1).reshape(-1, P), A(L1_ffn_bs1)[None],
        A(L1_ffn_be3).reshape(-1, P), A(L1_ffn_bs3)[None],
        A(L1_xattn_null_kv)[[0, 0]].reshape(1, P), A(L1_xattn_null_kv)[[1, 1]].reshape(1, P),
        A(L0_ffn_b2), A(L0_ffn_sb2)[None], A(L1_ffn_bs2)[None]]).T
    rows = np.concatenate([A(a).reshape(-1) for a in (
        L0_ffn_gate_w, L1_xattn_lnc_s, L1_xattn_lnc_b, L1_xattn_lno_s, L1_xattn_lno_b, L1_ffn_gate_b, g_xattn, g_ffn)])
    w1 = np.concatenate([A(L0_ffn_w1).transpose(1, 0, 2).reshape(P, -1), A(L0_ffn_sw1)], 1)
    w2 = np.concatenate([A(L0_ffn_w2).reshape(-1, P), A(L0_ffn_sw2)])
    data = {
        "in_x": x.transpose(1, 0, 2),
        "in_ctx": ctx.transpose(1, 0, 2),
        "in_ctxT": ctx.reshape(-1, P).T,
        "in_wredT": A(L0_xattn_W_reduce).T,
        "in_cols": cols,
        "in_rows": rows,
        "in_w1": chunks(w1),
        "in_w2": by_partition(w2),
        "in_wqT": by_partition(A(L1_xattn_Wq).T),
        "in_wkT": by_partition(wkv[:, :inner].T),
        "in_wvT": by_partition(wkv[:, inner:].T),
        "in_wo": by_partition(L1_xattn_Wo),
        "in_gw": A(L1_ffn_gate_w).T,
        "in_we1": chunks(np.concatenate([experts(L1_ffn_We1), A(L1_ffn_ws1)], 1)),
        "in_we3": chunks(np.concatenate([experts(L1_ffn_We3), A(L1_ffn_ws3)], 1)),
        "in_we2": by_partition(np.concatenate([A(L1_ffn_We2).reshape(-1, P), A(L1_ffn_ws2)])),
        "in_be2": A(L1_ffn_be2),
        "in_mask": A(mask_BxS2_bf1).reshape(1, -1).view(np.uint8),
    }
    data = {k: np.ascontiguousarray(v) for k, v in data.items()}
    nc = bacc.Bacc("TRN2", target_bir_lowering=False, num_devices=1)
    args = [nc.dram_tensor(k, v.shape, mybir.dt.from_np(v.dtype), kind="ExternalInput").ap()
            for k, v in data.items()]
    out = nc.dram_tensor("out_x", (P, B, P), mybir.dt.float32, kind="ExternalOutput").ap()
    gated_layers(nc, *args, out)
    r = run_bass_kernel_spmd(nc, [data], core_ids=[0])
    return r.results[0]["out_x"].transpose(1, 0, 2)
```
